# Optimizing a Trainium2 kernel written in Bass

```python
import numpy as np
import jax
import jax.numpy as jnp

def _softmax(x, axis=-1):
    return jax.nn.softmax(x, axis=axis)

def _gelu(x):
    return jax.nn.gelu(x, approximate=True)

def _silu(x):
    return jax.nn.silu(x)

def _sigmoid(x):
    return jax.nn.sigmoid(x)

def _layernorm(x, axis=-1, eps=1e-05):
    m = jnp.mean(x, axis=axis, keepdims=True)
    v = jnp.var(x, axis=axis, keepdims=True)
    return (x - m) / jnp.sqrt(v + eps)

def _scatter_add(tgt, idx, src, axis=0):
    return tgt.at[idx].add(src)

def _segment_sum(src, seg, n):
    return jax.ops.segment_sum(src, seg, n)
kernel_name = 'mk_flamingo_gated_d4_seqx_r8_d158c9'

def setup_inputs(seed: int=0):
    np.random.seed(seed)
    _w = jnp.asarray

    def _rec_inputs():
        import jax
        import jax.numpy as jnp
        _rk = jax.random.key(seed)
        x = -0.000125 + 0.9999 * jax.random.normal(jax.random.fold_in(_rk, 1), (32, 64, 128), jnp.float32)
        _lenS = 64 - jax.random.randint(jax.random.fold_in(_rk, 7), (32,), 0, max(1, 64 // 4) + 1, jnp.int32)
        _lenS2 = 64 - jax.random.randint(jax.random.fold_in(_rk, 8), (32,), 0, max(1, 64 // 4) + 1, jnp.int32)
        _ctx_1024P = jax.random.normal(jax.random.fold_in(_rk, 11), (32, 16, 128), jnp.float32)
        _ctx_1024c = jax.random.dirichlet(jax.random.fold_in(_rk, 511), 0.3 * jnp.ones((16,), jnp.float32), (32, 64))
        _ctx_1024t = jnp.einsum('bsk,bkd->bsd', _ctx_1024c, _ctx_1024P)
        _ctx_1024t = _ctx_1024t * jax.lax.rsqrt(jnp.mean(jnp.square(_ctx_1024t)) + 1e-12) * 0.953939
        ctx_1024 = -1.52775e-05 + 0.999936 * (_ctx_1024t + 0.3 * jax.random.normal(jax.random.fold_in(_rk, 611), (32, 64, 128), jnp.float32))
        _validS = jnp.arange(64)[None, :] < _lenS[:, None]
        _validS2 = jnp.arange(64)[None, :] < _lenS2[:, None]
        _causal = jnp.tril(jnp.ones((64, 64), dtype=bool))
        mask_BxSxS2_bf0 = jnp.logical_not(jnp.ones((32, 64, 64), dtype=bool))
        mask_BxS2_bf1 = jnp.ones((32, 64), dtype=bool)
        _g = jax.random.normal(jax.random.fold_in(_rk, 9001), (2, 4), jnp.float32)
        _g = jnp.sign(_g) * jnp.maximum(jnp.abs(_g), 1.0) + (_g == 0) * 1.0
        g_xattn = _g[0]
        g_ffn = _g[1]
        return (x, ctx_1024, mask_BxSxS2_bf0, mask_BxS2_bf1, g_xattn, g_ffn)
    x, ctx_1024, mask_BxSxS2_bf0, mask_BxS2_bf1, g_xattn, g_ffn = _rec_inputs()

    def _L0_xattn_setup():
        import jax, jax.numpy as jnp
        import numpy as np
        DECAY = 0.9
        key = jax.random.key(seed)
        k1, k2, k3 = jax.random.split(key, 3)
        B, S, D = (8, 512, 128)
        q = jax.random.normal(k1, (B, S, D), dtype=jnp.float32)
        k = jax.random.normal(k2, (B, S, D), dtype=jnp.float32)
        v = jax.random.normal(k3, (B, S, D), dtype=jnp.float32)
        return {'q': q, 'k': k, 'v': v}
    _L0_xattn_all = _L0_xattn_setup()
    _L0_xattn_in = {k: v for k, v in _L0_xattn_all.items() if k in ()}
    del _L0_xattn_all

    def _L0_ffn_setup():
        import jax, jax.numpy as jnp
        import numpy as np
        HIDDEN = 128
        MOE_FF = 64
        SHARED_FF = 352
        NUM_EXPERTS = 16
        TOP_K = 2
        NORM_TOPK = True
        key = jax.random.key(seed)
        ks = jax.random.split(key, 8)
        s = 0.02
        return {'layer_input': jax.random.normal(ks[0], (1, 256, HIDDEN), dtype=jnp.float32), 'gate_w': jax.random.normal(ks[1], (NUM_EXPERTS, HIDDEN), dtype=jnp.float32) * s, 'w_gate_up': jax.random.normal(ks[2], (NUM_EXPERTS, HIDDEN, 2 * MOE_FF), dtype=jnp.float32) * s, 'w_down': jax.random.normal(ks[3], (NUM_EXPERTS, MOE_FF, HIDDEN), dtype=jnp.float32) * s, 'shared_w_gate': jax.random.normal(ks[4], (SHARED_FF, HIDDEN), dtype=jnp.float32) * s, 'shared_w_up': jax.random.normal(ks[5], (SHARED_FF, HIDDEN), dtype=jnp.float32) * s, 'shared_w_down': jax.random.normal(ks[6], (HIDDEN, SHARED_FF), dtype=jnp.float32) * s, 'shared_gate_w': jax.random.normal(ks[7], (1, HIDDEN), dtype=jnp.float32) * s}
    _L0_ffn_all = _L0_ffn_setup()
    _L0_ffn_in = {k: v for k, v in _L0_ffn_all.items() if k in ('gate_w', 'w_gate_up', 'w_down', 'shared_w_gate', 'shared_w_up', 'shared_w_down', 'shared_gate_w')}
    del _L0_ffn_all

    def _L1_xattn_setup():
        import jax, jax.numpy as jnp
        import numpy as np
        D_MODEL = 128
        NUM_HEADS = 16
        DEPTH = D_MODEL // NUM_HEADS

        def _split_heads(x, B):
            return x.reshape(B, -1, NUM_HEADS, DEPTH).transpose(0, 2, 1, 3)
        key = jax.random.key(seed)
        ks = jax.random.split(key, 10)
        B, LQ, LK = (4, 256, 256)
        bound = float(np.sqrt(6.0 / (D_MODEL + D_MODEL)))

        def w(k):
            return jax.random.uniform(k, (D_MODEL, D_MODEL), jnp.float32, -bound, bound)
        return {'query': jax.random.normal(ks[0], (B, LQ, D_MODEL), jnp.float32), 'value': jax.random.normal(ks[1], (B, LK, D_MODEL), jnp.float32), 'wq': w(ks[2]), 'bq': jnp.zeros((D_MODEL,), jnp.float32), 'wk': w(ks[3]), 'bk': jnp.zeros((D_MODEL,), jnp.float32), 'wv': w(ks[4]), 'bv': jnp.zeros((D_MODEL,), jnp.float32), 'wo': w(ks[5]), 'bo': jnp.zeros((D_MODEL,), jnp.float32)}
    _L1_xattn_all = _L1_xattn_setup()
    _L1_xattn_in = {k: v for k, v in _L1_xattn_all.items() if k in ('wq', 'bq', 'wk', 'bk', 'wv', 'bv', 'wo', 'bo')}
    del _L1_xattn_all

    def _L1_ffn_setup():
        import jax, jax.numpy as jnp
        import numpy as np
        E = 8
        K = 2
        D = 128
        F = 512
        EPS = 1e-05

        def _layernorm(h, g, b):
            mu = h.mean(axis=-1, keepdims=True)
            var = ((h - mu) ** 2).mean(axis=-1, keepdims=True)
            return (h - mu) * jax.lax.rsqrt(var + EPS) * g[:, None, :] + b[:, None, :]
        key = jax.random.key(seed)
        ks = jax.random.split(key, 8)
        B, S = (2, 256)
        x = jax.random.normal(ks[0], (B, S, D), dtype=jnp.float32)
        Wr = jax.random.normal(ks[1], (D, E), dtype=jnp.float32) / np.sqrt(D)
        br = jnp.zeros((E,), dtype=jnp.float32)
        W1 = jax.random.normal(ks[2], (E, D, F), dtype=jnp.float32) / np.sqrt(D)
        b1 = jnp.zeros((E, F), dtype=jnp.float32)
        g1 = jnp.ones((E, F), dtype=jnp.float32)
        be1 = jnp.zeros((E, F), dtype=jnp.float32)
        W2 = jax.random.normal(ks[3], (E, F, D), dtype=jnp.float32) / np.sqrt(F)
        b2 = jnp.zeros((E, D), dtype=jnp.float32)
        g2 = jnp.ones((E, D), dtype=jnp.float32)
        be2 = jnp.zeros((E, D), dtype=jnp.float32)
        return {'x': x, 'Wr': Wr, 'br': br, 'W1': W1, 'b1': b1, 'g1': g1, 'be1': be1, 'W2': W2, 'b2': b2, 'g2': g2, 'be2': be2}
    _L1_ffn_all = _L1_ffn_setup()
    _L1_ffn_in = {k: v for k, v in _L1_ffn_all.items() if k in ('Wr', 'br', 'W1', 'b1', 'g1', 'be1', 'W2', 'b2', 'g2', 'be2')}
    del _L1_ffn_all

    def _L2_xattn_setup():
        import jax, jax.numpy as jnp
        import numpy as np
        D_MODEL = 128
        NUM_HEADS = 16
        D_K = D_MODEL // NUM_HEADS

        def _split_heads(x):
            B, S, _ = x.shape
            return x.reshape(B, S, NUM_HEADS, D_K).transpose(0, 2, 1, 3)
        key = jax.random.key(seed)
        ks = jax.random.split(key, 8)
        B, S = (2, 256)
        scale = 1.0 / np.sqrt(D_MODEL)
        return {'query': jax.random.normal(ks[0], (B, S, D_MODEL), jnp.float32), 'key': jax.random.normal(ks[1], (B, S, D_MODEL), jnp.float32), 'value': jax.random.normal(ks[2], (B, S, D_MODEL), jnp.float32), 'mask': jnp.zeros((B, S, S), dtype=bool), 'W_Q': jax.random.normal(ks[3], (D_MODEL, D_MODEL), jnp.float32) * scale, 'W_K': jax.random.normal(ks[4], (D_MODEL, D_MODEL), jnp.float32) * scale, 'W_V': jax.random.normal(ks[5], (D_MODEL, D_MODEL), jnp.float32) * scale, 'W_O': jax.random.normal(ks[6], (D_MODEL, D_MODEL), jnp.float32) * scale}
    _L2_xattn_all = _L2_xattn_setup()
    _L2_xattn_in = {k: v for k, v in _L2_xattn_all.items() if k in ('W_Q', 'W_K', 'W_V', 'W_O')}
    del _L2_xattn_all

    def _L2_ffn_setup():
        import jax, jax.numpy as jnp
        import numpy as np
        TOP_K = 2
        key = jax.random.key(seed)
        ks = jax.random.split(key, 7)
        B_, S, D, F, E, R = (2, 256, 128, 512, 4, 4)
        x = jax.random.normal(ks[0], (B_, S, D), dtype=jnp.float32)
        Wg = jax.random.normal(ks[1], (E, D), dtype=jnp.float32) * (1.0 / np.sqrt(D))
        bg = jnp.zeros((E,), dtype=jnp.float32)
        Wi = jax.random.normal(ks[2], (F, D), dtype=jnp.float32) * (1.0 / np.sqrt(D))
        Wo = jax.random.normal(ks[3], (D, F), dtype=jnp.float32) * (1.0 / np.sqrt(F))
        A = jax.random.normal(ks[4], (E, R, D), dtype=jnp.float32) * (1.0 / np.sqrt(D))
        Bm = jax.random.normal(ks[5], (E, F, R), dtype=jnp.float32) * 0.01
        return {'x': x, 'Wg': Wg, 'bg': bg, 'Wi': Wi, 'Wo': Wo, 'A': A, 'B': Bm}
    _L2_ffn_all = _L2_ffn_setup()
    _L2_ffn_in = {k: v for k, v in _L2_ffn_all.items() if k in ('Wg', 'bg', 'Wi', 'Wo', 'A', 'B')}
    del _L2_ffn_all

    def _L3_xattn_setup():
        import jax, jax.numpy as jnp
        import numpy as np
        DIM = 128
        DIM_LATENT = 128
        DIM_HEAD = 64
        HEADS = 16
        INNER = HEADS * DIM_HEAD

        def layernorm(x, g, b, eps=1e-05):
            m = jnp.mean(x, axis=-1, keepdims=True)
            v = jnp.mean((x - m) ** 2, axis=-1, keepdims=True)
            return (x - m) / jnp.sqrt(v + eps) * g + b

        def rmsnorm(x, gamma, eps=1e-08):
            n = jnp.linalg.norm(x, axis=-1, keepdims=True) * x.shape[-1] ** (-0.5)
            return x / jnp.maximum(n, eps) * gamma
        key = jax.random.key(seed)
        ks = jax.random.split(key, 8)
        b, n, m = (4, 512, 64)
        x = jax.random.normal(ks[0], (b, n, DIM), dtype=jnp.float32)
        latents = jax.random.normal(ks[1], (b, m, DIM_LATENT), dtype=jnp.float32)
        mask = jnp.ones((b, n), dtype=bool)
        s = 0.02
        return {'x': x, 'latents': latents, 'mask': mask, 'ln_x_g': jnp.ones((DIM,), jnp.float32), 'ln_x_b': jnp.zeros((DIM,), jnp.float32), 'ln_l_g': jnp.ones((DIM_LATENT,), jnp.float32), 'ln_l_b': jnp.zeros((DIM_LATENT,), jnp.float32), 'qn_g': jnp.ones((DIM_HEAD,), jnp.float32), 'kn_g': jnp.ones((DIM_HEAD,), jnp.float32), 'Wq': jax.random.normal(ks[2], (DIM_LATENT, INNER), jnp.float32) * s, 'Wkv': jax.random.normal(ks[3], (DIM, 2 * INNER), jnp.float32) * s, 'Wout': jax.random.normal(ks[4], (INNER, DIM_LATENT), jnp.float32) * s, 'bout': jnp.zeros((DIM_LATENT,), jnp.float32)}
    _L3_xattn_all = _L3_xattn_setup()
    _L3_xattn_in = {k: v for k, v in _L3_xattn_all.items() if k in ('ln_x_g', 'ln_x_b', 'ln_l_g', 'ln_l_b', 'qn_g', 'kn_g', 'Wq', 'Wkv', 'Wout', 'bout')}
    del _L3_xattn_all

    def _L3_ffn_setup():
        import jax, jax.numpy as jnp
        import numpy as np
        D_MODEL = 128
        N_HEADS = 16
        N_KV = 4
        NUM_REP = N_HEADS // N_KV
        HEAD_DIM = D_MODEL // N_HEADS
        N_EXPERTS = 8
        TOP_K = 2
        CAP_FACTOR = 1.25
        EPS_NORM = 1e-06

        def _rmsnorm(x, w):
            var = jnp.mean(x * x, axis=-1, keepdims=True)
            return w * (x * jax.lax.rsqrt(var + EPS_NORM))

        def _gqa(x, qw, qb, kw, kb, vw, vb, ow, ob):
            B, S, D = x.shape
            q = (x @ qw + qb).reshape(B, S, N_HEADS, HEAD_DIM).transpose(0, 2, 1, 3)
            k = (x @ kw + kb).reshape(B, S, N_KV, HEAD_DIM).transpose(0, 2, 1, 3)
            v = (x @ vw + vb).reshape(B, S, N_KV, HEAD_DIM).transpose(0, 2, 1, 3)
            k = jnp.repeat(k, NUM_REP, axis=1)
            v = jnp.repeat(v, NUM_REP, axis=1)
            scores = jnp.einsum('bhqd,bhkd->bhqk', q, k) / np.sqrt(HEAD_DIM).astype(np.float32)
            attn = jax.nn.softmax(scores, axis=-1)
            out = jnp.einsum('bhqk,bhkd->bhqd', attn, v)
            out = out.transpose(0, 2, 1, 3).reshape(B, S, D)
            return out @ ow + ob

        def _moe(x, gate_w, w1, w2):
            B, S, D = x.shape
            T = B * S
            x_flat = x.reshape(T, D)
            capacity = int(CAP_FACTOR * T * TOP_K / N_EXPERTS)
            logits = x_flat @ gate_w
            probs = jax.nn.sigmoid(logits)
            _, sel = jax.lax.top_k(probs, TOP_K)
            w_topk = jnp.take_along_axis(probs, sel, axis=1)
            w_topk = w_topk / (jnp.sum(w_topk, axis=-1, keepdims=True) + 1e-06)
            flat_sel = sel.reshape(-1)
            em = jax.nn.one_hot(flat_sel, N_EXPERTS, dtype=jnp.int32)
            ranks = jnp.take_along_axis(jnp.cumsum(em, axis=0), flat_sel[:, None], axis=1)[:, 0] - 1
            valid = ranks < capacity
            slot = flat_sel * capacity + ranks
            scatter_idx = jnp.where(valid, slot, N_EXPERTS * capacity)
            x_rep = jnp.repeat(x_flat, TOP_K, axis=0)
            padded = jnp.zeros((N_EXPERTS * capacity + 1, D), x.dtype).at[scatter_idx].set(x_rep)
            padded_x = padded[:N_EXPERTS * capacity].reshape(N_EXPERTS, capacity, D)
            h = jax.nn.gelu(jnp.einsum('ecd,edf->ecf', padded_x, w1), approximate=False)
            out_padded = jnp.einsum('ecf,efd->ecd', h, w2).reshape(N_EXPERTS * capacity, D)
            gather_idx = jnp.where(valid, slot, 0)
            out_rep = jnp.where(valid[:, None], out_padded[gather_idx], 0.0)
            out_w = out_rep * w_topk.reshape(-1)[:, None]
            return out_w.reshape(T, TOP_K, D).sum(axis=1).reshape(B, S, D)
        key = jax.random.key(seed)
        ks = jax.random.split(key, 12)
        s = 0.02
        return {'x': jax.random.normal(ks[0], (4, 128, D_MODEL), jnp.float32), 'qw': jax.random.normal(ks[1], (D_MODEL, D_MODEL), jnp.float32) * s, 'qb': jnp.zeros((D_MODEL,), jnp.float32), 'kw': jax.random.normal(ks[2], (D_MODEL, N_KV * HEAD_DIM), jnp.float32) * s, 'kb': jnp.zeros((N_KV * HEAD_DIM,), jnp.float32), 'vw': jax.random.normal(ks[3], (D_MODEL, N_KV * HEAD_DIM), jnp.float32) * s, 'vb': jnp.zeros((N_KV * HEAD_DIM,), jnp.float32), 'ow': jax.random.normal(ks[4], (D_MODEL, D_MODEL), jnp.float32) * s, 'ob': jnp.zeros((D_MODEL,), jnp.float32), 'gate_w': jax.random.normal(ks[5], (D_MODEL, N_EXPERTS), jnp.float32) * s, 'w1': jax.random.normal(ks[6], (N_EXPERTS, D_MODEL, 256), jnp.float32) * s, 'w2': jax.random.normal(ks[7], (N_EXPERTS, 256, D_MODEL), jnp.float32) * s, 'norm1_w': jnp.ones((D_MODEL,), jnp.float32), 'norm2_w': jnp.ones((D_MODEL,), jnp.float32)}
    _L3_ffn_all = _L3_ffn_setup()
    _L3_ffn_in = {k: v for k, v in _L3_ffn_all.items() if k in ('qw', 'qb', 'kw', 'kb', 'vw', 'vb', 'ow', 'ob', 'gate_w', 'w1', 'w2', 'norm1_w', 'norm2_w')}
    del _L3_ffn_all
    return {'x': x, 'ctx_1024': ctx_1024, 'mask_BxSxS2_bf0': mask_BxSxS2_bf0, 'mask_BxS2_bf1': mask_BxS2_bf1, 'g_xattn': g_xattn, 'g_ffn': g_ffn, 'L0_ffn_gate_w': _L0_ffn_in['gate_w'], 'L0_ffn_w_gate_up': _L0_ffn_in['w_gate_up'], 'L0_ffn_w_down': _L0_ffn_in['w_down'], 'L0_ffn_shared_w_gate': _L0_ffn_in['shared_w_gate'], 'L0_ffn_shared_w_up': _L0_ffn_in['shared_w_up'], 'L0_ffn_shared_w_down': _L0_ffn_in['shared_w_down'], 'L0_ffn_shared_gate_w': _L0_ffn_in['shared_gate_w'], 'L1_xattn_wq': _L1_xattn_in['wq'], 'L1_xattn_bq': _L1_xattn_in['bq'], 'L1_xattn_wk': _L1_xattn_in['wk'], 'L1_xattn_bk': _L1_xattn_in['bk'], 'L1_xattn_wv': _L1_xattn_in['wv'], 'L1_xattn_bv': _L1_xattn_in['bv'], 'L1_xattn_wo': _L1_xattn_in['wo'], 'L1_xattn_bo': _L1_xattn_in['bo'], 'L1_ffn_Wr': _L1_ffn_in['Wr'], 'L1_ffn_br': _L1_ffn_in['br'], 'L1_ffn_W1': _L1_ffn_in['W1'], 'L1_ffn_b1': _L1_ffn_in['b1'], 'L1_ffn_g1': _L1_ffn_in['g1'], 'L1_ffn_be1': _L1_ffn_in['be1'], 'L1_ffn_W2': _L1_ffn_in['W2'], 'L1_ffn_b2': _L1_ffn_in['b2'], 'L1_ffn_g2': _L1_ffn_in['g2'], 'L1_ffn_be2': _L1_ffn_in['be2'], 'L2_xattn_W_Q': _L2_xattn_in['W_Q'], 'L2_xattn_W_K': _L2_xattn_in['W_K'], 'L2_xattn_W_V': _L2_xattn_in['W_V'], 'L2_xattn_W_O': _L2_xattn_in['W_O'], 'L2_ffn_Wg': _L2_ffn_in['Wg'], 'L2_ffn_bg': _L2_ffn_in['bg'], 'L2_ffn_Wi': _L2_ffn_in['Wi'], 'L2_ffn_Wo': _L2_ffn_in['Wo'], 'L2_ffn_A': _L2_ffn_in['A'], 'L2_ffn_B': _L2_ffn_in['B'], 'L3_xattn_ln_x_g': _L3_xattn_in['ln_x_g'], 'L3_xattn_ln_x_b': _L3_xattn_in['ln_x_b'], 'L3_xattn_ln_l_g': _L3_xattn_in['ln_l_g'], 'L3_xattn_ln_l_b': _L3_xattn_in['ln_l_b'], 'L3_xattn_qn_g': _L3_xattn_in['qn_g'], 'L3_xattn_kn_g': _L3_xattn_in['kn_g'], 'L3_xattn_Wq': _L3_xattn_in['Wq'], 'L3_xattn_Wkv': _L3_xattn_in['Wkv'], 'L3_xattn_Wout': _L3_xattn_in['Wout'], 'L3_xattn_bout': _L3_xattn_in['bout'], 'L3_ffn_qw': _L3_ffn_in['qw'], 'L3_ffn_qb': _L3_ffn_in['qb'], 'L3_ffn_kw': _L3_ffn_in['kw'], 'L3_ffn_kb': _L3_ffn_in['kb'], 'L3_ffn_vw': _L3_ffn_in['vw'], 'L3_ffn_vb': _L3_ffn_in['vb'], 'L3_ffn_ow': _L3_ffn_in['ow'], 'L3_ffn_ob': _L3_ffn_in['ob'], 'L3_ffn_gate_w': _L3_ffn_in['gate_w'], 'L3_ffn_w1': _L3_ffn_in['w1'], 'L3_ffn_w2': _L3_ffn_in['w2'], 'L3_ffn_norm1_w': _L3_ffn_in['norm1_w'], 'L3_ffn_norm2_w': _L3_ffn_in['norm2_w']}

def reference(x, ctx_1024, mask_BxSxS2_bf0, mask_BxS2_bf1, g_xattn, g_ffn, L0_ffn_gate_w, L0_ffn_w_gate_up, L0_ffn_w_down, L0_ffn_shared_w_gate, L0_ffn_shared_w_up, L0_ffn_shared_w_down, L0_ffn_shared_gate_w, L1_xattn_wq, L1_xattn_bq, L1_xattn_wk, L1_xattn_bk, L1_xattn_wv, L1_xattn_bv, L1_xattn_wo, L1_xattn_bo, L1_ffn_Wr, L1_ffn_br, L1_ffn_W1, L1_ffn_b1, L1_ffn_g1, L1_ffn_be1, L1_ffn_W2, L1_ffn_b2, L1_ffn_g2, L1_ffn_be2, L2_xattn_W_Q, L2_xattn_W_K, L2_xattn_W_V, L2_xattn_W_O, L2_ffn_Wg, L2_ffn_bg, L2_ffn_Wi, L2_ffn_Wo, L2_ffn_A, L2_ffn_B, L3_xattn_ln_x_g, L3_xattn_ln_x_b, L3_xattn_ln_l_g, L3_xattn_ln_l_b, L3_xattn_qn_g, L3_xattn_kn_g, L3_xattn_Wq, L3_xattn_Wkv, L3_xattn_Wout, L3_xattn_bout, L3_ffn_qw, L3_ffn_qb, L3_ffn_kw, L3_ffn_kb, L3_ffn_vw, L3_ffn_vb, L3_ffn_ow, L3_ffn_ob, L3_ffn_gate_w, L3_ffn_w1, L3_ffn_w2, L3_ffn_norm1_w, L3_ffn_norm2_w):
    import jax
    import jax.numpy as jnp

    def _L0_xattn_ref(q, k, v):
        import jax, jax.numpy as jnp
        import numpy as np
        DECAY = 0.9
        kv = jnp.swapaxes(k * v, 0, 1)

        def step(r, kv_t):
            r = DECAY * r + kv_t
            return (r, r)
        r0 = jnp.zeros(q.shape[:1] + q.shape[2:], dtype=q.dtype)
        _, rs = jax.lax.scan(step, r0, kv)
        return q * jnp.swapaxes(rs, 0, 1)

    def _L0_ffn_ref(layer_input, gate_w, w_gate_up, w_down, shared_w_gate, shared_w_up, shared_w_down, shared_gate_w):
        import jax, jax.numpy as jnp
        import numpy as np
        HIDDEN = 128
        MOE_FF = 64
        SHARED_FF = 352
        NUM_EXPERTS = 16
        TOP_K = 2
        NORM_TOPK = True
        B, S, D = layer_input.shape
        x = layer_input.reshape(-1, D)
        N = x.shape[0]
        shared = jax.nn.silu(x @ shared_w_gate.T) * (x @ shared_w_up.T) @ shared_w_down.T
        shared = shared * jax.nn.sigmoid(x @ shared_gate_w.T)
        logits = x @ gate_w.T
        probs = jax.nn.softmax(logits.astype(jnp.float32), axis=-1)
        rw, sel = jax.lax.top_k(probs, TOP_K)
        if NORM_TOPK:
            rw = rw / rw.sum(axis=-1, keepdims=True)
        rw = rw.astype(x.dtype)
        combine = jnp.zeros((N, NUM_EXPERTS), x.dtype).at[jnp.arange(N)[:, None], sel].set(rw)
        gu = jnp.einsum('nd,edf->nef', x, w_gate_up)
        g, h = jnp.split(gu, 2, axis=-1)
        h = jax.nn.silu(g) * h
        expert_out = jnp.einsum('nef,efd,ne->nd', h, w_down, combine)
        out = expert_out + shared
        return out.reshape(B, S, D)

    def _L1_xattn_ref(query, value, wq, bq, wk, bk, wv, bv, wo, bo):
        import jax, jax.numpy as jnp
        import numpy as np
        D_MODEL = 128
        NUM_HEADS = 16
        DEPTH = D_MODEL // NUM_HEADS

        def _split_heads(x, B):
            return x.reshape(B, -1, NUM_HEADS, DEPTH).transpose(0, 2, 1, 3)
        B = query.shape[0]
        q = _split_heads(query @ wq.T + bq, B)
        k = _split_heads(value @ wk.T + bk, B)
        v = _split_heads(value @ wv.T + bv, B)
        scale = jnp.sqrt(jnp.asarray(DEPTH, dtype=q.dtype))
        scores = jnp.einsum('bhqd,bhkd->bhqk', q, k) / scale
        attn = jax.nn.softmax(scores, axis=-1)
        ctx = jnp.einsum('bhqk,bhkd->bhqd', attn, v)
        ctx = ctx.transpose(0, 2, 1, 3).reshape(B, -1, D_MODEL)
        return ctx @ wo.T + bo

    def _L1_ffn_ref(x, Wr, br, W1, b1, g1, be1, W2, b2, g2, be2):
        import jax, jax.numpy as jnp
        import numpy as np
        E = 8
        K = 2
        D = 128
        F = 512
        EPS = 1e-05

        def _layernorm(h, g, b):
            mu = h.mean(axis=-1, keepdims=True)
            var = ((h - mu) ** 2).mean(axis=-1, keepdims=True)
            return (h - mu) * jax.lax.rsqrt(var + EPS) * g[:, None, :] + b[:, None, :]
        B, S, _ = x.shape
        xt = x.reshape(-1, D)
        logits = xt @ Wr + br
        p = jax.nn.softmax(logits, axis=-1)
        probs, idx = jax.lax.top_k(p, K)
        probs = probs / probs.sum(axis=-1, keepdims=True)
        h = jnp.einsum('td,edf->etf', xt, W1) + b1[:, None, :]
        h = _layernorm(jax.nn.relu(h), g1, be1)
        y = jnp.einsum('etf,efd->etd', h, W2) + b2[:, None, :]
        y = _layernorm(jax.nn.relu(y), g2, be2)
        gate = (jax.nn.one_hot(idx, E, dtype=x.dtype) * probs[..., None]).sum(axis=1)
        out = jnp.einsum('te,etd->td', gate, y)
        return out.reshape(B, S, D)

    def _L2_xattn_ref(query, key, value, mask, W_Q, W_K, W_V, W_O):
        import jax, jax.numpy as jnp
        import numpy as np
        D_MODEL = 128
        NUM_HEADS = 16
        D_K = D_MODEL // NUM_HEADS

        def _split_heads(x):
            B, S, _ = x.shape
            return x.reshape(B, S, NUM_HEADS, D_K).transpose(0, 2, 1, 3)
        Q = _split_heads(jnp.einsum('bsd,ed->bse', query, W_Q))
        K = _split_heads(jnp.einsum('bsd,ed->bse', key, W_K))
        V = _split_heads(jnp.einsum('bsd,ed->bse', value, W_V))
        scores = jnp.einsum('bhqd,bhkd->bhqk', Q, K) / jnp.sqrt(jnp.float32(D_K))
        m = mask[:, None, :, :]
        scores = jnp.where(m, -jnp.inf, scores)
        attn = jax.nn.softmax(scores, axis=-1)
        attn = jnp.where(jnp.isnan(attn), 0.0, attn)
        out = jnp.einsum('bhqk,bhkd->bhqd', attn, V)
        B, H, S, _ = out.shape
        out = out.transpose(0, 2, 1, 3).reshape(B, S, D_MODEL)
        return jnp.einsum('bsd,ed->bse', out, W_O)

    def _L2_ffn_ref(x, Wg, bg, Wi, Wo, A, B):
        import jax, jax.numpy as jnp
        import numpy as np
        TOP_K = 2
        E = Wg.shape[0]
        logits = jnp.einsum('bsd,ed->bse', x, Wg) + bg
        scores = jax.nn.softmax(logits, axis=-1)
        topv, topi = jax.lax.top_k(scores, TOP_K)
        w = jnp.sum(jax.nn.one_hot(topi, E, dtype=x.dtype) * topv[..., None], axis=-2)
        base = jnp.einsum('bsd,fd->bsf', x, Wi)
        lora_low = jnp.einsum('bsd,erd->bser', x, A)
        lora = jnp.einsum('bser,efr->bsef', lora_low, B)
        h = jax.nn.relu(base[:, :, None, :] + lora)
        expert_out = jnp.einsum('bsef,df->bsed', h, Wo)
        out = jnp.einsum('bse,bsed->bsd', w, expert_out)
        return out

    def _L3_xattn_ref(x, latents, mask, ln_x_g, ln_x_b, ln_l_g, ln_l_b, qn_g, kn_g, Wq, Wkv, Wout, bout):
        import jax, jax.numpy as jnp
        import numpy as np
        DIM = 128
        DIM_LATENT = 128
        DIM_HEAD = 64
        HEADS = 16
        INNER = HEADS * DIM_HEAD

        def layernorm(x, g, b, eps=1e-05):
            m = jnp.mean(x, axis=-1, keepdims=True)
            v = jnp.mean((x - m) ** 2, axis=-1, keepdims=True)
            return (x - m) / jnp.sqrt(v + eps) * g + b

        def rmsnorm(x, gamma, eps=1e-08):
            n = jnp.linalg.norm(x, axis=-1, keepdims=True) * x.shape[-1] ** (-0.5)
            return x / jnp.maximum(n, eps) * gamma
        b, n, _ = x.shape
        m = latents.shape[1]
        h, d = (HEADS, DIM_HEAD)
        scale = d ** (-0.5)
        xn = layernorm(x, ln_x_g, ln_x_b)
        ln = layernorm(latents, ln_l_g, ln_l_b)
        q = (ln @ Wq).reshape(b, m, h, d).transpose(0, 2, 1, 3)
        kv = jnp.concatenate([xn @ Wkv, ln @ Wkv], axis=1)
        kv = kv.reshape(b, n + m, 2, h, d)
        k = kv[:, :, 0].transpose(0, 2, 1, 3)
        v = kv[:, :, 1].transpose(0, 2, 1, 3)
        qn = rmsnorm(q, qn_g) * scale
        kn = rmsnorm(k, kn_g)
        sim = jnp.einsum('bhid,bhjd->bhij', qn, kn)
        max_neg = -jnp.finfo(sim.dtype).max
        padded_mask = jnp.concatenate([mask, jnp.ones((b, m), bool)], axis=1)
        sim = jnp.where(padded_mask[:, None, None, :], sim, max_neg)
        attn = jax.nn.softmax(sim.astype(jnp.float32), axis=-1).astype(sim.dtype)
        out = jnp.einsum('bhij,bhjd->bhid', attn, v)
        out = out.transpose(0, 2, 1, 3).reshape(b, m, h * d)
        return out @ Wout + bout

    def _L3_ffn_ref(x, qw, qb, kw, kb, vw, vb, ow, ob, gate_w, w1, w2, norm1_w, norm2_w):
        import jax, jax.numpy as jnp
        import numpy as np
        D_MODEL = 128
        N_HEADS = 16
        N_KV = 4
        NUM_REP = N_HEADS // N_KV
        HEAD_DIM = D_MODEL // N_HEADS
        N_EXPERTS = 8
        TOP_K = 2
        CAP_FACTOR = 1.25
        EPS_NORM = 1e-06

        def _rmsnorm(x, w):
            var = jnp.mean(x * x, axis=-1, keepdims=True)
            return w * (x * jax.lax.rsqrt(var + EPS_NORM))

        def _gqa(x, qw, qb, kw, kb, vw, vb, ow, ob):
            B, S, D = x.shape
            q = (x @ qw + qb).reshape(B, S, N_HEADS, HEAD_DIM).transpose(0, 2, 1, 3)
            k = (x @ kw + kb).reshape(B, S, N_KV, HEAD_DIM).transpose(0, 2, 1, 3)
            v = (x @ vw + vb).reshape(B, S, N_KV, HEAD_DIM).transpose(0, 2, 1, 3)
            k = jnp.repeat(k, NUM_REP, axis=1)
            v = jnp.repeat(v, NUM_REP, axis=1)
            scores = jnp.einsum('bhqd,bhkd->bhqk', q, k) / np.sqrt(HEAD_DIM).astype(np.float32)
            attn = jax.nn.softmax(scores, axis=-1)
            out = jnp.einsum('bhqk,bhkd->bhqd', attn, v)
            out = out.transpose(0, 2, 1, 3).reshape(B, S, D)
            return out @ ow + ob

        def _moe(x, gate_w, w1, w2):
            B, S, D = x.shape
            T = B * S
            x_flat = x.reshape(T, D)
            capacity = int(CAP_FACTOR * T * TOP_K / N_EXPERTS)
            logits = x_flat @ gate_w
            probs = jax.nn.sigmoid(logits)
            _, sel = jax.lax.top_k(probs, TOP_K)
            w_topk = jnp.take_along_axis(probs, sel, axis=1)
            w_topk = w_topk / (jnp.sum(w_topk, axis=-1, keepdims=True) + 1e-06)
            flat_sel = sel.reshape(-1)
            em = jax.nn.one_hot(flat_sel, N_EXPERTS, dtype=jnp.int32)
            ranks = jnp.take_along_axis(jnp.cumsum(em, axis=0), flat_sel[:, None], axis=1)[:, 0] - 1
            valid = ranks < capacity
            slot = flat_sel * capacity + ranks
            scatter_idx = jnp.where(valid, slot, N_EXPERTS * capacity)
            x_rep = jnp.repeat(x_flat, TOP_K, axis=0)
            padded = jnp.zeros((N_EXPERTS * capacity + 1, D), x.dtype).at[scatter_idx].set(x_rep)
            padded_x = padded[:N_EXPERTS * capacity].reshape(N_EXPERTS, capacity, D)
            h = jax.nn.gelu(jnp.einsum('ecd,edf->ecf', padded_x, w1), approximate=False)
            out_padded = jnp.einsum('ecf,efd->ecd', h, w2).reshape(N_EXPERTS * capacity, D)
            gather_idx = jnp.where(valid, slot, 0)
            out_rep = jnp.where(valid[:, None], out_padded[gather_idx], 0.0)
            out_w = out_rep * w_topk.reshape(-1)[:, None]
            return out_w.reshape(T, TOP_K, D).sum(axis=1).reshape(B, S, D)
        src = x + _gqa(x, qw, qb, kw, kb, vw, vb, ow, ob)
        src = _rmsnorm(src, norm1_w)
        src = src + _moe(src, gate_w, w1, w2)
        return _rmsnorm(src, norm2_w)
    x = x + jnp.tanh(g_xattn[0]) * _L0_xattn_ref(_layernorm(x, axis=-1), ctx_1024, ctx_1024)
    x = x + jnp.tanh(g_ffn[0]) * _L0_ffn_ref(_layernorm(x, axis=-1), L0_ffn_gate_w, L0_ffn_w_gate_up, L0_ffn_w_down, L0_ffn_shared_w_gate, L0_ffn_shared_w_up, L0_ffn_shared_w_down, L0_ffn_shared_gate_w)
    x = x + jnp.tanh(g_xattn[1]) * _L1_xattn_ref(_layernorm(x, axis=-1), ctx_1024, L1_xattn_wq, L1_xattn_bq, L1_xattn_wk, L1_xattn_bk, L1_xattn_wv, L1_xattn_bv, L1_xattn_wo, L1_xattn_bo)
    x = x + jnp.tanh(g_ffn[1]) * _L1_ffn_ref(_layernorm(x, axis=-1), L1_ffn_Wr, L1_ffn_br, L1_ffn_W1, L1_ffn_b1, L1_ffn_g1, L1_ffn_be1, L1_ffn_W2, L1_ffn_b2, L1_ffn_g2, L1_ffn_be2)
    x = x + jnp.tanh(g_xattn[2]) * _L2_xattn_ref(_layernorm(x, axis=-1), ctx_1024, ctx_1024, mask_BxSxS2_bf0, L2_xattn_W_Q, L2_xattn_W_K, L2_xattn_W_V, L2_xattn_W_O)
    x = x + jnp.tanh(g_ffn[2]) * _L2_ffn_ref(_layernorm(x, axis=-1), L2_ffn_Wg, L2_ffn_bg, L2_ffn_Wi, L2_ffn_Wo, L2_ffn_A, L2_ffn_B)
    x = x + jnp.tanh(g_xattn[3]) * _L3_xattn_ref(ctx_1024, _layernorm(x, axis=-1), mask_BxS2_bf1, L3_xattn_ln_x_g, L3_xattn_ln_x_b, L3_xattn_ln_l_g, L3_xattn_ln_l_b, L3_xattn_qn_g, L3_xattn_kn_g, L3_xattn_Wq, L3_xattn_Wkv, L3_xattn_Wout, L3_xattn_bout)
    x = x + jnp.tanh(g_ffn[3]) * _L3_ffn_ref(_layernorm(x, axis=-1), L3_ffn_qw, L3_ffn_qb, L3_ffn_kw, L3_ffn_kb, L3_ffn_vw, L3_ffn_vb, L3_ffn_ow, L3_ffn_ob, L3_ffn_gate_w, L3_ffn_w1, L3_ffn_w2, L3_ffn_norm1_w, L3_ffn_norm2_w)
    return x

_drawn_inputs = setup_inputs


def setup_inputs(seed=0):
    import zlib

    import numpy as np

    out = dict(_drawn_inputs(seed))
    spreads = {'L1_xattn_bq': (0.0, 0.8),
     'L1_xattn_bk': (0.0, 0.8),
     'L1_xattn_bv': (0.0, 0.632),
     'L1_xattn_bo': (0.0, 0.586),
     'L1_ffn_br': (0.0, 0.405),
     'L1_ffn_b1': (0.0, 0.646),
     'L1_ffn_g1': (1.0, 0.6),
     'L1_ffn_be1': (0.0, 0.8),
     'L1_ffn_b2': (0.0, 0.8),
     'L1_ffn_g2': (1.0, 0.6),
     'L1_ffn_be2': (0.0, 0.8),
     'L2_ffn_bg': (0.0, 0.8),
     'L3_xattn_ln_x_g': (1.0, 0.6),
     'L3_xattn_ln_x_b': (0.0, 0.8),
     'L3_xattn_ln_l_g': (1.0, 0.6),
     'L3_xattn_ln_l_b': (0.0, 0.8),
     'L3_xattn_qn_g': (1.0, 0.6),
     'L3_xattn_kn_g': (1.0, 0.6),
     'L3_xattn_bout': (0.0, 0.8),
     'L3_ffn_qb': (0.0, 0.8),
     'L3_ffn_kb': (0.0, 0.8),
     'L3_ffn_vb': (0.0, 0.8),
     'L3_ffn_ob': (0.0, 0.8),
     'L3_ffn_norm1_w': (1.0, 0.6),
     'L3_ffn_norm2_w': (1.0, 0.6)}
    factors = {'g_ffn': 8.0,
     'L0_ffn_gate_w': 8.0,
     'L0_ffn_w_gate_up': 8.0,
     'L0_ffn_w_down': 8.0,
     'L0_ffn_shared_w_gate': 8.0,
     'L0_ffn_shared_w_up': 8.0,
     'L0_ffn_shared_w_down': 8.0,
     'L0_ffn_shared_gate_w': 8.0,
     'L2_xattn_W_Q': 2.828,
     'L2_xattn_W_K': 2.794,
     'L2_ffn_Wg': 8.0,
     'L2_ffn_A': 8.0,
     'L2_ffn_B': 8.0,
     'L3_xattn_Wq': 8.0,
     'L3_xattn_Wkv': 8.0,
     'L3_xattn_Wout': 8.0,
     'L3_ffn_qw': 8.0,
     'L3_ffn_kw': 8.0,
     'L3_ffn_vw': 8.0,
     'L3_ffn_ow': 8.0,
     'L3_ffn_gate_w': 8.0,
     'L3_ffn_w1': 8.0,
     'L3_ffn_w2': 8.0}
    for name, (base, spread) in spreads.items():
        noise = np.random.default_rng([zlib.crc32(name.encode()), seed]).standard_normal(out[name].shape)
        drawn = base * np.exp(spread * noise) if base else spread * noise
        out[name] = jnp.asarray(drawn.astype(out[name].dtype))
    for name, factor in factors.items():
        out[name] = (out[name] * factor).astype(out[name].dtype)
    return out
```

```python
from contextlib import ExitStack

import concourse.bass as bass
from concourse import mybir

F32 = mybir.dt.float32
I32 = mybir.dt.int32
U32 = mybir.dt.uint32
U8 = mybir.dt.uint8
ALU = mybir.AluOpType
ACT = mybir.ActivationFunctionType
AX = mybir.AxisListType.X

P = 128
BATCH, SEQ, D = 32, 64, 128
TILES = 4
TOK = TILES * P
PAIR = P // SEQ
BLOCKS = BATCH * SEQ // TOK
HEADS, HD = 16, 8
HP = HEADS // 2
XD = 64
LN_EPS, RMS_EPS = 1e-5, 1e-6
NEG = -1e30

CONST = dict(ident=P, hmask=HEADS, pmask=P, tri=P, iota=HEADS, decay=P)
L0 = dict(router=17, gu=4 * 512, sgu=704, down=11 * D)
XA = dict(wq=D, wk=D, wv=D, wo=D)
XB = dict(bq=1, bk=1, bv=D, bo=D)
L1F = dict(wr=8, br=8, b1=32, g1=32, be1=32, w1=8 * 512, g2=8 * D)
L2F = dict(wg=4, bg=4, wi=512, wo=4 * D)
L3X = dict(lxg=1, lxb=1, llg=1, llb=1, qn=1, kn=1, bout=D, wq=1024, wkv=2048, wout=8 * D)
L3F = dict(wr=8, n1=D, n2=D, w1=8 * 256, w2=16 * D)


def width(pieces):
    return sum(pieces.values())


def pieces_of(tensor, pieces):
    at, out = 0, {}
    for name, n in pieces.items():
        out[name] = tensor[:, at:at + n]
        at += n
    return out


class Chain:

    def __init__(self, engine, sem):
        self.engine, self.sem, self.n = engine, sem, 0

    def __call__(self, ins):
        self.n += 1
        ins.then_inc(self.sem, 1)
        self.engine.wait_ge(self.sem, self.n)

    def last_of(self, instructions):
        for ins in instructions:
            self.n += 1
            ins.then_inc(self.sem, 1)
        self.engine.wait_ge(self.sem, self.n)


def rsqrt(dve, link, y, v, tmp):
    vb, yb = v.bitcast(I32), y.bitcast(I32)
    link(dve.tensor_scalar(yb, vb, 1, None, ALU.logical_shift_right))
    link(dve.tensor_scalar(yb, yb, -1.0, 1597463007.0, ALU.mult, ALU.add))
    for _ in range(3):
        link(dve.tensor_tensor(tmp, y, y, ALU.mult))
        link(dve.scalar_tensor_tensor(tmp, tmp, -0.5, v, ALU.mult, ALU.mult))
        link(dve.scalar_tensor_tensor(y, tmp, 1.5, y, ALU.add, ALU.mult))


def build(nc, args, out):
    ctx = ExitStack()
    with ctx:
        def sb(name, shape, dt=F32):
            return ctx.enter_context(nc.sbuf_tensor(name, shape, dt))

        consts = sb("consts", [P, width(CONST)])
        ones = sb("ones", [P, P])
        w_l0 = sb("w_l0", [P, width(L0)])
        w_x1 = sb("w_x1", [P, width(XA) + width(XB)])
        w_f1 = sb("w_f1", [P, width(L1F)])
        w_f1b = sb("w_f1b", [8, D])
        w_f1d = sb("w_f1d", [P, 4, 8, D + 1])
        w_x2 = sb("w_x2", [P, width(XA)])
        w_f2 = sb("w_f2", [P, width(L2F)])
        w_f2e = sb("w_f2e", [P, 4, 512])
        w_x3 = sb("w_x3", [P, width(L3X)])
        w_a3 = sb("w_a3", [P, width(XA) + width(XB)])
        w_f3 = sb("w_f3", [P, width(L3F)])
        gates = sb("gates", [P, 8])
        tg = sb("tg", [P, 8])
        expert_bias = sb("expert_bias", [P, 8, D])
        scaled = sb("scaled", [P, 8])
        bo1 = sb("bo1", [P, D])
        bout3 = sb("bout3", [P, D])
        bv1 = sb("bv1", [P, D])
        bv3 = sb("bv3", [P, D])
        run_mask = sb("run_mask", [P, 8])
        v_blocks = sb("v_blocks", [P, TILES, HP, PAIR, 18])
        q_blocks = sb("q_blocks", [P, PAIR, 8, 2, XD])
        h_shared = sb("h_shared", [P, 2, 384])
        x = sb("x", [P, TILES, D])
        ctok = sb("ctok", [P, TILES, D])
        cT = sb("cT", [P, TOK])
        xn = sb("xn", [P, TILES, D])
        xnT = sb("xnT", [P, TOK])
        cxT = sb("cxT", [P, TILES * PAIR, 2, SEQ])
        mask2_words = sb("mask2", [P, TILES, SEQ // 4], I32)
        mask2 = mask2_words[:, :, :].bitcast(U8)
        mask3_words = sb("mask3", [P, TILES * PAIR, SEQ // 4], I32)
        mask3 = mask3_words[:, :, :].bitcast(U8)
        neg2 = sb("neg2", [P, TILES, SEQ])
        any2 = sb("any2", [P, TILES])
        neg3 = sb("neg3", [P, TILES * PAIR, 2, SEQ])
        small = sb("small", [P, 1024])
        work = sb("work", [P, 13312])
        lora_a = work[0:4, 0:4 * D].rearrange("p (e d) -> p e d", e=4)
        lora_b = work[0:4, 1024:1024 + 2048].rearrange("p (e f) -> p e f", e=4)
        b2 = work[:, 4096:4096 + 8 * D]

        banks = [ctx.enter_context(nc.psum_tensor(f"bank{i}", [P, 512], F32)) for i in range(8)]

        k_const = pieces_of(consts, CONST)
        k_l0 = pieces_of(w_l0, L0)
        k_x1 = pieces_of(w_x1, {**XA, **XB})
        k_f1 = pieces_of(w_f1, L1F)
        k_x2 = pieces_of(w_x2, XA)
        k_f2 = pieces_of(w_f2, L2F)
        k_x3 = pieces_of(w_x3, L3X)
        k_a3 = pieces_of(w_a3, {**XA, **XB})
        k_f3 = pieces_of(w_f3, L3F)
        ident = k_const["ident"]
        eps_cache = {}

        def stage(names, body):
            with ExitStack() as inner:
                stage.n += 1
                sems = [inner.enter_context(nc.semaphore(f"{n}_{stage.n}")) for n in names.split()]
                with nc.Block() as block:
                    body(block, *sems)
                nums = sorted(s.num for s in sems)
                starts = [n for n in nums if n - 1 not in nums]
                for a in starts:
                    b = a
                    while b in nums:
                        b += 1
                    nc.vector.sem_clear(range(a, b))
                nc.all_engine_barrier()
        stage.n = 0

        def load_all(block, loaded):
            @block.sync
            def _(sp):
                for name, dst in (("f1", w_f1[:, :]), ("consts", consts[:, :]), ("f1b", w_f1b[:, :]),
                                  ("gates", gates[:, :]), ("x1", w_x1[:, :]), ("lora_a", lora_a), ("lora_b", lora_b), ("b2", b2),
                                  ("f2", w_f2[:, :]), ("l0", w_l0[:, :]), ("x2", w_x2[:, :]),
                                  ("x3", w_x3[:, :]), ("a3", w_a3[:, :]), ("f3", w_f3[:, :])):
                    sp.dma_start(dst, args[name]).then_inc(loaded, 16)
                for c in range(4):
                    sp.dma_start(w_f1d[:, c, :, 0:D], args["f1d"][:, c, :, :]).then_inc(loaded, 16)
                sp.wait_ge(loaded, 16 * 18)

            @block.vector
            def _(dve):
                dve.memset(ones[:, :], 1.0)
                dve.memset(run_mask[:, :], 0.0)
                dve.memset(w_f1d[:, :, :, D:D + 1], 1.0)
                dve.memset(q_blocks[:, :, :, :, :], 0.0)
                dve.memset(h_shared[:, :, :], 0.0)
                dve.memset(v_blocks[:, :, :, :, :], 0.0)
                dve.memset(neg3[:, :, :, :], 0.0)
        stage("loaded", load_all)

        def prepare(block, link_sem, means, evacuated, tanh_done, ones_set):
            w2_raw = w_f1d[:, :, :, 0:D]

            @block.tensor
            def _(pe):
                for e in range(8):
                    for c in range(4):
                        m = pe.matmul(banks[e // 4][:, (e % 4) * D:(e % 4 + 1) * D],
                                      k_f1["be1"][:, e * 4 + c:e * 4 + c + 1].to_broadcast([P, P]),
                                      w_f1d[:, c, e, 0:D], start=(c == 0), stop=(c == 3))
                m.then_inc(means, 1)
                pe.wait_ge(evacuated, 1)
                for half in range(2):
                    for c in range(4):
                        m = pe.matmul(banks[2 + half][:, :], ones[:, :], w_f1d[:, c, 4 * half:4 * half + 4, 0:D],
                                      start=(c == 0), stop=(c == 3))
                m.then_inc(means, 1)
                for e in range(4):
                    m = pe.matmul(banks[4 + e][:, :], lora_a[:, e, :], lora_b[:, e, :], start=True, stop=True)
                m.then_inc(means, 1)

            @block.scalar
            def _(act):
                act.activation(tg[:, :], gates[:, :], ACT.Tanh).then_inc(tanh_done, 1)

            @block.vector
            def _(dve):
                link = Chain(dve, link_sem)
                dve.wait_ge(means, 1)
                for half in range(2):
                    dve.tensor_tensor(expert_bias[:, 4 * half:4 * half + 4, :],
                                      banks[half][:, :].rearrange("p (e d) -> p e d", d=D),
                                      b2[:, 512 * half:512 * half + 512].rearrange("p (e d) -> p e d", d=D),
                                      ALU.add)
                for c in range(4):
                    g1 = k_f1["g1"][:, c:32:4]
                    m = dve.tensor_tensor(w_f1d[:, c, :, 0:D], w_f1d[:, c, :, 0:D],
                                          g1.unsqueeze(2).to_broadcast([P, 8, D]), ALU.mult)
                m.then_inc(evacuated, 1)
                dve.wait_ge(means, 2)
                for half in range(2):
                    for c in range(4):
                        w = w_f1d[:, c, 4 * half:4 * half + 4, 0:D]
                        dve.scalar_tensor_tensor(w, banks[2 + half][:, :].rearrange("p (e d) -> p e d", d=D),
                                                 -1.0 / 512, w, ALU.mult, ALU.add)
                dve.wait_ge(means, 3)
                for e in range(4):
                    dve.tensor_tensor(w_f2e[:, e, :], banks[4 + e][:, :], k_f2["wi"], ALU.add)
                dve.wait_ge(tanh_done, 1)
                dve.tensor_scalar(bo1[:, :], k_x1["bo"], tg[:, 1:2], None, ALU.mult)
                dve.tensor_scalar(bout3[:, :], k_x3["bout"], tg[:, 3:4], None, ALU.mult)
                dve.tensor_tensor(bv1[:, :], k_x1["bv"], k_const["pmask"], ALU.mult)
                dve.tensor_tensor(bv3[:, :], k_a3["bv"], k_const["pmask"], ALU.mult)
                dve.tensor_scalar(scaled[:, 0:1], k_x1["bq"], HD ** -0.5, None, ALU.mult)
                dve.tensor_scalar(scaled[:, 1:2], k_a3["bq"], HD ** -0.5, None, ALU.mult)
                dve.scalar_tensor_tensor(scaled[:, 2:3], k_x3["qn"], XD ** -0.5, k_x3["kn"], ALU.mult, ALU.mult)
                for h2 in range(2):
                    m = dve.memset(v_blocks[64 * h2:64 * h2 + 64, :, :, :, 16 + h2:17 + h2], 1.0)
        stage("link means evacuated tanh ones_set", prepare)

        def layer_norm(src, dst, dstT=None, gain=None, bias=None, also=None):
            def body(block, link_sem, normed, turned):
                stats = small[:, 0:24].rearrange("p (t s) -> p t s", t=TILES)
                mv = small[:, 24:32].rearrange("p (t s) -> p t s", t=TILES)
                ve, rs, tmp = small[:, 32:36], small[:, 36:40], small[:, 40:44]

                @block.vector
                def _(dve):
                    link = Chain(dve, link_sem)
                    link.last_of([dve.bn_stats(stats[:, t, :], src[:, t, :]) for t in range(TILES)])
                    link.last_of([dve.bn_aggr(mv[:, t, :], stats[:, t, :]) for t in range(TILES)])
                    link(dve.tensor_scalar(ve, mv[:, :, 1], LN_EPS, None, ALU.add))
                    rsqrt(dve, link, rs, ve, tmp)
                    for t in range(TILES):
                        dve.tensor_scalar(dst[:, t, :], src[:, t, :], mv[:, t, 0:1], rs[:, t:t + 1],
                                          ALU.subtract, ALU.mult).then_inc(normed, 1)

                if dstT is None:
                    return

                @block.tensor
                def _(pe):
                    for t in range(TILES):
                        pe.wait_ge(normed, t + 1)
                        m = pe.transpose(banks[0][:, t * P:(t + 1) * P], dst[:, t, :], ident)
                    m.then_inc(turned, 1)

                @block.scalar
                def _(act):
                    act.wait_ge(turned, 1)
                    if gain is None:
                        act.copy(dstT, banks[0][:, :])
                    else:
                        bank = banks[0][:, :].rearrange("p (b s) -> p b s", s=SEQ)
                        act.activation(dstT, bank, ACT.Identity, bias=bias, scale=gain)
                        if also is not None:
                            act.activation(also, banks[0][:, :], ACT.Identity, bias=bias, scale=gain)
            stage("link normed turned", body)

        def top_two(dve, link, scores, n, at):
            best = small[:, at:at + 32].rearrange("p (t s) -> p t s", t=TILES)
            where = small[:, at + 32:at + 64].bitcast(U32).rearrange("p (t s) -> p t s", t=TILES)
            place = small[:, at + 64:at + 72].rearrange("p (t s) -> p t s", t=TILES)
            link.last_of([dve.max(best[:, t, :], scores[:, t, :]) for t in range(TILES)])
            link.last_of([dve.max_index(where[:, t, :], best[:, t, :], scores[:, t, :]) for t in range(TILES)])
            link(dve.tensor_copy(place, where[:, :, 0:2]))
            return best, place

        def spread(dve, link, dst, tmp, place, first, second, n):
            iota = k_const["iota"][:, 0:n].unsqueeze(1).to_broadcast([P, TILES, n])

            def wide(a):
                return a.to_broadcast([P, TILES, n])
            link.last_of([dve.tensor_tensor(dst, iota, wide(place[:, :, 0:1]), ALU.is_equal),
                          dve.tensor_tensor(tmp, iota, wide(place[:, :, 1:2]), ALU.is_equal)])
            link.last_of([dve.tensor_tensor(dst, dst, wide(first), ALU.mult),
                          dve.tensor_tensor(tmp, tmp, wide(second), ALU.mult)])
            link(dve.tensor_tensor(dst, dst, tmp, ALU.add))

        def attention(src_q, src_kv, w, scale_bias, k_bias, v_bias, neg, anyrow, finish):
            qT = work[:, 0:512]
            kT = work[:, 512:1024]
            kx = work[:, 1024:9216].rearrange("p (b h k) -> p b h k", b=TILES * PAIR, h=HEADS)
            s_sb = [work[:, 9216 + 1024 * i:10240 + 1024 * i] for i in range(2)]
            p_sb = s_sb
            pT = [work[:, 11264:12288], work[:, 12288:13312]]
            mx = small[:, 0:64].rearrange("p (t h) -> p t h", t=TILES)
            rc = small[:, 64:128].rearrange("p (t h) -> p t h", t=TILES)
            o_sb = [small[:, 128 + D * i:128 + D * (i + 1)] for i in range(2)]
            oT = [small[:, 384 + D * i:384 + D * (i + 1)] for i in range(2)]
            k_const_h = k_const["hmask"]

            def body(block, projected, q_ready, k_ready, v_ready, kx_pool, kx_dve, scored, link_sem,
                     s_ready, p_ready, turned, pT_ready, mixed, o_ready, o_turned, oT_ready, done, taken):
                def heads(a):
                    return a.rearrange("p (h k) -> p h k", k=SEQ)

                @block.tensor
                def _(pe):
                    pe.matmul(banks[4][:, :], w["wq"], src_q, start=True, stop=True).then_inc(projected, 1)
                    pe.matmul(banks[5][:, :], w["wk"], src_kv, start=True, stop=True).then_inc(projected, 1)
                    for b in range(TILES * PAIR):
                        for h2 in range(2):
                            m = pe.matmul(banks[6 + b // 4][64 * h2:64 * h2 + 64, (b % 4) * P:(b % 4 + 1) * P],
                                          src_kv[:, b * SEQ:(b + 1) * SEQ], w["wv"], start=True, stop=True)
                    m.then_inc(projected, 1)

                    def scores(t):
                        if t == 0:
                            pe.wait_ge(q_ready, 1)
                        pe.wait_ge(kx_dve, t + 1)
                        pe.wait_ge(kx_pool, t + 1)
                        if t >= 2:
                            pe.wait_ge(s_ready, t - 1)
                        for b in range(PAIR):
                            for half in range(2):
                                m = pe.matmul(banks[2 * (t % 2) + half][64 * b:64 * b + 64, :],
                                              qT[:, (2 * t + b) * SEQ:(2 * t + b + 1) * SEQ],
                                              kx[:, 2 * t + b, 8 * half:8 * half + 8, :], start=True, stop=True)
                        m.then_inc(scored, 1)

                    def turn(t):
                        pe.wait_ge(p_ready, t + 1)
                        if t == 0:
                            pe.wait_ge(k_ready, 1)
                            pe.wait_ge(q_ready, 1)
                        else:
                            pe.wait_ge(pT_ready, 2 * t)
                        for c in range(8):
                            m = pe.transpose(banks[4 + c // 4][:, (c % 4) * P:(c % 4 + 1) * P],
                                             p_sb[t % 2][:, c * P:(c + 1) * P], ident)
                        m.then_inc(turned, 1)

                    def mix(t):
                        pe.wait_ge(pT_ready, 2 * t + 2)
                        if t == 0:
                            pe.wait_ge(v_ready, 1)
                        else:
                            pe.wait_ge(o_ready, 2 * t)
                        for c in range(8):
                            m = pe.matmul(banks[6][:, c * 36:(c + 1) * 36], pT[t % 2][:, c * P:(c + 1) * P],
                                          v_blocks[:, t, c, :, :], start=True, stop=True)
                        m.then_inc(mixed, 1)

                    def project(t):
                        pe.wait_ge(o_ready, 2 * t + 2)
                        if t >= 1:
                            pe.wait_ge(taken, t)
                        pe.transpose(banks[7][:, 0:P], o_sb[t % 2], ident).then_inc(o_turned, 1)
                        pe.wait_ge(oT_ready, t + 1)
                        pe.matmul(banks[7][:, P:P + D], oT[t % 2], w["wo"], start=True, stop=True).then_inc(done, 1)

                    for step in range(TILES + 3):
                        if step < TILES:
                            scores(step)
                        if 0 <= step - 1 < TILES:
                            turn(step - 1)
                        if 0 <= step - 3 < TILES:
                            project(step - 3)
                        if 0 <= step - 2 < TILES:
                            mix(step - 2)

                @block.scalar
                def _(act):
                    act.wait_ge(projected, 1)
                    act.activation(qT, banks[4][:, :], ACT.Identity, scale=HD ** -0.5,
                                   bias=0.0 if scale_bias is None else scale_bias).then_inc(q_ready, 1)
                    act.wait_ge(projected, 2)
                    act.activation(kT, banks[5][:, :], ACT.Identity,
                                   bias=0.0 if k_bias is None else k_bias).then_inc(k_ready, 1)

                    def exps(t):
                        act.wait_ge(s_ready, t + 1)
                        act.activation(p_sb[t % 2], s_sb[t % 2], ACT.Exp).then_inc(p_ready, 1)

                    def take_pT(t):
                        act.wait_ge(turned, t + 1)
                        if t >= 2:
                            act.wait_ge(mixed, t - 1)
                        for half in range(2):
                            act.copy(pT[t % 2][:, 512 * half:512 * half + 512],
                                     banks[4 + half][:, :]).then_inc(pT_ready, 1)

                    def take_oT(t):
                        act.wait_ge(o_turned, t + 1)
                        act.copy(oT[t % 2], banks[7][:, 0:P]).then_inc(oT_ready, 1)

                    for step in range(TILES + 3):
                        if step < TILES:
                            exps(step)
                        if 0 <= step - 3 < TILES:
                            take_oT(step - 3)
                        if 0 <= step - 1 < TILES:
                            take_pT(step - 1)

                def key_blocks(engine, b, done_sem):
                    engine.tensor_tensor(kx[:, b, :, :],
                                         kT[:, b * SEQ:(b + 1) * SEQ].unsqueeze(1).to_broadcast([P, HEADS, SEQ]),
                                         k_const_h.unsqueeze(2).to_broadcast([P, HEADS, SEQ]),
                                         ALU.mult).then_inc(done_sem, 1)

                @block.gpsimd
                def _(pool):
                    pool.wait_ge(k_ready, 1)
                    for t in range(TILES):
                        key_blocks(pool, 2 * t + 1, kx_pool)

                @block.vector
                def _(dve):
                    link = Chain(dve, link_sem)
                    dve.wait_ge(k_ready, 1)
                    key_blocks(dve, 0, kx_dve)
                    key_blocks(dve, 2, kx_dve)
                    dve.wait_ge(projected, 3)
                    pm = k_const["pmask"].rearrange("p (c d) -> p c d", c=HP)
                    for t in range(TILES):
                        vv = banks[6 + t // 2][:, (t % 2) * 256:(t % 2) * 256 + 256]
                        for b in range(PAIR):
                            ins = dve.tensor_tensor(v_blocks[:, t, :, b, 0:16],
                                                    vv[:, b * P:(b + 1) * P].rearrange("p (c d) -> p c d", c=HP),
                                                    pm, ALU.mult)
                            if v_bias is not None:
                                link(ins)
                                ins = dve.tensor_tensor(v_blocks[:, t, :, b, 0:16], v_blocks[:, t, :, b, 0:16],
                                                        v_bias.rearrange("p (c d) -> p c d", c=HP), ALU.add)
                    ins.then_inc(v_ready, 1)

                    def shift(t):
                        dve.wait_ge(scored, t + 1)
                        if t >= 2:
                            dve.wait_ge(turned, t - 1)
                        for half in range(2):
                            s = heads(banks[2 * (t % 2) + half][:, :])
                            d = heads(s_sb[t % 2][:, 512 * half:512 * half + 512])
                            hs = slice(8 * half, 8 * half + 8)
                            if neg is not None:
                                link(dve.tensor_tensor(d, s, neg[:, t, :].unsqueeze(1).to_broadcast([P, 8, SEQ]),
                                                       ALU.add))
                                s = d
                            link(dve.tensor_reduce(mx[:, t, hs], s, AX, ALU.max))
                            ins = dve.tensor_tensor(d, s, mx[:, t, hs].unsqueeze(2).to_broadcast([P, 8, SEQ]),
                                                    ALU.subtract)
                            if half == 0:
                                link(ins)
                        ins.then_inc(s_ready, 1)

                    def normalise(t):
                        dve.wait_ge(mixed, t + 1)
                        o = banks[6][:, 0:288].rearrange("p (c b d) -> p c b d", c=HP, b=PAIR)
                        rv = rc[:, t, :].rearrange("p (c h) -> p c h", c=HP)
                        link.last_of([dve.reciprocal(rv[64 * b:64 * b + 64], o[64 * b:64 * b + 64, :, b, 16:18])
                                      for b in range(PAIR)])
                        if anyrow is not None:
                            link(dve.tensor_scalar(rc[:, t, :], rc[:, t, :], anyrow[:, t:t + 1], None, ALU.mult))
                        for b in range(PAIR):
                            r = slice(64 * b, 64 * b + 64)
                            dve.tensor_tensor(o_sb[t % 2][r].rearrange("p (c h d) -> p c h d", c=HP, h=2),
                                              o[r, :, b, 0:16].rearrange("p c (h d) -> p c h d", h=2),
                                              rv[r].unsqueeze(3).to_broadcast([SEQ, HP, 2, HD]),
                                              ALU.mult).then_inc(o_ready, 1)

                    for step in range(TILES + 3):
                        if step < TILES:
                            shift(step)
                        if 0 <= step - 3 < TILES:
                            dve.wait_ge(done, step - 2)
                            finish(dve, step - 3, banks[7][:, P:P + D]).then_inc(taken, 1)
                        if 0 <= step - 2 < TILES:
                            normalise(step - 2)
                        if step == 0:
                            for t in range(2, TILES):
                                key_blocks(dve, 2 * t, kx_dve)
            stage("projected q_ready k_ready v_ready kx_pool kx_dve scored link s_ready p_ready turned pT_ready "
                  "mixed o_ready o_turned oT_ready done taken", body)

        def add_gated(gate):
            return lambda dve, t, y: dve.scalar_tensor_tensor(x[:, t, :], y, tg[:, gate:gate + 1], x[:, t, :],
                                                              ALU.mult, ALU.add)

        def load_block(i):
            def body(block, loaded, turned, link_sem):
                xs = args["x"].rearrange("(i t p) d -> i p t d", t=TILES, p=P)
                cs = args["ctx"].rearrange("(i t p) d -> i p t d", t=TILES, p=P)
                m2 = args["mask2"].rearrange("(i t p) k -> i p t k", t=TILES, p=P)
                m3 = args["mask3"].rearrange("(i b) k -> i b k", b=TILES * PAIR)

                @block.sync
                def _(sp):
                    sp.dma_start(x[:, :, :], xs[bass.ds(i, 1)].rearrange("a p t d -> (a p) t d")).then_inc(loaded, 16)
                    sp.dma_start(ctok[:, :, :], cs[bass.ds(i, 1)].rearrange("a p t d -> (a p) t d")).then_inc(loaded, 16)
                    sp.dma_start(mask2_words[:, :, :], m2[bass.ds(i, 1)].rearrange("a p t k -> (a p) t k")).then_inc(loaded, 16)
                    sp.dma_start(mask3_words[:, :, :], m3[bass.ds(i, 1)].to_broadcast([P, TILES * PAIR, SEQ // 4])).then_inc(loaded, 16)
                    sp.wait_ge(loaded, 64)

                @block.tensor
                def _(pe):
                    pe.wait_ge(loaded, 64)
                    for t in range(TILES):
                        m = pe.transpose(banks[0][:, t * P:(t + 1) * P], ctok[:, t, :], ident)
                    m.then_inc(turned, 1)

                @block.scalar
                def _(act):
                    act.wait_ge(turned, 1)
                    act.copy(cT[:, :], banks[0][:, :])

                @block.vector
                def _(dve):
                    link = Chain(dve, link_sem)
                    dve.wait_ge(loaded, 64)
                    link(dve.tensor_scalar(neg2[:, :, :], mask2[:, :, :], NEG, None, ALU.mult))
                    link(dve.tensor_reduce(any2[:, :], neg2[:, :, :], AX, ALU.max))
                    dve.tensor_scalar(any2[:, :], any2[:, :], 0.5 * NEG, None, ALU.is_gt)
                    dve.tensor_scalar(neg3[:, :, 0, :], mask3[:, :, :], -NEG, NEG, ALU.mult, ALU.add)
            stage("loaded turned link", body)

        def store_block(i):
            def body(block, stored):
                os_ = out.rearrange("(i t p) d -> i p t d", t=TILES, p=P)

                @block.sync
                def _(sp):
                    sp.dma_start(os_[bass.ds(i, 1)].rearrange("a p t d -> (a p) t d"), x[:, :, :]).then_inc(stored, 16)
                    sp.wait_ge(stored, 16)
            stage("stored", body)

        def retention():
            kv = work[:, 0:512].rearrange("p (t d) -> p t d", t=TILES)
            part = work[:, 512:1024].rearrange("p (t d) -> p t d", t=TILES)

            def body(block, squared, summed, link_sem):
                @block.gpsimd
                def _(pool):
                    pool.tensor_tensor(kv, ctok[:, :, :], ctok[:, :, :], ALU.mult).then_inc(squared, 1)

                @block.tensor
                def _(pe):
                    pe.wait_ge(squared, 1)
                    for t in range(TILES):
                        m = pe.matmul(banks[0][:, t * D:(t + 1) * D], k_const["decay"], kv[:, t, :],
                                      start=True, stop=True)
                    m.then_inc(summed, 1)

                @block.vector
                def _(dve):
                    link = Chain(dve, link_sem)
                    dve.wait_ge(summed, 1)
                    link(dve.scalar_tensor_tensor(part, banks[0][:, :].rearrange("p (t d) -> p t d", t=TILES),
                                                  tg[:, 0:1], xn[:, :, :], ALU.mult, ALU.mult))
                    dve.tensor_tensor(x[:, :, :], x[:, :, :], part, ALU.add)
            stage("squared summed link", body)

        def ffn0():
            logits = small[:, 0:68].rearrange("p (t e) -> p t e", t=TILES)
            lg = small[:, 72:136].rearrange("p (t e) -> p t e", t=TILES)
            halves = small[:, 136:144].rearrange("p (t s) -> p t s", t=TILES)
            sig = small[:, 144:152].rearrange("p (t s) -> p t s", t=TILES)
            rest = small[:, 152:156].rearrange("p (t s) -> p t s", t=TILES)
            comb = small[:, 256:320].rearrange("p (t e) -> p t e", t=TILES)
            tmp = small[:, 320:384].rearrange("p (t e) -> p t e", t=TILES)
            sil = [work[:, 512 * i:512 * i + 512] for i in range(2)]
            hid = [work[:, 1024 + 512 * i:1536 + 512 * i] for i in range(2)]
            hidT = [work[:, 2048 + 512 * i:2560 + 512 * i] for i in range(2)]
            steps = [(t, g) for t in range(TILES) for g in range(5)]

            def body(block, routed, halves_ready, sig_ready, comb_ready, link_sem, up_done, sil_ready, hid_ready,
                     turned, hidT_ready, down_done, taken):
                def h_of(s):
                    return h_shared[:, (s // 5) % 2, :] if steps[s][1] == 4 else hid[s % 2]

                @block.tensor
                def _(pe):
                    for t in range(TILES):
                        m = pe.matmul(banks[6][:, t * 17:(t + 1) * 17], xnT[:, t * P:(t + 1) * P], k_l0["router"],
                                      start=True, stop=True)
                    m.then_inc(routed, 1)

                    def up(s):
                        t, g = steps[s]
                        if s >= 2:
                            pe.wait_ge(hid_ready, s - 1)
                        a, b = banks[2 * (s % 2)], banks[2 * (s % 2) + 1]
                        xt = xnT[:, t * P:(t + 1) * P]
                        if g < 4:
                            m = pe.matmul(a[:, :], xt, k_l0["gu"][:, g * 512:(g + 1) * 512], start=True, stop=True)
                        else:
                            pe.matmul(a[:, 0:352], xt, k_l0["sgu"][:, 0:352], start=True, stop=True)
                            m = pe.matmul(b[:, 0:352], xt, k_l0["sgu"][:, 352:704], start=True, stop=True)
                        m.then_inc(up_done, 1)

                    def turn(s):
                        pe.wait_ge(hid_ready, s + 1)
                        if s >= 2:
                            pe.wait_ge(hidT_ready, s - 1)
                        for c in range(3 if steps[s][1] == 4 else 2):
                            m = pe.transpose(banks[4 + s % 2][:, c * P:(c + 1) * P], h_of(s)[:, c * P:(c + 1) * P],
                                             ident)
                        m.then_inc(turned, 1)

                    def down(s):
                        t, g = steps[s]
                        pe.wait_ge(hidT_ready, s + 1)
                        if g == 0 and t >= 2:
                            pe.wait_ge(taken, t - 1)
                        if s == 0:
                            pe.wait_ge(comb_ready, 1)
                        n = 3 if g == 4 else 2
                        for c in range(n):
                            m = pe.matmul(banks[6 + t % 2][:, 0:D], hidT[s % 2][:, c * P:(c + 1) * P],
                                          k_l0["down"][:, (2 * g + c) * D:(2 * g + c + 1) * D],
                                          start=(g == 0 and c == 0), stop=(g == 4 and c == 2))
                        m.then_inc(down_done, 1)

                    n = len(steps)
                    for s in range(n + 2):
                        if s < n:
                            up(s)
                        if 0 <= s - 2 < n:
                            down(s - 2)
                        if 0 <= s - 1 < n:
                            turn(s - 1)

                @block.scalar
                def _(act):
                    act.wait_ge(halves_ready, 1)
                    act.activation(sig, halves, ACT.Tanh).then_inc(sig_ready, 1)

                    def silu(s):
                        act.wait_ge(up_done, s + 1)
                        if s >= 2:
                            act.wait_ge(hid_ready, s - 1)
                        n = 352 if steps[s][1] == 4 else 256
                        act.activation(sil[s % 2][:, 0:n], banks[2 * (s % 2)][:, 0:n], ACT.Silu).then_inc(sil_ready, 1)

                    def take_T(s):
                        act.wait_ge(turned, s + 1)
                        if s >= 2:
                            act.wait_ge(down_done, s - 1)
                        n = 384 if steps[s][1] == 4 else 256
                        act.copy(hidT[s % 2][:, 0:n], banks[4 + s % 2][:, 0:n]).then_inc(hidT_ready, 1)

                    for s in range(len(steps) + 1):
                        if s < len(steps):
                            silu(s)
                        if s >= 1:
                            take_T(s - 1)

                @block.vector
                def _(dve):
                    link = Chain(dve, link_sem)
                    dve.wait_ge(routed, 1)
                    link(dve.tensor_copy(logits, banks[6][:, 0:68].rearrange("p (t e) -> p t e", t=TILES)))
                    link(dve.tensor_copy(lg, logits[:, :, 0:16]))
                    best, place = top_two(dve, link, lg, 16, 160)
                    link(dve.tensor_tensor(halves[:, :, 0:1], best[:, :, 0:1], best[:, :, 1:2], ALU.subtract))
                    link(dve.tensor_scalar(halves[:, :, 0:1], halves[:, :, 0:1], 0.5, None, ALU.mult))
                    dve.tensor_scalar(halves[:, :, 1:2], logits[:, :, 16:17], 0.5, None,
                                      ALU.mult).then_inc(halves_ready, 1)
                    dve.wait_ge(sig_ready, 1)
                    link(dve.tensor_scalar(sig, sig, 0.5, 0.5, ALU.mult, ALU.add))
                    link(dve.tensor_scalar(rest, sig[:, :, 0:1], -1.0, 1.0, ALU.mult, ALU.add))
                    spread(dve, link, comb, tmp, place, sig[:, :, 0:1], rest, 16)
                    dve.sem_inc(comb_ready, 1)

                    def gate_up(s):
                        t, g = steps[s]
                        dve.wait_ge(sil_ready, s + 1)
                        if s >= 2:
                            dve.wait_ge(turned, s - 1)
                        a, b = banks[2 * (s % 2)], banks[2 * (s % 2) + 1]
                        if g < 4:
                            q = sil[s % 2][:, 0:256].rearrange("p (e f) -> p e f", e=4)
                            c = comb[:, t, 4 * g:4 * g + 4].unsqueeze(2).to_broadcast([P, 4, 64])
                            link(dve.tensor_tensor(q, q, c, ALU.mult))
                            dve.tensor_tensor(h_of(s)[:, 0:256], a[:, 256:512], sil[s % 2][:, 0:256],
                                              ALU.mult).then_inc(hid_ready, 1)
                        else:
                            dve.scalar_tensor_tensor(h_of(s)[:, 0:352], b[:, 0:352], sig[:, t, 1:2],
                                                     sil[s % 2][:, 0:352], ALU.mult, ALU.mult).then_inc(hid_ready, 1)

                    n = len(steps)
                    for s in range(n + 2):
                        if s < n:
                            gate_up(s)
                        if s >= 2 and steps[s - 2][1] == 4:
                            t = steps[s - 2][0]
                            dve.wait_ge(down_done, s - 1)
                            dve.scalar_tensor_tensor(x[:, t, :], banks[6 + t % 2][:, 0:D], tg[:, 4:5], x[:, t, :],
                                                     ALU.mult, ALU.add).then_inc(taken, 1)
            stage("routed halves sig comb link up sil hid turned hidT down taken", body)

        def ffn1():
            lg = small[:, 72:104].rearrange("p (t e) -> p t e", t=TILES)
            half = small[:, 136:140].rearrange("p (t s) -> p t s", t=TILES)
            sig = small[:, 144:148].rearrange("p (t s) -> p t s", t=TILES)
            rest = small[:, 152:156].rearrange("p (t s) -> p t s", t=TILES)
            comb = small[:, 256:288].rearrange("p (t e) -> p t e", t=TILES)
            tmp = small[:, 288:320].rearrange("p (t e) -> p t e", t=TILES)
            comb_e = small[:, 320:352].rearrange("p (e t) -> p e t", t=TILES)
            combT = small[0:8, 384:896]
            sums = small[:, 352:360].rearrange("p (t s) -> p t s", t=TILES)
            vs, rs, t4 = small[:, 360:364], small[:, 364:368], small[:, 368:372]
            stats = small[:, 896:920].rearrange("p (t s) -> p t s", t=TILES)
            mv = small[:, 920:928].rearrange("p (t s) -> p t s", t=TILES)
            v2, r2, u4 = small[:, 928:932], small[:, 932:936], small[:, 936:940]
            hT = [work[:, 2048 * i:2048 * i + 2048].rearrange("p (c n) -> p c n", c=4) for i in range(2)]
            sq = [work[:, 4096 + 2048 * i:6144 + 2048 * i].rearrange("p (c n) -> p c n", c=4) for i in range(2)]
            y = [work[:, 8192 + 512 * i:8704 + 512 * i].rearrange("p (t d) -> p t d", t=TILES) for i in range(2)]
            z = [work[:, 9216 + 512 * i:9728 + 512 * i].rearrange("p (t d) -> p t d", t=TILES) for i in range(2)]
            acc = work[:, 10240:10752].rearrange("p (t d) -> p t d", t=TILES)

            def body(block, routed, half_ready, sig_ready, comb_ready, link_sem, up_done, hT_ready, sq_pool, sq_dve,
                     down_done, y_raw, y_ready, z_ready, added, combT_done, combT_ready, last_done, pool_link):
                @block.tensor
                def _(pe):
                    for t in range(TILES):
                        m = pe.matmul(banks[3][:, t * 8:(t + 1) * 8], xnT[:, t * P:(t + 1) * P], k_f1["wr"],
                                      start=True, stop=True)
                    m.then_inc(routed, 1)

                    def up(e):
                        for c in range(4):
                            n = 4 * e + c
                            if n >= 3:
                                pe.wait_ge(hT_ready, n - 2)
                            pe.matmul(banks[n % 3][:, :], k_f1["w1"][:, e * 512 + c * P:e * 512 + (c + 1) * P], xnT[:, :],
                                      start=True, stop=True).then_inc(up_done, 1)

                    def down(e):
                        pe.wait_ge(hT_ready, 4 * e + 4)
                        pe.wait_ge(sq_pool, 2 * e + 2)
                        pe.wait_ge(sq_dve, 2 * e + 2)
                        if e >= 2:
                            pe.wait_ge(y_raw, e - 1)
                        for t in range(TILES):
                            zb = banks[4 + 2 * (e % 2) + t // 2][:, (t % 2) * 130:(t % 2) * 130 + 130]
                            for c in range(4):
                                pe.matmul(zb[:, 0:129], hT[e % 2][:, c, t * P:(t + 1) * P], w_f1d[:, c, e, :],
                                          start=(c == 0), stop=(c == 3))
                            for c in range(4):
                                m = pe.matmul(zb[:, 129:130], sq[e % 2][:, c, t * P:(t + 1) * P], ones[:, 0:1],
                                              start=(c == 0), stop=(c == 3))
                        m.then_inc(down_done, 1)

                    for e in range(9):
                        if e < 8:
                            up(e)
                        if e >= 1:
                            down(e - 1)
                    pe.wait_ge(comb_ready, 1)
                    for t in range(TILES):
                        m = pe.transpose(banks[3][0:8, t * P:(t + 1) * P], comb[:, t, :], ident)
                    m.then_inc(combT_done, 1)
                    pe.wait_ge(combT_ready, 1)
                    for t in range(TILES):
                        m = pe.matmul(banks[3][:, t * D:(t + 1) * D], combT[:, t * P:(t + 1) * P], w_f1b[:, :],
                                      start=True, stop=True)
                    m.then_inc(last_done, 1)

                @block.scalar
                def _(act):
                    def relu_up(e):
                        for c in range(4):
                            n = 4 * e + c
                            act.wait_ge(up_done, n + 1)
                            if e >= 2 and c == 0:
                                act.wait_ge(down_done, e - 1)
                            act.activation(hT[e % 2][:, c, :], banks[n % 3][:, :], ACT.Relu,
                                           bias=k_f1["b1"][:, n:n + 1]).then_inc(hT_ready, 1)

                    for e in range(10):
                        if e == 0:
                            act.wait_ge(half_ready, 1)
                            act.activation(sig, half, ACT.Tanh).then_inc(sig_ready, 1)
                        if e < 8:
                            relu_up(e)
                        if e >= 2:
                            act.wait_ge(y_raw, e - 1)
                            act.activation(y[e % 2], y[e % 2], ACT.Relu).then_inc(y_ready, 1)
                    act.wait_ge(combT_done, 1)
                    act.copy(combT, banks[3][0:8, :]).then_inc(combT_ready, 1)

                @block.gpsimd
                def _(pool):
                    link = Chain(pool, pool_link)
                    link(pool.memset(acc, 0.0))
                    for e in range(10):
                        if e < 8:
                            for c in (1, 3):
                                pool.wait_ge(hT_ready, 4 * e + c + 1)
                                if e >= 2 and c == 1:
                                    pool.wait_ge(down_done, e - 1)
                                pool.tensor_tensor(sq[e % 2][:, c, :], hT[e % 2][:, c, :], hT[e % 2][:, c, :],
                                                   ALU.mult).then_inc(sq_pool, 1)
                        if e >= 2:
                            q = e - 2
                            pool.wait_ge(z_ready, q + 1)
                            g2 = k_f1["g2"][:, q * D:(q + 1) * D].unsqueeze(1).to_broadcast([P, TILES, D])
                            link(pool.tensor_tensor(z[q % 2], z[q % 2], g2, ALU.mult))
                            ins = pool.tensor_tensor(acc, acc, z[q % 2], ALU.add)
                            ins.then_inc(added, 1)
                            pool.wait_ge(added, q + 1)

                @block.vector
                def _(dve):
                    link = Chain(dve, link_sem)
                    dve.wait_ge(routed, 1)
                    link(dve.tensor_tensor(lg, banks[3][:, 0:32].rearrange("p (t e) -> p t e", t=TILES),
                                           k_f1["br"].unsqueeze(1).to_broadcast([P, TILES, 8]), ALU.add))
                    best, place = top_two(dve, link, lg, 8, 160)
                    link(dve.tensor_tensor(half, best[:, :, 0:1], best[:, :, 1:2], ALU.subtract))
                    dve.tensor_scalar(half, half, 0.5, None, ALU.mult).then_inc(half_ready, 1)
                    dve.wait_ge(sig_ready, 1)
                    link(dve.tensor_scalar(sig, sig, 0.5, 0.5, ALU.mult, ALU.add))
                    link(dve.tensor_scalar(rest, sig, -1.0, 1.0, ALU.mult, ALU.add))
                    spread(dve, link, comb, tmp, place, sig, rest, 8)
                    link(dve.tensor_copy(comb_e, comb.rearrange("p t e -> p e t")))
                    dve.sem_inc(comb_ready, 1)

                    def squares(e):
                        for c in (0, 2):
                            dve.wait_ge(hT_ready, 4 * e + c + 1)
                            if e >= 2 and c == 0:
                                dve.wait_ge(down_done, e - 1)
                            dve.tensor_tensor(sq[e % 2][:, c, :], hT[e % 2][:, c, :], hT[e % 2][:, c, :],
                                              ALU.mult).then_inc(sq_dve, 1)

                    def first_norm(e):
                        dve.wait_ge(down_done, e + 1)
                        zs = [banks[4 + 2 * (e % 2) + j][:, 0:260].rearrange("p (t d) -> p t d", t=2) for j in range(2)]
                        link.last_of([dve.tensor_copy(sums[:, 2 * j:2 * j + 2, :], zs[j][:, :, 128:130])
                                      for j in range(2)])
                        link(dve.tensor_scalar(sums, sums, 1.0 / 512, None, ALU.mult))
                        link(dve.tensor_tensor(t4, sums[:, :, 0], sums[:, :, 0], ALU.mult))
                        link(dve.tensor_tensor(vs, sums[:, :, 1], t4, ALU.subtract))
                        link(dve.tensor_scalar(vs, vs, 0.0, LN_EPS, ALU.max, ALU.add))
                        rsqrt(dve, link, rs, vs, t4)
                        if e >= 2:
                            dve.wait_ge(z_ready, e - 1)
                        for t in range(TILES):
                            ins = dve.scalar_tensor_tensor(y[e % 2][:, t, :], zs[t // 2][:, t % 2, 0:D], rs[:, t:t + 1],
                                                           expert_bias[:, e, :], ALU.mult, ALU.add)
                            if t < TILES - 1:
                                continue
                            ins.then_inc(y_raw, 1)

                    def second_norm(e):
                        dve.wait_ge(y_ready, e + 1)
                        link.last_of([dve.bn_stats(stats[:, t, :], y[e % 2][:, t, :]) for t in range(TILES)])
                        link.last_of([dve.bn_aggr(mv[:, t, :], stats[:, t, :]) for t in range(TILES)])
                        link(dve.tensor_scalar(v2, mv[:, :, 1], LN_EPS, None, ALU.add))
                        rsqrt(dve, link, r2, v2, u4)
                        link(dve.tensor_tensor(r2, r2, comb_e[:, e, :], ALU.mult))
                        if e >= 2:
                            dve.wait_ge(added, e - 1)
                        for t in range(TILES):
                            ins = dve.tensor_scalar(z[e % 2][:, t, :], y[e % 2][:, t, :], mv[:, t, 0:1], r2[:, t:t + 1],
                                                    ALU.subtract, ALU.mult)
                        ins.then_inc(z_ready, 1)

                    for e in range(10):
                        if e < 8:
                            squares(e)
                        if 1 <= e < 9:
                            first_norm(e - 1)
                        if e >= 2:
                            second_norm(e - 2)
                    dve.wait_ge(last_done, 1)
                    dve.wait_ge(added, 8)
                    link(dve.tensor_tensor(acc, acc, banks[3][:, :].rearrange("p (t d) -> p t d", t=TILES), ALU.add))
                    dve.scalar_tensor_tensor(x[:, :, :], acc, tg[:, 5:6], x[:, :, :], ALU.mult, ALU.add)
            stage("routed half sig comb link up hT sqp sqd down yraw yready zready added combTd combTr last plink", body)

        def ffn2():
            lg = small[:, 72:104].rearrange("p (t e) -> p t e", t=TILES)
            ex = small[:, 104:120].rearrange("p (t e) -> p t e", t=TILES)
            den = small[:, 120:124].rearrange("p (t s) -> p t s", t=TILES)
            top = small[:, 124:132].rearrange("p (t s) -> p t s", t=TILES)
            comb = small[:, 256:272].rearrange("p (t e) -> p t e", t=TILES)
            tmp = small[:, 272:288].rearrange("p (t e) -> p t e", t=TILES)
            r = [[work[:, 2048 * i + 512 * e:2048 * i + 512 * e + 512] for e in range(4)] for i in range(2)]
            gT = [work[:, 4096 + 512 * i:4608 + 512 * i] for i in range(2)]

            def body(block, routed, shifted, exp_ready, comb_ready, link_sem, up_done, r_ready, pair_ready,
                     sum_ready, turned, gT_ready, down_done, taken):
                @block.tensor
                def _(pe):
                    for t in range(TILES):
                        m = pe.matmul(banks[6][:, t * 4:(t + 1) * 4], xnT[:, t * P:(t + 1) * P], k_f2["wg"],
                                      start=True, stop=True)
                    m.then_inc(routed, 1)

                    def up(t):
                        for e in range(4):
                            n = 4 * t + e
                            if n >= 4:
                                pe.wait_ge(r_ready, n - 3)
                            pe.matmul(banks[e][:, :], xnT[:, t * P:(t + 1) * P], w_f2e[:, e, :],
                                      start=True, stop=True).then_inc(up_done, 1)

                    def turn(t):
                        pe.wait_ge(sum_ready, t + 1)
                        if t >= 2:
                            pe.wait_ge(gT_ready, t - 1)
                        for c in range(4):
                            m = pe.transpose(banks[4 + t % 2][:, c * P:(c + 1) * P], r[t % 2][0][:, c * P:(c + 1) * P],
                                             ident)
                        m.then_inc(turned, 1)
                        pe.wait_ge(gT_ready, t + 1)
                        if t >= 2:
                            pe.wait_ge(taken, t - 1)
                        for c in range(4):
                            m = pe.matmul(banks[6 + t % 2][:, 0:D], gT[t % 2][:, c * P:(c + 1) * P],
                                          k_f2["wo"][:, c * D:(c + 1) * D], start=(c == 0), stop=(c == 3))
                        m.then_inc(down_done, 1)

                    for t in range(TILES + 1):
                        if t < TILES:
                            up(t)
                        if t == 0:
                            pe.wait_ge(comb_ready, 1)
                        if t >= 1:
                            turn(t - 1)

                @block.scalar
                def _(act):
                    act.wait_ge(shifted, 1)
                    act.activation(ex, lg[:, :, 0:4], ACT.Exp).then_inc(exp_ready, 1)
                    act.wait_ge(comb_ready, 1)
                    for t in range(TILES + 1):
                        if t < TILES:
                            for e in range(4):
                                act.wait_ge(up_done, 4 * t + e + 1)
                                if t >= 2 and e == 0:
                                    act.wait_ge(turned, t - 1)
                                act.activation(r[t % 2][e], banks[e][:, :], ACT.Relu,
                                               scale=comb[:, t, e:e + 1]).then_inc(r_ready, 1)
                        if t >= 1:
                            act.wait_ge(turned, t)
                            if t >= 3:
                                act.wait_ge(down_done, t - 2)
                            act.copy(gT[(t - 1) % 2], banks[4 + (t - 1) % 2][:, :]).then_inc(gT_ready, 1)

                @block.gpsimd
                def _(pool):
                    for t in range(TILES):
                        pool.wait_ge(r_ready, 4 * t + 4)
                        pool.tensor_tensor(r[t % 2][2], r[t % 2][2], r[t % 2][3], ALU.add).then_inc(pair_ready, 1)

                @block.vector
                def _(dve):
                    link = Chain(dve, link_sem)
                    link(dve.memset(lg, NEG))
                    dve.wait_ge(routed, 1)
                    link(dve.tensor_tensor(lg[:, :, 0:4], banks[6][:, 0:16].rearrange("p (t e) -> p t e", t=TILES),
                                           k_f2["bg"].unsqueeze(1).to_broadcast([P, TILES, 4]), ALU.add))
                    best, place = top_two(dve, link, lg, 8, 160)
                    link(dve.tensor_tensor(lg[:, :, 0:4], lg[:, :, 0:4], best[:, :, 0:1].to_broadcast([P, TILES, 4]),
                                           ALU.subtract))
                    dve.sem_inc(shifted, 1)
                    dve.wait_ge(exp_ready, 1)
                    link(dve.tensor_reduce(den[:, :, 0], ex, AX, ALU.add))
                    link(dve.reciprocal(den, den))
                    link(dve.tensor_tensor(ex, ex, den.to_broadcast([P, TILES, 4]), ALU.mult))
                    link.last_of([dve.memset(top, 1.0)])
                    spread(dve, link, comb, tmp, place, top[:, :, 0:1], top[:, :, 1:2], 4)
                    link(dve.tensor_tensor(comb, comb, ex, ALU.mult))
                    dve.sem_inc(comb_ready, 1)
                    for t in range(TILES + 1):
                        if t < TILES:
                            dve.wait_ge(r_ready, 4 * t + 2)
                            link(dve.tensor_tensor(r[t % 2][0], r[t % 2][0], r[t % 2][1], ALU.add))
                            dve.wait_ge(pair_ready, t + 1)
                            dve.tensor_tensor(r[t % 2][0], r[t % 2][0], r[t % 2][2], ALU.add).then_inc(sum_ready, 1)
                        if t >= 1:
                            dve.wait_ge(down_done, t)
                            dve.scalar_tensor_tensor(x[:, t - 1, :], banks[6 + (t - 1) % 2][:, 0:D], tg[:, 6:7],
                                                     x[:, t - 1, :], ALU.mult, ALU.add).then_inc(taken, 1)
            stage("routed shifted expd comb link up r pair sum turned gT down taken", body)

        def perceiver():
            ssq = small[:, 0:64]
            rk = [small[:, 64 + 16 * i:80 + 16 * i] for i in range(4)]
            den = small[:, 160:176]
            oT = [work[:, 512 * i:512 * i + 512].rearrange("p (c q) -> p c q", c=8) for i in range(2)]
            qkt = [work[:, 1024 + 1024 * i:2048 + 1024 * i] for i in range(2)]
            kn_ = work[:, 3072:4096]
            kT = [work[:, 4096 + 1024 * i:5120 + 1024 * i] for i in range(2)]
            v = [work[:, 6144 + 1024 * i:7168 + 1024 * i] for i in range(2)]
            s_sb = [work[:, 8192 + 1024 * i:9216 + 1024 * i] for i in range(2)]
            pT = work[:, 10240:11264]
            qn_ = work[:, 11264:12288]

            def halves(a):
                return [a[:, 0:512], a[:, 512:1024]]

            def body(block, link_sem, q_done, qsq, q_normed, q_turned, q_ready, k_done, ksq, k_normed, k_turned,
                     kT_ready, v_done, v_ready, scored, mx_ready, p_ready, p_scaled, p_turned, pT_ready, mixed,
                     oT_ready, done, taken):
                @block.tensor
                def _(pe):
                    def queries(t):
                        if t >= 1:
                            pe.wait_ge(pT_ready, 2 * (2 * t))
                        for i in range(2):
                            m = pe.matmul(banks[i][:, :], latT(t), k_x3["wq"][:, 512 * i:512 * i + 512],
                                          start=True, stop=True)
                        m.then_inc(q_done, 1)

                    def latT(t):
                        return xnT[:, t * P:(t + 1) * P]

                    def turn_queries(t):
                        pe.wait_ge(q_normed, t + 1)
                        for c in range(8):
                            m = pe.transpose(banks[c // 4][:, (c % 4) * P:(c % 4 + 1) * P],
                                             qn_[:, c * P:(c + 1) * P], ident)
                        m.then_inc(q_turned, 1)

                    def keys_values(b):
                        if b >= 1:
                            pe.wait_ge(kT_ready, 2 * b)
                        for i in range(2):
                            m = pe.matmul(banks[2 + i][:, :], cxT[:, b, :, :], k_x3["wkv"][:, 512 * i:512 * i + 512],
                                          start=True, stop=True)
                        m.then_inc(k_done, 1)
                        if b >= 1:
                            pe.wait_ge(mx_ready, b)
                        for i in range(2):
                            m = pe.matmul(banks[4 + i][:, :], cxT[:, b, :, :],
                                          k_x3["wkv"][:, 1024 + 512 * i:1536 + 512 * i], start=True, stop=True)
                        m.then_inc(v_done, 1)

                    def turn_keys(b):
                        pe.wait_ge(k_normed, b + 1)
                        for c in range(8):
                            m = pe.transpose(banks[2 + c // 4][:, (c % 4) * P:(c % 4 + 1) * P],
                                             kn_[:, c * P:(c + 1) * P], ident)
                        m.then_inc(k_turned, 1)

                    def scores(b):
                        pe.wait_ge(kT_ready, 2 * b + 2)
                        pe.wait_ge(q_ready, 2 * (b // 2) + 2)
                        pe.wait_ge(v_ready, 2 * b + 2)
                        for c in range(8):
                            m = pe.matmul(banks[4 + c // 4][:, (c % 4) * P:(c % 4 + 1) * P],
                                          q_blocks[:, b % 2, c, :, :], kT[b % 2][:, c * P:(c + 1) * P],
                                          start=True, stop=True)
                        m.then_inc(scored, 1)

                    def turn_probs(b):
                        pe.wait_ge(p_scaled, b + 1)
                        if b % 2 == 0:
                            pe.wait_ge(q_ready, b + 2)
                        if b >= 1:
                            pe.wait_ge(pT_ready, 2 * b)
                        for c in range(8):
                            m = pe.transpose(banks[c // 4][:, (c % 4) * P:(c % 4 + 1) * P],
                                             s_sb[b % 2][:, c * P:(c + 1) * P], ident)
                        m.then_inc(p_turned, 1)

                    def mix(b):
                        pe.wait_ge(pT_ready, 2 * b + 2)
                        if b >= 1:
                            pe.wait_ge(oT_ready, 2 * b)
                        for c in range(8):
                            m = pe.matmul(banks[6][:, c * SEQ:(c + 1) * SEQ][0:64], v[b % 2][:, c * P:c * P + 64],
                                          pT[:, c * P:c * P + 64], start=True, stop=True)
                            m = pe.matmul(banks[6][:, c * SEQ:(c + 1) * SEQ][64:128], v[b % 2][:, c * P + 64:c * P + 128],
                                          pT[:, c * P + 64:c * P + 128], start=True, stop=True)
                        m.then_inc(mixed, 1)

                    def project(b):
                        pe.wait_ge(oT_ready, 2 * b + 2)
                        if b % 2 == 0 and b >= 2:
                            pe.wait_ge(taken, b // 2)
                        r = slice(64 * (b % 2), 64 * (b % 2) + 64)
                        for c in range(8):
                            m = pe.matmul(banks[7][r, 0:D], oT[b % 2][:, c, :], k_x3["wout"][:, c * D:(c + 1) * D],
                                          start=(c == 0), stop=(c == 7))
                        m.then_inc(done, 1)

                    for b in range(TILES * PAIR):
                        if b % 2 == 0:
                            queries(b // 2)
                        keys_values(b)
                        if b % 2 == 0:
                            turn_queries(b // 2)
                        turn_keys(b)
                        scores(b)
                        turn_probs(b)
                        mix(b)
                        project(b)

                @block.scalar
                def _(act):
                    for b in range(TILES * PAIR):
                        t = b // 2
                        if b % 2 == 0:
                            act.wait_ge(q_done, t + 1)
                            for i in range(2):
                                ins = act.activation(qkt[0][:, 512 * i:512 * i + 512], banks[i][:, :], ACT.Square)
                            ins.then_inc(qsq, 1)
                        act.wait_ge(k_done, b + 1)
                        for i in range(2):
                            if i == 0 and b >= 1:
                                act.wait_ge(k_normed, b)
                            ins = act.activation(qkt[1][:, 512 * i:512 * i + 512], banks[2 + i][:, :], ACT.Square)
                        ins.then_inc(ksq, 1)
                        act.wait_ge(v_done, b + 1)
                        if b >= 2:
                            act.wait_ge(mixed, b - 1)
                        for i in range(2):
                            act.copy(v[b % 2][:, 512 * i:512 * i + 512], banks[4 + i][:, :]).then_inc(v_ready, 1)
                        if b % 2 == 0:
                            act.wait_ge(q_turned, t + 1)
                            if b >= 1:
                                act.wait_ge(scored, b)
                            for h2 in range(2):
                                r = slice(64 * h2, 64 * h2 + 64)
                                for i in range(2):
                                    ins = act.copy(q_blocks[r, :, 4 * i:4 * i + 4, h2, :].rearrange("p b c q -> p c b q"),
                                                   banks[i][r, :].rearrange("p (c b q) -> p c b q", c=4, b=2))
                                ins.then_inc(q_ready, 1)
                        act.wait_ge(k_turned, b + 1)
                        if b >= 2:
                            act.wait_ge(scored, b - 1)
                        for i in range(2):
                            act.activation(kT[b % 2][:, 512 * i:512 * i + 512], banks[2 + i][:, :], ACT.Identity,
                                           scale=scaled[:, 2:3]).then_inc(kT_ready, 1)
                        act.wait_ge(mx_ready, b + 1)
                        act.activation(s_sb[b % 2], s_sb[b % 2], ACT.Exp).then_inc(p_ready, 1)
                        act.wait_ge(p_turned, b + 1)
                        if b >= 1:
                            act.wait_ge(mixed, b)
                        for i in range(2):
                            act.copy(pT[:, 512 * i:512 * i + 512], banks[i][:, :]).then_inc(pT_ready, 1)
                        act.wait_ge(mixed, b + 1)
                        if b >= 2:
                            act.wait_ge(done, b - 1)
                        for i in range(2):
                            r = slice(64 * i, 64 * i + 64)
                            act.copy(oT[b % 2][r], banks[6][r, :].rearrange("p (c q) -> p c q", c=8)).then_inc(oT_ready, 1)

                @block.vector
                def _(dve):
                    link = Chain(dve, link_sem)

                    def norms(sq, rows, at, dst, done_sem):
                        link(dve.tensor_reduce(ssq[:, 0:16], sq.rearrange("p (h d) -> p h d", d=XD), AX, ALU.add))
                        link(dve.tensor_scalar(ssq[:, 0:16], ssq[:, 0:16], 1.0 / XD, 1e-16, ALU.mult, ALU.max))
                        rsqrt(dve, link, ssq[:, 16:32], ssq[:, 0:16], ssq[:, 32:48])
                        for i in range(2):
                            ins = dve.tensor_tensor(dst[:, 512 * i:512 * i + 512].rearrange("p (h d) -> p h d", d=XD),
                                                    rows[i][:, :].rearrange("p (h d) -> p h d", d=XD),
                                                    ssq[:, 16 + 8 * i:24 + 8 * i].unsqueeze(2).to_broadcast([P, 8, XD]),
                                                    ALU.mult)
                        ins.then_inc(done_sem, 1)

                    for b in range(TILES * PAIR):
                        if b % 2 == 0:
                            dve.wait_ge(qsq, b // 2 + 1)
                            norms(qkt[0], banks[0:2], 0, qn_, q_normed)
                            dve.wait_ge(q_normed, b // 2 + 1)
                        dve.wait_ge(ksq, b + 1)
                        norms(qkt[1], banks[2:4], 0, kn_, k_normed)
                        dve.wait_ge(scored, b + 1)
                        if b >= 2:
                            dve.wait_ge(p_turned, b - 1)
                        s = s_sb[b % 2]
                        s3 = s.rearrange("p (c j) -> p c j", c=8)
                        nb = neg3[:, b, :, :].rearrange("p a s -> p (a s)")
                        link.last_of([dve.tensor_tensor(s3[:, 4 * i:4 * i + 4, :],
                                                        banks[4 + i][:, :].rearrange("p (c j) -> p c j", c=4),
                                                        nb.unsqueeze(1).to_broadcast([P, 4, P]), ALU.add)
                                      for i in range(2)])
                        link(dve.tensor_reduce(den[:, 0:8], s3, AX, ALU.max))
                        dve.tensor_tensor(s3, s3, den[:, 0:8].unsqueeze(2).to_broadcast([P, 8, P]),
                                          ALU.subtract).then_inc(mx_ready, 1)
                        dve.wait_ge(p_ready, b + 1)
                        link(dve.tensor_reduce(den[:, 8:16], s3, AX, ALU.add))
                        link(dve.reciprocal(den[:, 8:16], den[:, 8:16]))
                        dve.tensor_tensor(s3, s3, den[:, 8:16].unsqueeze(2).to_broadcast([P, 8, P]),
                                          ALU.mult).then_inc(p_scaled, 1)
                        if b % 2 == 1:
                            t = b // 2
                            dve.wait_ge(done, b + 1)
                            link(dve.scalar_tensor_tensor(x[:, t, :], banks[7][:, 0:D], tg[:, 3:4], x[:, t, :],
                                                          ALU.mult, ALU.add))
                            dve.tensor_tensor(x[:, t, :], x[:, t, :], bout3[:, :], ALU.add).then_inc(taken, 1)
            stage("link q_done qsq q_normed q_turned q_ready k_done ksq k_normed k_turned kT_ready v_done v_ready "
                  "scored mx_ready p_ready p_scaled p_turned pT_ready mixed oT_ready done taken", body)

        def rms_norm(src, gain, dst=None, dstT=None, gate=None):
            sq = work[:, 0:512].rearrange("p (t d) -> p t d", t=TILES)
            ms, rs, tmp = small[:, 0:4], small[:, 4:8], small[:, 8:12]

            def body(block, squared, link_sem, normed, turned):
                @block.gpsimd
                def _(pool):
                    pool.tensor_tensor(sq, src[:, :, :], src[:, :, :], ALU.mult).then_inc(squared, 1)

                @block.vector
                def _(dve):
                    link = Chain(dve, link_sem)
                    dve.wait_ge(squared, 1)
                    link(dve.tensor_reduce(ms, sq, AX, ALU.add))
                    link(dve.tensor_scalar(ms, ms, 1.0 / D, RMS_EPS, ALU.mult, ALU.add))
                    rsqrt(dve, link, rs, ms, tmp)
                    to = sq if gate is not None else dst
                    for t in range(TILES):
                        ins = dve.scalar_tensor_tensor(to[:, t, :], src[:, t, :], rs[:, t:t + 1], gain, ALU.mult, ALU.mult)
                        if gate is None:
                            ins.then_inc(normed, 1)
                        else:
                            link(ins)
                    if gate is not None:
                        dve.scalar_tensor_tensor(x[:, :, :], sq, gate, x[:, :, :], ALU.mult, ALU.add)

                if dstT is None:
                    return

                @block.tensor
                def _(pe):
                    for t in range(TILES):
                        pe.wait_ge(normed, t + 1)
                        m = pe.transpose(banks[0][:, t * P:(t + 1) * P], dst[:, t, :], ident)
                    m.then_inc(turned, 1)

                @block.scalar
                def _(act):
                    act.wait_ge(turned, 1)
                    act.copy(dstT, banks[0][:, :])
            stage("squared link normed turned", body)

        def ffn3(src):
            probs = small[:, 72:104].rearrange("p (t e) -> p t e", t=TILES)
            tot = small[:, 136:140].rearrange("p (t s) -> p t s", t=TILES)
            wts = small[:, 140:148].rearrange("p (t s) -> p t s", t=TILES)
            comb = small[:, 256:288].rearrange("p (t e) -> p t e", t=TILES)
            chosen = small[:, 288:320].rearrange("p (t e) -> p t e", t=TILES)
            tmp = small[:, 320:352].rearrange("p (t e) -> p t e", t=TILES)
            ran = small[:, 352:392].rearrange("p (t e) -> p t e", t=TILES + 1)
            top = small[:, 392:400].rearrange("p (t s) -> p t s", t=TILES)
            h = [work[:, 512 * i:512 * i + 512] for i in range(2)]
            hT = [work[:, 1024 + 512 * i:1536 + 512 * i] for i in range(2)]
            g = [work[:, 2048 + 512 * i:2560 + 512 * i] for i in range(2)]
            capacity = float(int(1.25 * BATCH * SEQ * 2 / 8))
            steps = [(t, q) for t in range(TILES) for q in range(4)]

            def body(block, routed, tanh_done, chosen_ready, ranked, comb_ready, link_sem, up_done, g_ready, h_ready,
                     turned, hT_ready, down_done, taken):
                @block.tensor
                def _(pe):
                    for t in range(TILES):
                        m = pe.matmul(banks[6][:, t * 8:(t + 1) * 8], xnT[:, t * P:(t + 1) * P], k_f3["wr"],
                                      start=True, stop=True)
                    m.then_inc(routed, 1)
                    pe.wait_ge(chosen_ready, 1)
                    for t in range(TILES):
                        pe.matmul(banks[7][:, t * 8:(t + 1) * 8], k_const["tri"], chosen[:, t, :],
                                  start=True, stop=False)
                        m = pe.matmul(banks[7][:, t * 8:(t + 1) * 8], ones[:, :], ran[:, t, :],
                                      start=False, stop=True)
                    m.then_inc(ranked, 1)

                    def up(s):
                        t, q = steps[s]
                        if s >= 2:
                            pe.wait_ge(g_ready, s - 1)
                        pe.matmul(banks[s % 2][:, :], xnT[:, t * P:(t + 1) * P], k_f3["w1"][:, q * 512:(q + 1) * 512],
                                  start=True, stop=True).then_inc(up_done, 1)

                    def turn(s):
                        pe.wait_ge(h_ready, s + 1)
                        if s >= 2:
                            pe.wait_ge(hT_ready, s - 1)
                        for c in range(4):
                            m = pe.transpose(banks[4 + s % 2][:, c * P:(c + 1) * P], h[s % 2][:, c * P:(c + 1) * P], ident)
                        m.then_inc(turned, 1)

                    def down(s):
                        t, q = steps[s]
                        pe.wait_ge(hT_ready, s + 1)
                        if s == 0:
                            pe.wait_ge(comb_ready, 1)
                        if q == 0 and t >= 2:
                            pe.wait_ge(taken, t - 1)
                        for c in range(4):
                            m = pe.matmul(banks[6 + t % 2][:, 0:D], hT[s % 2][:, c * P:(c + 1) * P],
                                          k_f3["w2"][:, (4 * q + c) * D:(4 * q + c + 1) * D],
                                          start=(q == 0 and c == 0), stop=(q == 3 and c == 3))
                        m.then_inc(down_done, 1)

                    n = len(steps)
                    for s in range(n + 2):
                        if s < n:
                            up(s)
                        if 0 <= s - 2 < n:
                            down(s - 2)
                        if 0 <= s - 1 < n:
                            turn(s - 1)

                @block.scalar
                def _(act):
                    act.wait_ge(routed, 1)
                    act.activation(probs, banks[6][:, 0:32].rearrange("p (t e) -> p t e", t=TILES), ACT.Tanh,
                                   scale=0.5).then_inc(tanh_done, 1)
                    n = len(steps)
                    for s in range(n + 1):
                        if s < n:
                            act.wait_ge(up_done, s + 1)
                            if s >= 2:
                                act.wait_ge(h_ready, s - 1)
                            act.activation(g[s % 2], banks[s % 2][:, :], ACT.Gelu).then_inc(g_ready, 1)
                        if s >= 1:
                            act.wait_ge(turned, s)
                            if s >= 3:
                                act.wait_ge(down_done, s - 2)
                            act.copy(hT[(s - 1) % 2], banks[4 + (s - 1) % 2][:, :]).then_inc(hT_ready, 1)

                @block.vector
                def _(dve):
                    link = Chain(dve, link_sem)
                    dve.wait_ge(tanh_done, 1)
                    link(dve.tensor_scalar(probs, probs, 0.5, 0.5, ALU.mult, ALU.add))
                    best, place = top_two(dve, link, probs, 8, 160)
                    link(dve.memset(top, 1.0))
                    spread(dve, link, chosen, tmp, place, top[:, :, 0:1], top[:, :, 1:2], 8)
                    link(dve.tensor_copy(ran[:, 0, :], run_mask[:, :]))
                    for t in range(TILES):
                        link(dve.tensor_tensor(ran[:, t + 1, :], ran[:, t, :], chosen[:, t, :], ALU.add))
                    dve.sem_inc(chosen_ready, 1)
                    link(dve.tensor_copy(run_mask[:, :], ran[:, TILES, :]))
                    link(dve.tensor_tensor(tot, best[:, :, 0:1], best[:, :, 1:2], ALU.add))
                    link(dve.tensor_scalar(tot, tot, 1e-6, None, ALU.add))
                    link(dve.reciprocal(tot, tot))
                    link(dve.tensor_tensor(wts, best[:, :, 0:2], tot.to_broadcast([P, TILES, 2]), ALU.mult))
                    spread(dve, link, comb, tmp, place, wts[:, :, 0:1], wts[:, :, 1:2], 8)
                    dve.wait_ge(ranked, 1)
                    link(dve.tensor_scalar(tmp, banks[7][:, 0:32].rearrange("p (t e) -> p t e", t=TILES), capacity, None,
                                           ALU.is_lt))
                    link(dve.tensor_tensor(comb, comb, tmp, ALU.mult))
                    dve.sem_inc(comb_ready, 1)
                    n = len(steps)
                    for s in range(n + 2):
                        if s < n:
                            t, q = steps[s]
                            dve.wait_ge(g_ready, s + 1)
                            if s >= 2:
                                dve.wait_ge(turned, s - 1)
                            for j in range(2):
                                ins = dve.tensor_scalar(h[s % 2][:, 256 * j:256 * j + 256], g[s % 2][:, 256 * j:256 * j + 256],
                                                        comb[:, t, 2 * q + j:2 * q + j + 1], None, ALU.mult)
                            ins.then_inc(h_ready, 1)
                        if s >= 2 and steps[s - 2][1] == 3:
                            t = steps[s - 2][0]
                            dve.wait_ge(down_done, s - 1)
                            dve.tensor_tensor(src[:, t, :], banks[6 + t % 2][:, 0:D], src[:, t, :],
                                              ALU.add).then_inc(taken, 1)
            stage("routed tanh chosen ranked comb link up g h turned hT down taken", body)

        with nc.Fori(0, BLOCKS) as i:
            load_block(i)
            layer_norm(x, xn)
            retention()
            layer_norm(x, xn, xnT[:, :])
            ffn0()
            layer_norm(x, xn, xnT[:, :])
            with_bias = add_gated(1)

            def finish1(dve, t, y):
                return with_bias(dve, t, y)

            def add_bias(bias):
                def body(block):
                    @block.gpsimd
                    def _(pool):
                        pool.tensor_tensor(x[:, :, :], x[:, :, :], bias.unsqueeze(1).to_broadcast([P, TILES, D]), ALU.add)
                with nc.Block() as block:
                    body(block)
            add_bias(bo1[:, :])
            attention(xnT[:, :], cT[:, :], k_x1, scaled[:, 0:1], k_x1["bk"], bv1[:, :], None, None, finish1)
            layer_norm(x, xn, xnT[:, :])
            ffn1()
            layer_norm(x, xn, xnT[:, :])
            attention(xnT[:, :], cT[:, :], k_x2, None, None, None, neg2, any2, add_gated(2))
            layer_norm(x, xn, xnT[:, :])
            ffn2()
            layer_norm(x, xn)
            layer_norm(xn, xn, cxT[:, :, 1, :], k_x3["llg"], k_x3["llb"], also=xnT[:, :])
            layer_norm(ctok, xn, cxT[:, :, 0, :], k_x3["lxg"], k_x3["lxb"])
            perceiver()
            layer_norm(x, xn, xnT[:, :])
            add_to_z = lambda dve, t, y: dve.tensor_tensor(xn[:, t, :], y, xn[:, t, :], ALU.add)

            def add_ob(block):
                @block.gpsimd
                def _(pool):
                    pool.tensor_tensor(xn[:, :, :], xn[:, :, :],
                                       k_a3["bo"].unsqueeze(1).to_broadcast([P, TILES, D]), ALU.add)
            with nc.Block() as block:
                add_ob(block)
            attention(xnT[:, :], xnT[:, :], k_a3, scaled[:, 1:2], k_a3["bk"], bv3[:, :], None, None, add_to_z)
            rms_norm(xn, k_f3["n1"], xn, xnT[:, :])
            ffn3(xn)
            rms_norm(xn, k_f3["n2"], gate=tg[:, 7:8])
            store_block(i)


def layouts(a):
    import numpy as np

    f = np.float32
    rows = lambda v: np.broadcast_to(np.asarray(v).reshape(1, -1), (P, np.asarray(v).size))
    col = lambda v: np.asarray(v).reshape(-1, 1)
    pack = lambda *xs: np.ascontiguousarray(np.concatenate([np.asarray(z).reshape(P, -1) for z in xs], axis=1))
    n = np.arange(P)
    gap = n[None, :] - n[:, None]
    same = (n[None, :] // SEQ) == (n[:, None] // SEQ)
    decay = np.where(same & (gap >= 0), 0.9 ** np.maximum(gap, 0), 0.0)
    pmask = (n[:, None] // SEQ) == (n[None, :] // HD % 2)
    out = {"consts": pack(np.eye(P, dtype=f), (n[:, None] // HD == np.arange(HEADS)).astype(f), pmask.astype(f),
                          (gap > 0).astype(f), rows(np.arange(HEADS, dtype=f)), decay.astype(f))}
    out["l0"] = pack(a["L0_ffn_gate_w"].T, a["L0_ffn_shared_gate_w"].T) if False else pack(
        np.concatenate([a["L0_ffn_gate_w"].T, a["L0_ffn_shared_gate_w"].T], axis=1),
        a["L0_ffn_w_gate_up"].reshape(4, 4, D, 2, 64).transpose(2, 0, 3, 1, 4),
        a["L0_ffn_shared_w_gate"].T, a["L0_ffn_shared_w_up"].T,
        a["L0_ffn_w_down"].reshape(8, P, D).transpose(1, 0, 2),
        np.concatenate([a["L0_ffn_shared_w_down"].T, np.zeros((32, D), f)]).reshape(3, P, D).transpose(1, 0, 2))
    out["x1"] = pack(*[a["L1_xattn_w" + c].T for c in "qkvo"], col(a["L1_xattn_bq"]), col(a["L1_xattn_bk"]),
                     rows(a["L1_xattn_bv"]), rows(a["L1_xattn_bo"]))
    chunked = lambda v: v.reshape(8, 4, P).transpose(2, 0, 1)
    out["f1"] = pack(a["L1_ffn_Wr"], rows(a["L1_ffn_br"]), chunked(a["L1_ffn_b1"]), chunked(a["L1_ffn_g1"]),
                     chunked(a["L1_ffn_be1"]), a["L1_ffn_W1"].transpose(1, 0, 2), rows(a["L1_ffn_g2"]))
    out["b2"] = np.ascontiguousarray(rows(a["L1_ffn_b2"]))
    out["f1b"] = np.ascontiguousarray(a["L1_ffn_be2"])
    out["f1d"] = np.ascontiguousarray(a["L1_ffn_W2"].reshape(8, 4, P, D).transpose(2, 1, 0, 3))
    out["gates"] = np.ascontiguousarray(rows(np.concatenate([a["g_xattn"], a["g_ffn"]])))
    out["x2"] = pack(*[a["L2_xattn_W_" + c].T for c in "QKVO"])
    out["f2"] = pack(a["L2_ffn_Wg"].T, rows(a["L2_ffn_bg"]), a["L2_ffn_Wi"].T,
                     a["L2_ffn_Wo"].T.reshape(4, P, D).transpose(1, 0, 2))
    out["lora_a"] = np.ascontiguousarray(a["L2_ffn_A"].transpose(1, 0, 2))
    out["lora_b"] = np.ascontiguousarray(a["L2_ffn_B"].transpose(2, 0, 1))
    twice = lambda v: col(np.concatenate([v, v]))
    out["x3"] = pack(col(a["L3_xattn_ln_x_g"]), col(a["L3_xattn_ln_x_b"]), col(a["L3_xattn_ln_l_g"]),
                     col(a["L3_xattn_ln_l_b"]), twice(a["L3_xattn_qn_g"]), twice(a["L3_xattn_kn_g"]),
                     rows(a["L3_xattn_bout"]), a["L3_xattn_Wq"], a["L3_xattn_Wkv"],
                     a["L3_xattn_Wout"].reshape(8, P, D).transpose(1, 0, 2))
    rep = lambda w: np.repeat(w.reshape(-1, 4, HD), 4, axis=1).reshape(-1, D)
    out["a3"] = pack(a["L3_ffn_qw"], rep(a["L3_ffn_kw"]), rep(a["L3_ffn_vw"]), a["L3_ffn_ow"],
                     col(a["L3_ffn_qb"]), col(rep(a["L3_ffn_kb"])), rows(rep(a["L3_ffn_vb"])), rows(a["L3_ffn_ob"]))
    out["f3"] = pack(a["L3_ffn_gate_w"], rows(a["L3_ffn_norm1_w"]), rows(a["L3_ffn_norm2_w"]),
                     a["L3_ffn_w1"].transpose(1, 0, 2), a["L3_ffn_w2"].reshape(8, 2, P, D).transpose(2, 0, 1, 3))
    out["x"] = np.ascontiguousarray(a["x"]).reshape(BATCH * SEQ, D)
    out["ctx"] = np.ascontiguousarray(a["ctx_1024"]).reshape(BATCH * SEQ, D)
    out["mask2"] = np.ascontiguousarray(a["mask_BxSxS2_bf0"]).reshape(BATCH * SEQ, SEQ).view(np.int32)
    out["mask3"] = np.ascontiguousarray(a["mask_BxS2_bf1"]).view(np.int32)
    return out


def kernel(**inputs):
    import numpy as _np
    import concourse.bacc as _bacc
    from concourse import mybir as _mybir
    from concourse.bass_utils import run_bass_kernel_spmd as _run

    nc = _bacc.Bacc("TRN2", target_bir_lowering=False, num_devices=1)
    arrays, args = {}, {}
    for name, a in layouts({k: _np.asarray(v) for k, v in inputs.items()}).items():
        arrays[f"in_{name}_dram"] = a
        args[name] = nc.dram_tensor(f"in_{name}_dram", a.shape, _mybir.dt.from_np(a.dtype), kind="ExternalInput").ap()
    out = nc.dram_tensor("out_0_dram", (BATCH * SEQ, D), _mybir.dt.float32, kind="ExternalOutput").ap()
    build(nc, args, out)
    r = _run(nc, [arrays], core_ids=[0])
    return r.results[0]["out_0_dram"].reshape(BATCH, SEQ, D)
```

```python
from contextlib import ExitStack

import concourse.bass as bass
from concourse import mybir

F32 = mybir.dt.float32
I32 = mybir.dt.int32
U32 = mybir.dt.uint32
U8 = mybir.dt.uint8
ALU = mybir.AluOpType
ACT = mybir.ActivationFunctionType
AX = mybir.AxisListType.X

P = 128
BATCH, SEQ, D = 32, 64, 128
TILES = 4
TOK = TILES * P
PAIR = P // SEQ
BLOCKS = BATCH * SEQ // TOK
HEADS, HD = 16, 8
HP = HEADS // 2
XD = 64
LN_EPS, RMS_EPS = 1e-5, 1e-6
NEG = -1e30

CONST = dict(ident=P, hmask=HEADS, pmask=P, tri=P, iota=HEADS, decay=P)
L0 = dict(router=17, gu=4 * 512, sgu=704, down=11 * D)
XA = dict(wq=D, wk=D, wv=D, wo=D)
XB = dict(bq=1, bk=1, bv=D, bo=D)
L1F = dict(wr=8, br=8, b1=32, g1=32, be1=32, w1=8 * 512, g2=8 * D)
L2F = dict(wg=4, bg=4, wi=512, wo=4 * D)
L3X = dict(lxg=1, lxb=1, llg=1, llb=1, qn=1, kn=1, bout=D, wq=1024, wkv=2048, wout=8 * D)
L3F = dict(wr=8, n1=D, n2=D, w1=8 * 256, w2=16 * D)


def width(pieces):
    return sum(pieces.values())


def pieces_of(tensor, pieces):
    at, out = 0, {}
    for name, n in pieces.items():
        out[name] = tensor[:, at:at + n]
        at += n
    return out


class Chain:

    def __init__(self, engine, sem):
        self.engine, self.sem, self.n = engine, sem, 0

    def __call__(self, ins):
        self.n += 1
        ins.then_inc(self.sem, 1)
        self.engine.wait_ge(self.sem, self.n)

    def last_of(self, instructions):
        for ins in instructions:
            self.n += 1
            ins.then_inc(self.sem, 1)
        self.engine.wait_ge(self.sem, self.n)


def rsqrt(dve, link, y, v, tmp):
    vb, yb = v.bitcast(I32), y.bitcast(I32)
    link(dve.tensor_scalar(yb, vb, 1, None, ALU.logical_shift_right))
    link(dve.tensor_scalar(yb, yb, -1.0, 1597463007.0, ALU.mult, ALU.add))
    for _ in range(3):
        link(dve.tensor_tensor(tmp, y, y, ALU.mult))
        link(dve.scalar_tensor_tensor(tmp, tmp, -0.5, v, ALU.mult, ALU.mult))
        link(dve.scalar_tensor_tensor(y, tmp, 1.5, y, ALU.add, ALU.mult))


def build(nc, args, out):
    ctx = ExitStack()
    with ctx:
        def sb(name, shape, dt=F32):
            return ctx.enter_context(nc.sbuf_tensor(name, shape, dt))

        consts = sb("consts", [P, width(CONST)])
        ones = sb("ones", [P, P])
        w_l0 = sb("w_l0", [P, width(L0)])
        w_x1 = sb("w_x1", [P, width(XA) + width(XB)])
        w_f1 = sb("w_f1", [P, width(L1F)])
        w_f1b = sb("w_f1b", [8, D])
        w_f1d = sb("w_f1d", [P, 4, 8, D + 1])
        w_x2 = sb("w_x2", [P, width(XA)])
        w_f2 = sb("w_f2", [P, width(L2F)])
        w_f2e = sb("w_f2e", [P, 4, 512])
        w_x3 = sb("w_x3", [P, width(L3X)])
        w_a3 = sb("w_a3", [P, width(XA) + width(XB)])
        w_f3 = sb("w_f3", [P, width(L3F)])
        gates = sb("gates", [P, 8])
        tg = sb("tg", [P, 8])
        expert_bias = sb("expert_bias", [P, 8, D])
        scaled = sb("scaled", [P, 8])
        bo1 = sb("bo1", [P, D])
        bout3 = sb("bout3", [P, D])
        bv1 = sb("bv1", [P, D])
        bv3 = sb("bv3", [P, D])
        run_mask = sb("run_mask", [P, 8])
        v_blocks = sb("v_blocks", [P, TILES, HP, PAIR, 18])
        q_blocks = sb("q_blocks", [P, PAIR, 8, 2, XD])
        h_shared = sb("h_shared", [P, 2, 384])
        x = sb("x", [P, TILES, D])
        ctok = sb("ctok", [P, TILES, D])
        cT = sb("cT", [P, TOK])
        xn = sb("xn", [P, TILES, D])
        xnT = sb("xnT", [P, TOK])
        cxT = sb("cxT", [P, TILES * PAIR, 2, SEQ])
        mask2_words = sb("mask2", [P, TILES, SEQ // 4], I32)
        mask2 = mask2_words[:, :, :].bitcast(U8)
        mask3_words = sb("mask3", [P, TILES * PAIR, SEQ // 4], I32)
        mask3 = mask3_words[:, :, :].bitcast(U8)
        neg2 = sb("neg2", [P, TILES, SEQ])
        any2 = sb("any2", [P, TILES])
        neg3 = sb("neg3", [P, TILES * PAIR, 2, SEQ])
        small = sb("small", [P, 1024])
        work = sb("work", [P, 13312])
        lora_a = work[0:4, 0:4 * D].rearrange("p (e d) -> p e d", e=4)
        lora_b = work[0:4, 1024:1024 + 2048].rearrange("p (e f) -> p e f", e=4)
        b2 = work[:, 4096:4096 + 8 * D]

        banks = [ctx.enter_context(nc.psum_tensor(f"bank{i}", [P, 512], F32)) for i in range(8)]

        k_const = pieces_of(consts, CONST)
        k_l0 = pieces_of(w_l0, L0)
        k_x1 = pieces_of(w_x1, {**XA, **XB})
        k_f1 = pieces_of(w_f1, L1F)
        k_x2 = pieces_of(w_x2, XA)
        k_f2 = pieces_of(w_f2, L2F)
        k_x3 = pieces_of(w_x3, L3X)
        k_a3 = pieces_of(w_a3, {**XA, **XB})
        k_f3 = pieces_of(w_f3, L3F)
        ident = k_const["ident"]
        eps_cache = {}

        def stage(names, body):
            with ExitStack() as inner:
                stage.n += 1
                sems = [inner.enter_context(nc.semaphore(f"{n}_{stage.n}")) for n in names.split()]
                with nc.Block() as block:
                    body(block, *sems)
                nums = sorted(s.num for s in sems)
                starts = [n for n in nums if n - 1 not in nums]
                for a in starts:
                    b = a
                    while b in nums:
                        b += 1
                    nc.vector.sem_clear(range(a, b))
                nc.all_engine_barrier()
        stage.n = 0

        def load_all(block, loaded):
            @block.sync
            def _(sp):
                for name, dst in (("f1", w_f1[:, :]), ("consts", consts[:, :]), ("f1b", w_f1b[:, :]),
                                  ("gates", gates[:, :]), ("x1", w_x1[:, :]), ("lora_a", lora_a), ("lora_b", lora_b), ("b2", b2),
                                  ("f2", w_f2[:, :]), ("l0", w_l0[:, :]), ("x2", w_x2[:, :]),
                                  ("x3", w_x3[:, :]), ("a3", w_a3[:, :]), ("f3", w_f3[:, :])):
                    sp.dma_start(dst, args[name]).then_inc(loaded, 16)
                for c in range(4):
                    sp.dma_start(w_f1d[:, c, :, 0:D], args["f1d"][:, c, :, :]).then_inc(loaded, 16)
                sp.wait_ge(loaded, 16 * 18)

            @block.vector
            def _(dve):
                dve.memset(ones[:, :], 1.0)
                dve.memset(run_mask[:, :], 0.0)
                dve.memset(w_f1d[:, :, :, D:D + 1], 1.0)
                dve.memset(q_blocks[:, :, :, :, :], 0.0)
                dve.memset(h_shared[:, :, :], 0.0)
                dve.memset(v_blocks[:, :, :, :, :], 0.0)
                dve.memset(neg3[:, :, :, :], 0.0)
        stage("loaded", load_all)

        def prepare(block, link_sem, means, evacuated, tanh_done, ones_set):
            w2_raw = w_f1d[:, :, :, 0:D]

            @block.tensor
            def _(pe):
                for e in range(8):
                    for c in range(4):
                        m = pe.matmul(banks[e // 4][:, (e % 4) * D:(e % 4 + 1) * D],
                                      k_f1["be1"][:, e * 4 + c:e * 4 + c + 1].to_broadcast([P, P]),
                                      w_f1d[:, c, e, 0:D], start=(c == 0), stop=(c == 3))
                m.then_inc(means, 1)
                pe.wait_ge(evacuated, 1)
                for half in range(2):
                    for c in range(4):
                        m = pe.matmul(banks[2 + half][:, :], ones[:, :], w_f1d[:, c, 4 * half:4 * half + 4, 0:D],
                                      start=(c == 0), stop=(c == 3))
                m.then_inc(means, 1)
                for e in range(4):
                    m = pe.matmul(banks[4 + e][:, :], lora_a[:, e, :], lora_b[:, e, :], start=True, stop=True)
                m.then_inc(means, 1)

            @block.scalar
            def _(act):
                act.activation(tg[:, :], gates[:, :], ACT.Tanh).then_inc(tanh_done, 1)

            @block.vector
            def _(dve):
                link = Chain(dve, link_sem)
                dve.wait_ge(means, 1)
                for half in range(2):
                    dve.tensor_tensor(expert_bias[:, 4 * half:4 * half + 4, :],
                                      banks[half][:, :].rearrange("p (e d) -> p e d", d=D),
                                      b2[:, 512 * half:512 * half + 512].rearrange("p (e d) -> p e d", d=D),
                                      ALU.add)
                for c in range(4):
                    g1 = k_f1["g1"][:, c:32:4]
                    m = dve.tensor_tensor(w_f1d[:, c, :, 0:D], w_f1d[:, c, :, 0:D],
                                          g1.unsqueeze(2).to_broadcast([P, 8, D]), ALU.mult)
                m.then_inc(evacuated, 1)
                dve.wait_ge(means, 2)
                for half in range(2):
                    for c in range(4):
                        w = w_f1d[:, c, 4 * half:4 * half + 4, 0:D]
                        dve.scalar_tensor_tensor(w, banks[2 + half][:, :].rearrange("p (e d) -> p e d", d=D),
                                                 -1.0 / 512, w, ALU.mult, ALU.add)
                dve.wait_ge(means, 3)
                for e in range(4):
                    dve.tensor_tensor(w_f2e[:, e, :], banks[4 + e][:, :], k_f2["wi"], ALU.add)
                dve.wait_ge(tanh_done, 1)
                dve.tensor_scalar(bo1[:, :], k_x1["bo"], tg[:, 1:2], None, ALU.mult)
                dve.tensor_scalar(bout3[:, :], k_x3["bout"], tg[:, 3:4], None, ALU.mult)
                dve.tensor_tensor(bv1[:, :], k_x1["bv"], k_const["pmask"], ALU.mult)
                dve.tensor_tensor(bv3[:, :], k_a3["bv"], k_const["pmask"], ALU.mult)
                dve.tensor_scalar(scaled[:, 0:1], k_x1["bq"], HD ** -0.5, None, ALU.mult)
                dve.tensor_scalar(scaled[:, 1:2], k_a3["bq"], HD ** -0.5, None, ALU.mult)
                dve.scalar_tensor_tensor(scaled[:, 2:3], k_x3["qn"], XD ** -0.5, k_x3["kn"], ALU.mult, ALU.mult)
                for h2 in range(2):
                    m = dve.memset(v_blocks[64 * h2:64 * h2 + 64, :, :, :, 16 + h2:17 + h2], 1.0)
        stage("link means evacuated tanh ones_set", prepare)

        def layer_norm(src, dst, dstT=None, gain=None, bias=None, also=None):
            def body(block, link_sem, normed, turned):
                stats = small[:, 0:24].rearrange("p (t s) -> p t s", t=TILES)
                mv = small[:, 24:32].rearrange("p (t s) -> p t s", t=TILES)
                ve, rs, tmp = small[:, 32:36], small[:, 36:40], small[:, 40:44]

                @block.vector
                def _(dve):
                    link = Chain(dve, link_sem)
                    link.last_of([dve.bn_stats(stats[:, t, :], src[:, t, :]) for t in range(TILES)])
                    link.last_of([dve.bn_aggr(mv[:, t, :], stats[:, t, :]) for t in range(TILES)])
                    link(dve.tensor_scalar(ve, mv[:, :, 1], LN_EPS, None, ALU.add))
                    rsqrt(dve, link, rs, ve, tmp)
                    for t in range(TILES):
                        dve.tensor_scalar(dst[:, t, :], src[:, t, :], mv[:, t, 0:1], rs[:, t:t + 1],
                                          ALU.subtract, ALU.mult).then_inc(normed, 1)

                if dstT is None:
                    return

                @block.tensor
                def _(pe):
                    for t in range(TILES):
                        pe.wait_ge(normed, t + 1)
                        m = pe.transpose(banks[0][:, t * P:(t + 1) * P], dst[:, t, :], ident)
                    m.then_inc(turned, 1)

                @block.scalar
                def _(act):
                    act.wait_ge(turned, 1)
                    if gain is None:
                        act.copy(dstT, banks[0][:, :])
                    else:
                        bank = banks[0][:, :].rearrange("p (b s) -> p b s", s=SEQ)
                        act.activation(dstT, bank, ACT.Identity, bias=bias, scale=gain)
                        if also is not None:
                            act.activation(also, banks[0][:, :], ACT.Identity, bias=bias, scale=gain)
            stage("link normed turned", body)

        def top_two(dve, link, scores, n, at):
            best = small[:, at:at + 32].rearrange("p (t s) -> p t s", t=TILES)
            where = small[:, at + 32:at + 64].bitcast(U32).rearrange("p (t s) -> p t s", t=TILES)
            place = small[:, at + 64:at + 72].rearrange("p (t s) -> p t s", t=TILES)
            link.last_of([dve.max(best[:, t, :], scores[:, t, :]) for t in range(TILES)])
            link.last_of([dve.max_index(where[:, t, :], best[:, t, :], scores[:, t, :]) for t in range(TILES)])
            link(dve.tensor_copy(place, where[:, :, 0:2]))
            return best, place

        def spread(dve, link, dst, tmp, place, first, second, n):
            iota = k_const["iota"][:, 0:n].unsqueeze(1).to_broadcast([P, TILES, n])

            def wide(a):
                return a.to_broadcast([P, TILES, n])
            link.last_of([dve.tensor_tensor(dst, iota, wide(place[:, :, 0:1]), ALU.is_equal),
                          dve.tensor_tensor(tmp, iota, wide(place[:, :, 1:2]), ALU.is_equal)])
            link.last_of([dve.tensor_tensor(dst, dst, wide(first), ALU.mult),
                          dve.tensor_tensor(tmp, tmp, wide(second), ALU.mult)])
            link(dve.tensor_tensor(dst, dst, tmp, ALU.add))

        def attention(src_q, src_kv, w, scale_bias, k_bias, v_bias, neg, anyrow, finish):
            qT = work[:, 0:512]
            kT = work[:, 512:1024]
            kx = work[:, 1024:9216].rearrange("p (b h k) -> p b h k", b=TILES * PAIR, h=HEADS)
            s_sb = [work[:, 9216 + 1024 * i:10240 + 1024 * i] for i in range(2)]
            p_sb = s_sb
            pT = [work[:, 11264:12288], work[:, 12288:13312]]
            mx = small[:, 0:64].rearrange("p (t h) -> p t h", t=TILES)
            rc = small[:, 64:128].rearrange("p (t h) -> p t h", t=TILES)
            o_sb = [small[:, 128 + D * i:128 + D * (i + 1)] for i in range(2)]
            oT = [small[:, 384 + D * i:384 + D * (i + 1)] for i in range(2)]
            k_const_h = k_const["hmask"]

            def body(block, projected, q_ready, k_ready, v_ready, kx_pool, kx_dve, scored, link_sem,
                     s_ready, p_ready, turned, pT_ready, mixed, o_ready, o_turned, oT_ready, done, taken):
                def heads(a):
                    return a.rearrange("p (h k) -> p h k", k=SEQ)

                @block.tensor
                def _(pe):
                    pe.matmul(banks[4][:, :], w["wq"], src_q, start=True, stop=True).then_inc(projected, 1)
                    pe.matmul(banks[5][:, :], w["wk"], src_kv, start=True, stop=True).then_inc(projected, 1)
                    for b in range(TILES * PAIR):
                        for h2 in range(2):
                            m = pe.matmul(banks[6 + b // 4][64 * h2:64 * h2 + 64, (b % 4) * P:(b % 4 + 1) * P],
                                          src_kv[:, b * SEQ:(b + 1) * SEQ], w["wv"], start=True, stop=True)
                    m.then_inc(projected, 1)

                    def scores(t):
                        if t == 0:
                            pe.wait_ge(q_ready, 1)
                        pe.wait_ge(kx_dve, t + 1)
                        pe.wait_ge(kx_pool, t + 1)
                        if t >= 2:
                            pe.wait_ge(s_ready, t - 1)
                        for b in range(PAIR):
                            for half in range(2):
                                m = pe.matmul(banks[2 * (t % 2) + half][64 * b:64 * b + 64, :],
                                              qT[:, (2 * t + b) * SEQ:(2 * t + b + 1) * SEQ],
                                              kx[:, 2 * t + b, 8 * half:8 * half + 8, :], start=True, stop=True)
                        m.then_inc(scored, 1)

                    def turn(t):
                        pe.wait_ge(p_ready, t + 1)
                        if t == 0:
                            pe.wait_ge(k_ready, 1)
                            pe.wait_ge(q_ready, 1)
                        else:
                            pe.wait_ge(pT_ready, 2 * t)
                        for c in range(8):
                            m = pe.transpose(banks[4 + c // 4][:, (c % 4) * P:(c % 4 + 1) * P],
                                             p_sb[t % 2][:, c * P:(c + 1) * P], ident)
                        m.then_inc(turned, 1)

                    def mix(t):
                        pe.wait_ge(pT_ready, 2 * t + 2)
                        if t == 0:
                            pe.wait_ge(v_ready, 1)
                        else:
                            pe.wait_ge(o_ready, 2 * t)
                        for c in range(8):
                            m = pe.matmul(banks[6][:, c * 36:(c + 1) * 36], pT[t % 2][:, c * P:(c + 1) * P],
                                          v_blocks[:, t, c, :, :], start=True, stop=True)
                        m.then_inc(mixed, 1)

                    def project(t):
                        pe.wait_ge(o_ready, 2 * t + 2)
                        if t >= 1:
                            pe.wait_ge(taken, t)
                        pe.transpose(banks[7][:, 0:P], o_sb[t % 2], ident).then_inc(o_turned, 1)
                        pe.wait_ge(oT_ready, t + 1)
                        pe.matmul(banks[7][:, P:P + D], oT[t % 2], w["wo"], start=True, stop=True).then_inc(done, 1)

                    for step in range(TILES + 3):
                        if step < TILES:
                            scores(step)
                        if 0 <= step - 1 < TILES:
                            turn(step - 1)
                        if 0 <= step - 3 < TILES:
                            project(step - 3)
                        if 0 <= step - 2 < TILES:
                            mix(step - 2)

                @block.scalar
                def _(act):
                    act.wait_ge(projected, 1)
                    act.activation(qT, banks[4][:, :], ACT.Identity, scale=HD ** -0.5,
                                   bias=0.0 if scale_bias is None else scale_bias).then_inc(q_ready, 1)
                    act.wait_ge(projected, 2)
                    act.activation(kT, banks[5][:, :], ACT.Identity,
                                   bias=0.0 if k_bias is None else k_bias).then_inc(k_ready, 1)

                    def exps(t):
                        act.wait_ge(s_ready, t + 1)
                        act.activation(p_sb[t % 2], s_sb[t % 2], ACT.Exp).then_inc(p_ready, 1)

                    def take_pT(t):
                        act.wait_ge(turned, t + 1)
                        if t >= 2:
                            act.wait_ge(mixed, t - 1)
                        for half in range(2):
                            act.copy(pT[t % 2][:, 512 * half:512 * half + 512],
                                     banks[4 + half][:, :]).then_inc(pT_ready, 1)

                    def take_oT(t):
                        act.wait_ge(o_turned, t + 1)
                        act.copy(oT[t % 2], banks[7][:, 0:P]).then_inc(oT_ready, 1)

                    for step in range(TILES + 3):
                        if step < TILES:
                            exps(step)
                        if 0 <= step - 3 < TILES:
                            take_oT(step - 3)
                        if 0 <= step - 1 < TILES:
                            take_pT(step - 1)

                def key_blocks(engine, b, done_sem):
                    engine.tensor_tensor(kx[:, b, :, :],
                                         kT[:, b * SEQ:(b + 1) * SEQ].unsqueeze(1).to_broadcast([P, HEADS, SEQ]),
                                         k_const_h.unsqueeze(2).to_broadcast([P, HEADS, SEQ]),
                                         ALU.mult).then_inc(done_sem, 1)

                @block.gpsimd
                def _(pool):
                    pool.wait_ge(k_ready, 1)
                    for t in range(TILES):
                        key_blocks(pool, 2 * t + 1, kx_pool)

                @block.vector
                def _(dve):
                    link = Chain(dve, link_sem)
                    dve.wait_ge(k_ready, 1)
                    key_blocks(dve, 0, kx_dve)
                    key_blocks(dve, 2, kx_dve)
                    dve.wait_ge(projected, 3)
                    pm = k_const["pmask"].rearrange("p (c d) -> p c d", c=HP)
                    for t in range(TILES):
                        vv = banks[6 + t // 2][:, (t % 2) * 256:(t % 2) * 256 + 256]
                        for b in range(PAIR):
                            ins = dve.tensor_tensor(v_blocks[:, t, :, b, 0:16],
                                                    vv[:, b * P:(b + 1) * P].rearrange("p (c d) -> p c d", c=HP),
                                                    pm, ALU.mult)
                            if v_bias is not None:
                                link(ins)
                                ins = dve.tensor_tensor(v_blocks[:, t, :, b, 0:16], v_blocks[:, t, :, b, 0:16],
                                                        v_bias.rearrange("p (c d) -> p c d", c=HP), ALU.add)
                    ins.then_inc(v_ready, 1)

                    def shift(t):
                        dve.wait_ge(scored, t + 1)
                        if t >= 2:
                            dve.wait_ge(turned, t - 1)
                        for half in range(2):
                            s = heads(banks[2 * (t % 2) + half][:, :])
                            d = heads(s_sb[t % 2][:, 512 * half:512 * half + 512])
                            hs = slice(8 * half, 8 * half + 8)
                            if neg is not None:
                                link(dve.tensor_tensor(d, s, neg[:, t, :].unsqueeze(1).to_broadcast([P, 8, SEQ]),
                                                       ALU.add))
                                s = d
                            link(dve.tensor_reduce(mx[:, t, hs], s, AX, ALU.max))
                            ins = dve.tensor_tensor(d, s, mx[:, t, hs].unsqueeze(2).to_broadcast([P, 8, SEQ]),
                                                    ALU.subtract)
                            if half == 0:
                                link(ins)
                        ins.then_inc(s_ready, 1)

                    def normalise(t):
                        dve.wait_ge(mixed, t + 1)
                        o = banks[6][:, 0:288].rearrange("p (c b d) -> p c b d", c=HP, b=PAIR)
                        rv = rc[:, t, :].rearrange("p (c h) -> p c h", c=HP)
                        link.last_of([dve.reciprocal(rv[64 * b:64 * b + 64], o[64 * b:64 * b + 64, :, b, 16:18])
                                      for b in range(PAIR)])
                        if anyrow is not None:
                            link(dve.tensor_scalar(rc[:, t, :], rc[:, t, :], anyrow[:, t:t + 1], None, ALU.mult))
                        for b in range(PAIR):
                            r = slice(64 * b, 64 * b + 64)
                            dve.tensor_tensor(o_sb[t % 2][r].rearrange("p (c h d) -> p c h d", c=HP, h=2),
                                              o[r, :, b, 0:16].rearrange("p c (h d) -> p c h d", h=2),
                                              rv[r].unsqueeze(3).to_broadcast([SEQ, HP, 2, HD]),
                                              ALU.mult).then_inc(o_ready, 1)

                    for step in range(TILES + 3):
                        if step < TILES:
                            shift(step)
                        if 0 <= step - 3 < TILES:
                            dve.wait_ge(done, step - 2)
                            finish(dve, step - 3, banks[7][:, P:P + D]).then_inc(taken, 1)
                        if 0 <= step - 2 < TILES:
                            normalise(step - 2)
                        if step == 0:
                            for t in range(2, TILES):
                                key_blocks(dve, 2 * t, kx_dve)
            stage("projected q_ready k_ready v_ready kx_pool kx_dve scored link s_ready p_ready turned pT_ready "
                  "mixed o_ready o_turned oT_ready done taken", body)

        def add_gated(gate):
            return lambda dve, t, y: dve.scalar_tensor_tensor(x[:, t, :], y, tg[:, gate:gate + 1], x[:, t, :],
                                                              ALU.mult, ALU.add)

        def load_block(i):
            def body(block, loaded, turned, link_sem):
                xs = args["x"].rearrange("(i t p) d -> i p t d", t=TILES, p=P)
                cs = args["ctx"].rearrange("(i t p) d -> i p t d", t=TILES, p=P)
                m2 = args["mask2"].rearrange("(i t p) k -> i p t k", t=TILES, p=P)
                m3 = args["mask3"].rearrange("(i b) k -> i b k", b=TILES * PAIR)

                @block.sync
                def _(sp):
                    sp.dma_start(x[:, :, :], xs[bass.ds(i, 1)].rearrange("a p t d -> (a p) t d")).then_inc(loaded, 16)
                    sp.dma_start(ctok[:, :, :], cs[bass.ds(i, 1)].rearrange("a p t d -> (a p) t d")).then_inc(loaded, 16)
                    sp.dma_start(mask2_words[:, :, :], m2[bass.ds(i, 1)].rearrange("a p t k -> (a p) t k")).then_inc(loaded, 16)
                    sp.dma_start(mask3_words[:, :, :], m3[bass.ds(i, 1)].to_broadcast([P, TILES * PAIR, SEQ // 4])).then_inc(loaded, 16)
                    sp.wait_ge(loaded, 64)

                @block.tensor
                def _(pe):
                    pe.wait_ge(loaded, 64)
                    for t in range(TILES):
                        m = pe.transpose(banks[0][:, t * P:(t + 1) * P], ctok[:, t, :], ident)
                    m.then_inc(turned, 1)

                @block.scalar
                def _(act):
                    act.wait_ge(turned, 1)
                    act.copy(cT[:, :], banks[0][:, :])

                @block.vector
                def _(dve):
                    link = Chain(dve, link_sem)
                    dve.wait_ge(loaded, 64)
                    link(dve.tensor_scalar(neg2[:, :, :], mask2[:, :, :], NEG, None, ALU.mult))
                    link(dve.tensor_reduce(any2[:, :], neg2[:, :, :], AX, ALU.max))
                    dve.tensor_scalar(any2[:, :], any2[:, :], 0.5 * NEG, None, ALU.is_gt)
                    dve.tensor_scalar(neg3[:, :, 0, :], mask3[:, :, :], -NEG, NEG, ALU.mult, ALU.add)
            stage("loaded turned link", body)

        def store_block(i):
            def body(block, stored):
                os_ = out.rearrange("(i t p) d -> i p t d", t=TILES, p=P)

                @block.sync
                def _(sp):
                    sp.dma_start(os_[bass.ds(i, 1)].rearrange("a p t d -> (a p) t d"), x[:, :, :]).then_inc(stored, 16)
                    sp.wait_ge(stored, 16)
            stage("stored", body)

        def retention():
            kv = work[:, 0:512].rearrange("p (t d) -> p t d", t=TILES)
            part = work[:, 512:1024].rearrange("p (t d) -> p t d", t=TILES)

            def body(block, squared, summed, link_sem):
                @block.gpsimd
                def _(pool):
                    pool.tensor_tensor(kv, ctok[:, :, :], ctok[:, :, :], ALU.mult).then_inc(squared, 1)

                @block.tensor
                def _(pe):
                    pe.wait_ge(squared, 1)
                    for t in range(TILES):
                        m = pe.matmul(banks[0][:, t * D:(t + 1) * D], k_const["decay"], kv[:, t, :],
                                      start=True, stop=True)
                    m.then_inc(summed, 1)

                @block.vector
                def _(dve):
                    link = Chain(dve, link_sem)
                    dve.wait_ge(summed, 1)
                    link(dve.scalar_tensor_tensor(part, banks[0][:, :].rearrange("p (t d) -> p t d", t=TILES),
                                                  tg[:, 0:1], xn[:, :, :], ALU.mult, ALU.mult))
                    dve.tensor_tensor(x[:, :, :], x[:, :, :], part, ALU.add)
            stage("squared summed link", body)

        def ffn0():
            logits = small[:, 0:68].rearrange("p (t e) -> p t e", t=TILES)
            lg = small[:, 72:136].rearrange("p (t e) -> p t e", t=TILES)
            halves = small[:, 136:144].rearrange("p (t s) -> p t s", t=TILES)
            sig = small[:, 144:152].rearrange("p (t s) -> p t s", t=TILES)
            rest = small[:, 152:156].rearrange("p (t s) -> p t s", t=TILES)
            comb = small[:, 256:320].rearrange("p (t e) -> p t e", t=TILES)
            tmp = small[:, 320:384].rearrange("p (t e) -> p t e", t=TILES)
            sil = [work[:, 512 * i:512 * i + 512] for i in range(2)]
            hid = [work[:, 1024 + 512 * i:1536 + 512 * i] for i in range(2)]
            hidT = [work[:, 2048 + 512 * i:2560 + 512 * i] for i in range(2)]
            steps = [(t, g) for t in range(TILES) for g in range(5)]

            def body(block, routed, halves_ready, sig_ready, comb_ready, link_sem, up_done, sil_ready, hid_ready,
                     turned, hidT_ready, down_done, taken):
                def h_of(s):
                    return h_shared[:, (s // 5) % 2, :] if steps[s][1] == 4 else hid[s % 2]

                @block.tensor
                def _(pe):
                    for t in range(TILES):
                        m = pe.matmul(banks[6][:, t * 17:(t + 1) * 17], xnT[:, t * P:(t + 1) * P], k_l0["router"],
                                      start=True, stop=True)
                    m.then_inc(routed, 1)

                    def up(s):
                        t, g = steps[s]
                        if s >= 2:
                            pe.wait_ge(hid_ready, s - 1)
                        a, b = banks[2 * (s % 2)], banks[2 * (s % 2) + 1]
                        xt = xnT[:, t * P:(t + 1) * P]
                        if g < 4:
                            m = pe.matmul(a[:, :], xt, k_l0["gu"][:, g * 512:(g + 1) * 512], start=True, stop=True)
                        else:
                            pe.matmul(a[:, 0:352], xt, k_l0["sgu"][:, 0:352], start=True, stop=True)
                            m = pe.matmul(b[:, 0:352], xt, k_l0["sgu"][:, 352:704], start=True, stop=True)
                        m.then_inc(up_done, 1)

                    def turn(s):
                        pe.wait_ge(hid_ready, s + 1)
                        if s >= 2:
                            pe.wait_ge(hidT_ready, s - 1)
                        for c in range(3 if steps[s][1] == 4 else 2):
                            m = pe.transpose(banks[4 + s % 2][:, c * P:(c + 1) * P], h_of(s)[:, c * P:(c + 1) * P],
                                             ident)
                        m.then_inc(turned, 1)

                    def down(s):
                        t, g = steps[s]
                        pe.wait_ge(hidT_ready, s + 1)
                        if g == 0 and t >= 2:
                            pe.wait_ge(taken, t - 1)
                        if s == 0:
                            pe.wait_ge(comb_ready, 1)
                        n = 3 if g == 4 else 2
                        for c in range(n):
                            m = pe.matmul(banks[6 + t % 2][:, 0:D], hidT[s % 2][:, c * P:(c + 1) * P],
                                          k_l0["down"][:, (2 * g + c) * D:(2 * g + c + 1) * D],
                                          start=(g == 0 and c == 0), stop=(g == 4 and c == 2))
                        m.then_inc(down_done, 1)

                    n = len(steps)
                    for s in range(n + 2):
                        if s < n:
                            up(s)
                        if 0 <= s - 2 < n:
                            down(s - 2)
                        if 0 <= s - 1 < n:
                            turn(s - 1)

                @block.scalar
                def _(act):
                    act.wait_ge(halves_ready, 1)
                    act.activation(sig, halves, ACT.Tanh).then_inc(sig_ready, 1)

                    def silu(s):
                        act.wait_ge(up_done, s + 1)
                        if s >= 2:
                            act.wait_ge(hid_ready, s - 1)
                        n = 352 if steps[s][1] == 4 else 256
                        act.activation(sil[s % 2][:, 0:n], banks[2 * (s % 2)][:, 0:n], ACT.Silu).then_inc(sil_ready, 1)

                    def take_T(s):
                        act.wait_ge(turned, s + 1)
                        if s >= 2:
                            act.wait_ge(down_done, s - 1)
                        n = 384 if steps[s][1] == 4 else 256
                        act.copy(hidT[s % 2][:, 0:n], banks[4 + s % 2][:, 0:n]).then_inc(hidT_ready, 1)

                    for s in range(len(steps) + 1):
                        if s < len(steps):
                            silu(s)
                        if s >= 1:
                            take_T(s - 1)

                @block.vector
                def _(dve):
                    link = Chain(dve, link_sem)
                    dve.wait_ge(routed, 1)
                    link(dve.tensor_copy(logits, banks[6][:, 0:68].rearrange("p (t e) -> p t e", t=TILES)))
                    link(dve.tensor_copy(lg, logits[:, :, 0:16]))
                    best, place = top_two(dve, link, lg, 16, 160)
                    link(dve.tensor_tensor(halves[:, :, 0:1], best[:, :, 0:1], best[:, :, 1:2], ALU.subtract))
                    link(dve.tensor_scalar(halves[:, :, 0:1], halves[:, :, 0:1], 0.5, None, ALU.mult))
                    dve.tensor_scalar(halves[:, :, 1:2], logits[:, :, 16:17], 0.5, None,
                                      ALU.mult).then_inc(halves_ready, 1)
                    dve.wait_ge(sig_ready, 1)
                    link(dve.tensor_scalar(sig, sig, 0.5, 0.5, ALU.mult, ALU.add))
                    link(dve.tensor_scalar(rest, sig[:, :, 0:1], -1.0, 1.0, ALU.mult, ALU.add))
                    spread(dve, link, comb, tmp, place, sig[:, :, 0:1], rest, 16)
                    dve.sem_inc(comb_ready, 1)

                    def gate_up(s):
                        t, g = steps[s]
                        dve.wait_ge(sil_ready, s + 1)
                        if s >= 2:
                            dve.wait_ge(turned, s - 1)
                        a, b = banks[2 * (s % 2)], banks[2 * (s % 2) + 1]
                        if g < 4:
                            q = sil[s % 2][:, 0:256].rearrange("p (e f) -> p e f", e=4)
                            c = comb[:, t, 4 * g:4 * g + 4].unsqueeze(2).to_broadcast([P, 4, 64])
                            link(dve.tensor_tensor(q, q, c, ALU.mult))
                            dve.tensor_tensor(h_of(s)[:, 0:256], a[:, 256:512], sil[s % 2][:, 0:256],
                                              ALU.mult).then_inc(hid_ready, 1)
                        else:
                            dve.scalar_tensor_tensor(h_of(s)[:, 0:352], b[:, 0:352], sig[:, t, 1:2],
                                                     sil[s % 2][:, 0:352], ALU.mult, ALU.mult).then_inc(hid_ready, 1)

                    n = len(steps)
                    for s in range(n + 2):
                        if s < n:
                            gate_up(s)
                        if s >= 2 and steps[s - 2][1] == 4:
                            t = steps[s - 2][0]
                            dve.wait_ge(down_done, s - 1)
                            dve.scalar_tensor_tensor(x[:, t, :], banks[6 + t % 2][:, 0:D], tg[:, 4:5], x[:, t, :],
                                                     ALU.mult, ALU.add).then_inc(taken, 1)
            stage("routed halves sig comb link up sil hid turned hidT down taken", body)

        def ffn1():
            lg = small[:, 72:104].rearrange("p (t e) -> p t e", t=TILES)
            half = small[:, 136:140].rearrange("p (t s) -> p t s", t=TILES)
            sig = small[:, 144:148].rearrange("p (t s) -> p t s", t=TILES)
            rest = small[:, 152:156].rearrange("p (t s) -> p t s", t=TILES)
            comb = small[:, 256:288].rearrange("p (t e) -> p t e", t=TILES)
            tmp = small[:, 288:320].rearrange("p (t e) -> p t e", t=TILES)
            comb_e = small[:, 320:352].rearrange("p (e t) -> p e t", t=TILES)
            combT = small[0:8, 384:896]
            sums = small[:, 352:360].rearrange("p (t s) -> p t s", t=TILES)
            vs, rs, t4 = small[:, 952:960], small[:, 960:968], small[:, 968:972]
            stats = small[:, 896:920].rearrange("p (t s) -> p t s", t=TILES)
            mv = small[:, 920:928].rearrange("p (t s) -> p t s", t=TILES)
            r2, u4 = small[:, 932:936], small[:, 936:944]
            hT = [work[:, 2048 * i:2048 * i + 2048].rearrange("p (c n) -> p c n", c=4) for i in range(2)]
            sq = [work[:, 4096 + 2048 * i:6144 + 2048 * i].rearrange("p (c n) -> p c n", c=4) for i in range(2)]
            y = [work[:, 8192 + 512 * i:8704 + 512 * i].rearrange("p (t d) -> p t d", t=TILES) for i in range(2)]
            z = [work[:, 9216 + 512 * i:9728 + 512 * i].rearrange("p (t d) -> p t d", t=TILES) for i in range(2)]
            acc = work[:, 10240:10752].rearrange("p (t d) -> p t d", t=TILES)

            def body(block, routed, half_ready, sig_ready, comb_ready, link_sem, up_done, hT_ready, sq_pool, sq_dve,
                     sq_act, down_done, y_raw, z_ready, added, combT_done, combT_ready, last_done, pool_link):
                @block.tensor
                def _(pe):
                    for t in range(TILES):
                        m = pe.matmul(banks[3][:, t * 8:(t + 1) * 8], xnT[:, t * P:(t + 1) * P], k_f1["wr"],
                                      start=True, stop=True)
                    m.then_inc(routed, 1)

                    def up(e):
                        for c in range(4):
                            n = 4 * e + c
                            if n >= 3:
                                pe.wait_ge(hT_ready, n - 2)
                            pe.matmul(banks[n % 3][:, :], k_f1["w1"][:, e * 512 + c * P:e * 512 + (c + 1) * P], xnT[:, :],
                                      start=True, stop=True).then_inc(up_done, 1)

                    def down(e):
                        pe.wait_ge(hT_ready, 4 * e + 4)
                        pe.wait_ge(sq_dve, e + 1)
                        pe.wait_ge(sq_pool, e + 1)
                        pe.wait_ge(sq_act, e + 1)
                        if e >= 2:
                            pe.wait_ge(y_raw, e - 1)
                        for t in range(TILES):
                            zb = banks[4 + 2 * (e % 2) + t // 2][:, (t % 2) * 130:(t % 2) * 130 + 130]
                            for c in range(4):
                                pe.matmul(zb[:, 0:129], hT[e % 2][:, c, t * P:(t + 1) * P], w_f1d[:, c, e, :],
                                          start=(c == 0), stop=(c == 3))
                            for c in range(4):
                                m = pe.matmul(zb[:, 129:130], sq[e % 2][:, c, t * P:(t + 1) * P], ones[:, 0:1],
                                              start=(c == 0), stop=(c == 3))
                        m.then_inc(down_done, 1)

                    for e in range(9):
                        if e < 8:
                            up(e)
                        if e >= 1:
                            down(e - 1)
                    pe.wait_ge(comb_ready, 1)
                    for t in range(TILES):
                        m = pe.transpose(banks[3][0:8, t * P:(t + 1) * P], comb[:, t, :], ident)
                    m.then_inc(combT_done, 1)
                    pe.wait_ge(combT_ready, 1)
                    for t in range(TILES):
                        m = pe.matmul(banks[3][:, t * D:(t + 1) * D], combT[:, t * P:(t + 1) * P], w_f1b[:, :],
                                      start=True, stop=True)
                    m.then_inc(last_done, 1)

                @block.scalar
                def _(act):
                    act.wait_ge(half_ready, 1)
                    act.activation(sig, half, ACT.Tanh).then_inc(sig_ready, 1)
                    for e in range(8):
                        for c in range(4):
                            n = 4 * e + c
                            act.wait_ge(up_done, n + 1)
                            if e >= 2 and c == 0:
                                act.wait_ge(down_done, e - 1)
                            act.activation(hT[e % 2][:, c, :], banks[n % 3][:, :], ACT.Relu,
                                           bias=k_f1["b1"][:, n:n + 1]).then_inc(hT_ready, 1)
                        act.wait_ge(hT_ready, 4 * e + 4)
                        act.activation(sq[e % 2][:, 2:4, :], hT[e % 2][:, 2:4, :], ACT.Square).then_inc(sq_act, 1)
                    act.wait_ge(combT_done, 1)
                    act.copy(combT, banks[3][0:8, :]).then_inc(combT_ready, 1)

                @block.gpsimd
                def _(pool):
                    link = Chain(pool, pool_link)
                    link(pool.memset(acc, 0.0))
                    for e in range(10):
                        if e < 8:
                            pool.wait_ge(hT_ready, 4 * e + 2)
                            if e >= 2:
                                pool.wait_ge(down_done, e - 1)
                            pool.tensor_tensor(sq[e % 2][:, 1, :], hT[e % 2][:, 1, :], hT[e % 2][:, 1, :],
                                               ALU.mult).then_inc(sq_pool, 1)
                        if e >= 2:
                            q = e - 2
                            pool.wait_ge(z_ready, q + 1)
                            g2 = k_f1["g2"][:, q * D:(q + 1) * D].unsqueeze(1).to_broadcast([P, TILES, D])
                            link(pool.tensor_tensor(z[q % 2], z[q % 2], g2, ALU.mult))
                            ins = pool.tensor_tensor(acc, acc, z[q % 2], ALU.add)
                            ins.then_inc(added, 1)
                            pool.wait_ge(added, q + 1)

                @block.vector
                def _(dve):
                    link = Chain(dve, link_sem)
                    dve.wait_ge(routed, 1)
                    link(dve.tensor_tensor(lg, banks[3][:, 0:32].rearrange("p (t e) -> p t e", t=TILES),
                                           k_f1["br"].unsqueeze(1).to_broadcast([P, TILES, 8]), ALU.add))
                    best, place = top_two(dve, link, lg, 8, 160)
                    link(dve.tensor_tensor(half, best[:, :, 0:1], best[:, :, 1:2], ALU.subtract))
                    dve.tensor_scalar(half, half, 0.5, None, ALU.mult).then_inc(half_ready, 1)
                    dve.wait_ge(sig_ready, 1)
                    link(dve.tensor_scalar(sig, sig, 0.5, 0.5, ALU.mult, ALU.add))
                    link(dve.tensor_scalar(rest, sig, -1.0, 1.0, ALU.mult, ALU.add))
                    spread(dve, link, comb, tmp, place, sig, rest, 8)
                    link(dve.tensor_copy(comb_e, comb.rearrange("p t e -> p e t")))
                    dve.sem_inc(comb_ready, 1)

                    link(dve.memset(vs, 1.0))

                    def square(e):
                        dve.wait_ge(hT_ready, 4 * e + 1)
                        if e >= 2:
                            dve.wait_ge(down_done, e - 1)
                        dve.tensor_tensor(sq[e % 2][:, 0, :], hT[e % 2][:, 0, :], hT[e % 2][:, 0, :],
                                          ALU.mult).then_inc(sq_dve, 1)

                    def sums_of(e):
                        dve.wait_ge(down_done, e + 1)
                        link.last_of([dve.tensor_scalar(sums[:, 2 * j:2 * j + 2, :], zs(e, j)[:, :, 128:130], 1.0 / 512,
                                                        None, ALU.mult) for j in range(2)])
                        link(dve.tensor_tensor(t4, sums[:, :, 0], sums[:, :, 0], ALU.mult))
                        link(dve.tensor_tensor(vs[:, 0:4], sums[:, :, 1], t4, ALU.subtract))
                        link(dve.tensor_scalar(vs[:, 0:4], vs[:, 0:4], 0.0, LN_EPS, ALU.max, ALU.add))

                    def zs(e, j):
                        return banks[4 + 2 * (e % 2) + j][:, 0:260].rearrange("p (t d) -> p t d", t=2)

                    def second_norm(e):
                        link(dve.tensor_tensor(r2, rs[:, 4:8], comb_e[:, e, :], ALU.mult))
                        if e >= 2:
                            dve.wait_ge(added, e - 1)
                        for t in range(TILES):
                            ins = dve.tensor_scalar(z[e % 2][:, t, :], y[e % 2][:, t, :], mv[:, t, 0:1], r2[:, t:t + 1],
                                                    ALU.subtract, ALU.mult)
                        ins.then_inc(z_ready, 1)

                    def first_norm(e):
                        if e >= 2:
                            dve.wait_ge(z_ready, e - 1)
                        for t in range(TILES):
                            ins = dve.scalar_tensor_tensor(y[e % 2][:, t, :], zs(e, t // 2)[:, t % 2, 0:D], rs[:, t:t + 1],
                                                           expert_bias[:, e, :], ALU.mult, ALU.add)
                        ins.then_inc(y_raw, 1)
                        dve.wait_ge(y_raw, e + 1)
                        link(dve.tensor_scalar(y[e % 2], y[e % 2], 0.0, None, ALU.max))
                        link.last_of([dve.bn_stats(stats[:, t, :], y[e % 2][:, t, :]) for t in range(TILES)])
                        if e >= 1:
                            dve.wait_ge(z_ready, e)
                        link.last_of([dve.bn_aggr(mv[:, t, :], stats[:, t, :]) for t in range(TILES)])
                        link(dve.tensor_scalar(vs[:, 4:8], mv[:, :, 1], LN_EPS, None, ALU.add))

                    for e in range(10):
                        if e < 8:
                            square(e)
                        if 1 <= e < 9:
                            sums_of(e - 1)
                        if e >= 1:
                            rsqrt(dve, link, rs, vs, u4)
                        if e >= 2:
                            second_norm(e - 2)
                        if 1 <= e < 9:
                            first_norm(e - 1)
                    dve.wait_ge(last_done, 1)
                    dve.wait_ge(added, 8)
                    link(dve.tensor_tensor(acc, acc, banks[3][:, :].rearrange("p (t d) -> p t d", t=TILES), ALU.add))
                    dve.scalar_tensor_tensor(x[:, :, :], acc, tg[:, 5:6], x[:, :, :], ALU.mult, ALU.add)
            stage("routed half sig comb link up hT sq_pool sq_dve sq_act down y_raw z_ready added combTd combTr last plink", body)

        def ffn2():
            lg = small[:, 72:104].rearrange("p (t e) -> p t e", t=TILES)
            ex = small[:, 104:120].rearrange("p (t e) -> p t e", t=TILES)
            den = small[:, 120:124].rearrange("p (t s) -> p t s", t=TILES)
            top = small[:, 124:132].rearrange("p (t s) -> p t s", t=TILES)
            comb = small[:, 256:272].rearrange("p (t e) -> p t e", t=TILES)
            tmp = small[:, 272:288].rearrange("p (t e) -> p t e", t=TILES)
            r = [[work[:, 2048 * i + 512 * e:2048 * i + 512 * e + 512] for e in range(4)] for i in range(2)]
            gT = [work[:, 4096 + 512 * i:4608 + 512 * i] for i in range(2)]

            def body(block, routed, shifted, exp_ready, comb_ready, link_sem, up_done, r_ready, pair_ready,
                     sum_ready, turned, gT_ready, down_done, taken):
                @block.tensor
                def _(pe):
                    for t in range(TILES):
                        m = pe.matmul(banks[6][:, t * 4:(t + 1) * 4], xnT[:, t * P:(t + 1) * P], k_f2["wg"],
                                      start=True, stop=True)
                    m.then_inc(routed, 1)

                    def up(t):
                        for e in range(4):
                            n = 4 * t + e
                            if n >= 4:
                                pe.wait_ge(r_ready, n - 3)
                            pe.matmul(banks[e][:, :], xnT[:, t * P:(t + 1) * P], w_f2e[:, e, :],
                                      start=True, stop=True).then_inc(up_done, 1)

                    def turn(t):
                        pe.wait_ge(sum_ready, t + 1)
                        if t >= 2:
                            pe.wait_ge(gT_ready, t - 1)
                        for c in range(4):
                            m = pe.transpose(banks[4 + t % 2][:, c * P:(c + 1) * P], r[t % 2][0][:, c * P:(c + 1) * P],
                                             ident)
                        m.then_inc(turned, 1)
                        pe.wait_ge(gT_ready, t + 1)
                        if t >= 2:
                            pe.wait_ge(taken, t - 1)
                        for c in range(4):
                            m = pe.matmul(banks[6 + t % 2][:, 0:D], gT[t % 2][:, c * P:(c + 1) * P],
                                          k_f2["wo"][:, c * D:(c + 1) * D], start=(c == 0), stop=(c == 3))
                        m.then_inc(down_done, 1)

                    for t in range(TILES + 1):
                        if t < TILES:
                            up(t)
                        if t == 0:
                            pe.wait_ge(comb_ready, 1)
                        if t >= 1:
                            turn(t - 1)

                @block.scalar
                def _(act):
                    act.wait_ge(shifted, 1)
                    act.activation(ex, lg[:, :, 0:4], ACT.Exp).then_inc(exp_ready, 1)
                    act.wait_ge(comb_ready, 1)
                    for t in range(TILES + 1):
                        if t < TILES:
                            for e in range(4):
                                act.wait_ge(up_done, 4 * t + e + 1)
                                if t >= 2 and e == 0:
                                    act.wait_ge(turned, t - 1)
                                act.activation(r[t % 2][e], banks[e][:, :], ACT.Relu,
                                               scale=comb[:, t, e:e + 1]).then_inc(r_ready, 1)
                        if t >= 1:
                            act.wait_ge(turned, t)
                            if t >= 3:
                                act.wait_ge(down_done, t - 2)
                            act.copy(gT[(t - 1) % 2], banks[4 + (t - 1) % 2][:, :]).then_inc(gT_ready, 1)

                @block.gpsimd
                def _(pool):
                    for t in range(TILES):
                        pool.wait_ge(r_ready, 4 * t + 4)
                        pool.tensor_tensor(r[t % 2][2], r[t % 2][2], r[t % 2][3], ALU.add).then_inc(pair_ready, 1)

                @block.vector
                def _(dve):
                    link = Chain(dve, link_sem)
                    link(dve.memset(lg, NEG))
                    dve.wait_ge(routed, 1)
                    link(dve.tensor_tensor(lg[:, :, 0:4], banks[6][:, 0:16].rearrange("p (t e) -> p t e", t=TILES),
                                           k_f2["bg"].unsqueeze(1).to_broadcast([P, TILES, 4]), ALU.add))
                    best, place = top_two(dve, link, lg, 8, 160)
                    link(dve.tensor_tensor(lg[:, :, 0:4], lg[:, :, 0:4], best[:, :, 0:1].to_broadcast([P, TILES, 4]),
                                           ALU.subtract))
                    dve.sem_inc(shifted, 1)
                    dve.wait_ge(exp_ready, 1)
                    link(dve.tensor_reduce(den[:, :, 0], ex, AX, ALU.add))
                    link(dve.reciprocal(den, den))
                    link(dve.tensor_tensor(ex, ex, den.to_broadcast([P, TILES, 4]), ALU.mult))
                    link.last_of([dve.memset(top, 1.0)])
                    spread(dve, link, comb, tmp, place, top[:, :, 0:1], top[:, :, 1:2], 4)
                    link(dve.tensor_tensor(comb, comb, ex, ALU.mult))
                    dve.sem_inc(comb_ready, 1)
                    for t in range(TILES + 1):
                        if t < TILES:
                            dve.wait_ge(r_ready, 4 * t + 2)
                            link(dve.tensor_tensor(r[t % 2][0], r[t % 2][0], r[t % 2][1], ALU.add))
                            dve.wait_ge(pair_ready, t + 1)
                            dve.tensor_tensor(r[t % 2][0], r[t % 2][0], r[t % 2][2], ALU.add).then_inc(sum_ready, 1)
                        if t >= 1:
                            dve.wait_ge(down_done, t)
                            dve.scalar_tensor_tensor(x[:, t - 1, :], banks[6 + (t - 1) % 2][:, 0:D], tg[:, 6:7],
                                                     x[:, t - 1, :], ALU.mult, ALU.add).then_inc(taken, 1)
            stage("routed shifted expd comb link up r pair sum turned gT down taken", body)

        def perceiver():
            ssq = small[:, 0:48]
            negmax = [small[:, 64 + 8 * i:72 + 8 * i] for i in range(2)]
            den = [small[:, 80 + 8 * i:88 + 8 * i] for i in range(2)]
            rden = [small[:, 96 + 8 * i:104 + 8 * i] for i in range(2)]
            oT = [work[:, 1024 * i:1024 * i + 1024].rearrange("p (c b q) -> p c b q", c=8, b=2) for i in range(2)]
            ksq = work[:, 2048:3072]
            k_rows = work[:, 3072:4096]
            kT = work[:, 4096:5120]
            v = [work[:, 5120 + 1024 * i:6144 + 1024 * i] for i in range(3)]
            s_sb = [work[:, 8192 + 1024 * i:9216 + 1024 * i] for i in range(2)]
            pT = work[:, 10240:11264]
            q_rows = work[:, 11264:12288]
            q_sq = work[:, 12288:13312]
            n = TILES * PAIR

            def body(block, link_sem, pool_link, q_done, q_copied, q_squared, q_normed, q_turned, q_ready, k_done,
                     k_squared, k_normed, k_turned, kT_ready, v_done, v_ready, scored, mx_ready, p_ready, r_ready,
                     p_scaled, p_turned, pT_ready, mixed, oT_ready, done, taken):
                @block.tensor
                def _(pe):
                    def queries(t):
                        pe.wait_ge(v_ready, 2 * (2 * t) + 2)
                        for i in range(2):
                            m = pe.matmul(banks[2 + i][:, :], xnT[:, t * P:(t + 1) * P],
                                          k_x3["wq"][:, 512 * i:512 * i + 512], start=True, stop=True)
                        m.then_inc(q_done, 1)

                    def values(b):
                        if b >= 3:
                            pe.wait_ge(pT_ready, 2 * (b - 2))
                        if b % 2 == 1:
                            pe.wait_ge(q_copied, b // 2 + 1)
                        for i in range(2):
                            m = pe.matmul(banks[2 + i][:, :], cxT[:, b, :, :],
                                          k_x3["wkv"][:, 1024 + 512 * i:1536 + 512 * i], start=True, stop=True)
                        m.then_inc(v_done, 1)

                    def keys(b):
                        if b >= 1:
                            pe.wait_ge(k_normed, b)
                        for i in range(2):
                            m = pe.matmul(banks[i][:, :], cxT[:, b, :, :], k_x3["wkv"][:, 512 * i:512 * i + 512],
                                          start=True, stop=True)
                        m.then_inc(k_done, 1)

                    def turn_keys(b):
                        pe.wait_ge(k_normed, b + 1)
                        if b >= 1:
                            pe.wait_ge(mx_ready, b)
                        for c in range(8):
                            m = pe.transpose(banks[4 + c // 4][:, (c % 4) * P:(c % 4 + 1) * P],
                                             k_rows[:, c * P:(c + 1) * P], ident)
                        m.then_inc(k_turned, 1)

                    def turn_queries(t):
                        pe.wait_ge(q_normed, t + 1)
                        pe.wait_ge(kT_ready, 2 * (2 * t) + 2)
                        for c in range(8):
                            m = pe.transpose(banks[4 + c // 4][:, (c % 4) * P:(c % 4 + 1) * P],
                                             q_rows[:, c * P:(c + 1) * P], ident)
                        m.then_inc(q_turned, 1)

                    def scores(b):
                        pe.wait_ge(kT_ready, 2 * b + 2)
                        pe.wait_ge(q_ready, 2 * (b // 2) + 2)
                        for c in range(8):
                            m = pe.matmul(banks[4 + c // 4][:, (c % 4) * P:(c % 4 + 1) * P],
                                          q_blocks[:, b % 2, c, :, :], kT[:, c * P:(c + 1) * P],
                                          start=True, stop=True)
                        m.then_inc(scored, 1)

                    def turn_probs(b):
                        pe.wait_ge(p_scaled, b + 1)
                        pe.wait_ge(v_ready, 2 * min(b + 2, n - 1) + 2)
                        if b % 2 == 0:
                            pe.wait_ge(q_copied, min(b // 2 + 2, TILES))
                        else:
                            pe.wait_ge(q_copied, min((b + 1) // 2 + 1, TILES))
                        if b >= 1:
                            pe.wait_ge(pT_ready, 2 * b)
                        for c in range(8):
                            m = pe.transpose(banks[2 + c // 4][:, (c % 4) * P:(c % 4 + 1) * P],
                                             s_sb[b % 2][:, c * P:(c + 1) * P], ident)
                        m.then_inc(p_turned, 1)

                    def mix(b):
                        pe.wait_ge(pT_ready, 2 * b + 2)
                        if b >= 1:
                            pe.wait_ge(oT_ready, 2 * b)
                        for c in range(8):
                            for h2 in range(2):
                                r = slice(64 * h2, 64 * h2 + 64)
                                f = slice(c * P + 64 * h2, c * P + 64 * h2 + 64)
                                m = pe.matmul(banks[6][r, c * SEQ:(c + 1) * SEQ], v[b % 3][:, f], pT[:, f],
                                              start=True, stop=True)
                        m.then_inc(mixed, 1)

                    def project(t):
                        pe.wait_ge(oT_ready, 4 * t + 4)
                        if t >= 1:
                            pe.wait_ge(taken, t)
                        for c in range(8):
                            m = pe.matmul(banks[7][:, 0:D], oT[t % 2][:, c, :, :], k_x3["wout"][:, c * D:(c + 1) * D],
                                          start=(c == 0), stop=(c == 7))
                        m.then_inc(done, 1)

                    for i in range(n + 3):
                        if 0 <= i - 1 < n:
                            turn_keys(i - 1)
                        if i >= 4 and i % 2 == 0 and (i - 4) // 2 < TILES:
                            project((i - 4) // 2)
                        if i < n:
                            values(i)
                            keys(i)
                            if i % 2 == 0:
                                queries(i // 2)
                        if i % 2 == 1 and i // 2 < TILES:
                            turn_queries(i // 2)
                        if 0 <= i - 1 < n:
                            scores(i - 1)
                        if 0 <= i - 2 < n:
                            turn_probs(i - 2)
                            mix(i - 2)

                @block.scalar
                def _(act):
                    for i in range(n + 3):
                        b = i - 1
                        if 0 <= b < n:
                            act.wait_ge(k_turned, b + 1)
                            if b >= 1:
                                act.wait_ge(scored, b)
                            for j in range(2):
                                act.activation(kT[:, 512 * j:512 * j + 512], banks[4 + j][:, :], ACT.Identity,
                                               scale=scaled[:, 2:3]).then_inc(kT_ready, 1)
                        if i < n:
                            act.wait_ge(v_done, i + 1)
                            if i >= 3:
                                act.wait_ge(mixed, i - 2)
                            for j in range(2):
                                act.copy(v[i % 3][:, 512 * j:512 * j + 512], banks[2 + j][:, :]).then_inc(v_ready, 1)
                            act.wait_ge(k_done, i + 1)
                            for j in range(2):
                                ins = act.activation(ksq[:, 512 * j:512 * j + 512], banks[j][:, :], ACT.Square)
                            ins.then_inc(k_squared, 1)
                            if i % 2 == 0:
                                act.wait_ge(q_done, i // 2 + 1)
                                if i >= 2:
                                    act.wait_ge(q_turned, i // 2)
                                for j in range(2):
                                    ins = act.copy(q_rows[:, 512 * j:512 * j + 512], banks[2 + j][:, :])
                                ins.then_inc(q_copied, 1)
                        if i % 2 == 1 and i // 2 < TILES:
                            act.wait_ge(q_turned, i // 2 + 1)
                            for h2 in range(2):
                                r = slice(64 * h2, 64 * h2 + 64)
                                for j in range(2):
                                    ins = act.copy(q_blocks[r, :, 4 * j:4 * j + 4, h2, :].rearrange("p b c q -> p c b q"),
                                                   banks[4 + j][r, :].rearrange("p (c b q) -> p c b q", c=4, b=2))
                                ins.then_inc(q_ready, 1)
                        b = i - 2
                        if 0 <= b < n:
                            act.wait_ge(p_turned, b + 1)
                            if b >= 1:
                                act.wait_ge(mixed, b)
                            for j in range(2):
                                act.copy(pT[:, 512 * j:512 * j + 512], banks[2 + j][:, :]).then_inc(pT_ready, 1)
                        b = i - 1
                        if 0 <= b < n:
                            act.wait_ge(mx_ready, b + 1)
                            if b >= 2:
                                act.wait_ge(r_ready, b - 1)
                            for c in range(8):
                                ins = act.activation(s_sb[b % 2][:, c * P:(c + 1) * P], s_sb[b % 2][:, c * P:(c + 1) * P],
                                                     ACT.Exp, bias=negmax[b % 2][:, c:c + 1],
                                                     accum_out=den[b % 2][:, c:c + 1])
                            ins.then_inc(p_ready, 1)
                        b = i - 2
                        if 0 <= b < n:
                            act.wait_ge(mixed, b + 1)
                            if b % 2 == 0 and b >= 4:
                                act.wait_ge(done, (b - 4) // 2 + 1)
                            for h2 in range(2):
                                r = slice(64 * h2, 64 * h2 + 64)
                                act.copy(oT[(b // 2) % 2][r, :, b % 2, :],
                                         banks[6][r, :].rearrange("p (c q) -> p c q", c=8)).then_inc(oT_ready, 1)

                @block.gpsimd
                def _(pool):
                    for i in range(n + 3):
                        b = i - 2
                        if 0 <= b < n:
                            pool.wait_ge(r_ready, b + 1)
                            s3 = s_sb[b % 2].rearrange("p (c j) -> p c j", c=8)
                            pool.tensor_tensor(s3, s3, rden[b % 2].unsqueeze(2).to_broadcast([P, 8, P]),
                                               ALU.mult).then_inc(p_scaled, 1)
                        if i % 2 == 0 and i < n:
                            pool.wait_ge(q_copied, i // 2 + 1)
                            if i >= 2:
                                pool.wait_ge(q_normed, i // 2)
                            pool.tensor_tensor(q_sq, q_rows, q_rows, ALU.mult).then_inc(q_squared, 1)

                @block.vector
                def _(dve):
                    link = Chain(dve, link_sem)

                    def norms(sq):
                        link(dve.tensor_reduce(ssq[:, 0:16], sq.rearrange("p (h d) -> p h d", d=XD), AX, ALU.add))
                        link(dve.tensor_scalar(ssq[:, 0:16], ssq[:, 0:16], 1.0 / XD, 1e-16, ALU.mult, ALU.max))
                        rsqrt(dve, link, ssq[:, 16:32], ssq[:, 0:16], ssq[:, 32:48])

                    def scale_rows(dst, src, j):
                        return dve.tensor_tensor(dst[:, 512 * j:512 * j + 512].rearrange("p (h d) -> p h d", d=XD),
                                                 src.rearrange("p (h d) -> p h d", d=XD),
                                                 ssq[:, 16 + 8 * j:24 + 8 * j].unsqueeze(2).to_broadcast([P, 8, XD]),
                                                 ALU.mult)

                    for i in range(n + 3):
                        b = i - 2
                        if 0 <= b < n:
                            dve.wait_ge(p_ready, b + 1)
                            if b >= 2:
                                dve.wait_ge(p_scaled, b - 1)
                            dve.reciprocal(rden[b % 2], den[b % 2]).then_inc(r_ready, 1)
                        if i < n:
                            dve.wait_ge(k_squared, i + 1)
                            norms(ksq)
                            if i >= 1:
                                dve.wait_ge(k_turned, i)
                            link.last_of([scale_rows(k_rows, banks[j][:, :], j) for j in range(2)])
                            dve.sem_inc(k_normed, 1)
                        b = i - 1
                        if 0 <= b < n:
                            dve.wait_ge(scored, b + 1)
                            if b >= 2:
                                dve.wait_ge(p_turned, b - 1)
                            s3 = s_sb[b % 2].rearrange("p (c j) -> p c j", c=8)
                            nb = neg3[:, b, :, :].rearrange("p a s -> p (a s)")
                            link.last_of([dve.tensor_tensor(s3[:, 4 * j:4 * j + 4, :],
                                                            banks[4 + j][:, :].rearrange("p (c j) -> p c j", c=4),
                                                            nb.unsqueeze(1).to_broadcast([P, 4, P]), ALU.add)
                                          for j in range(2)])
                            dve.tensor_reduce(negmax[b % 2], s3, AX, ALU.max, negate=True).then_inc(mx_ready, 1)
                        if i % 2 == 0 and i < n:
                            dve.wait_ge(q_squared, i // 2 + 1)
                            norms(q_sq)
                            link.last_of([scale_rows(q_rows, q_rows[:, 512 * j:512 * j + 512], j) for j in range(2)])
                            dve.sem_inc(q_normed, 1)
                        if i >= 4 and i % 2 == 0 and (i - 4) // 2 < TILES:
                            t = (i - 4) // 2
                            dve.wait_ge(done, t + 1)
                            link(dve.scalar_tensor_tensor(x[:, t, :], banks[7][:, 0:D], tg[:, 3:4], x[:, t, :],
                                                          ALU.mult, ALU.add))
                            dve.tensor_tensor(x[:, t, :], x[:, t, :], bout3[:, :], ALU.add).then_inc(taken, 1)
            stage("link plink q_done q_copied q_sq q_normed q_turned q_ready k_done k_sq k_normed k_turned kT_ready "
                  "v_done v_ready scored mx_ready p_ready r_ready p_scaled p_turned pT_ready mixed oT_ready done taken",
                  body)

        def rms_norm(src, gain, dst=None, dstT=None, gate=None):
            sq = work[:, 0:512].rearrange("p (t d) -> p t d", t=TILES)
            ms, rs, tmp = small[:, 0:4], small[:, 4:8], small[:, 8:12]

            def body(block, squared, link_sem, normed, turned):
                @block.gpsimd
                def _(pool):
                    pool.tensor_tensor(sq, src[:, :, :], src[:, :, :], ALU.mult).then_inc(squared, 1)

                @block.vector
                def _(dve):
                    link = Chain(dve, link_sem)
                    dve.wait_ge(squared, 1)
                    link(dve.tensor_reduce(ms, sq, AX, ALU.add))
                    link(dve.tensor_scalar(ms, ms, 1.0 / D, RMS_EPS, ALU.mult, ALU.add))
                    rsqrt(dve, link, rs, ms, tmp)
                    to = sq if gate is not None else dst
                    for t in range(TILES):
                        ins = dve.scalar_tensor_tensor(to[:, t, :], src[:, t, :], rs[:, t:t + 1], gain, ALU.mult, ALU.mult)
                        if gate is None:
                            ins.then_inc(normed, 1)
                        else:
                            link(ins)
                    if gate is not None:
                        dve.scalar_tensor_tensor(x[:, :, :], sq, gate, x[:, :, :], ALU.mult, ALU.add)

                if dstT is None:
                    return

                @block.tensor
                def _(pe):
                    for t in range(TILES):
                        pe.wait_ge(normed, t + 1)
                        m = pe.transpose(banks[0][:, t * P:(t + 1) * P], dst[:, t, :], ident)
                    m.then_inc(turned, 1)

                @block.scalar
                def _(act):
                    act.wait_ge(turned, 1)
                    act.copy(dstT, banks[0][:, :])
            stage("squared link normed turned", body)

        def ffn3(src):
            probs = small[:, 72:104].rearrange("p (t e) -> p t e", t=TILES)
            tot = small[:, 136:140].rearrange("p (t s) -> p t s", t=TILES)
            wts = small[:, 140:148].rearrange("p (t s) -> p t s", t=TILES)
            comb = small[:, 256:288].rearrange("p (t e) -> p t e", t=TILES)
            chosen = small[:, 288:320].rearrange("p (t e) -> p t e", t=TILES)
            tmp = small[:, 320:352].rearrange("p (t e) -> p t e", t=TILES)
            ran = small[:, 352:392].rearrange("p (t e) -> p t e", t=TILES + 1)
            top = small[:, 392:400].rearrange("p (t s) -> p t s", t=TILES)
            h = [work[:, 512 * i:512 * i + 512] for i in range(2)]
            hT = [work[:, 1024 + 512 * i:1536 + 512 * i] for i in range(2)]
            g = [work[:, 2048 + 512 * i:2560 + 512 * i] for i in range(2)]
            capacity = float(int(1.25 * BATCH * SEQ * 2 / 8))
            steps = [(t, q) for t in range(TILES) for q in range(4)]

            def body(block, routed, tanh_done, chosen_ready, ranked, comb_ready, link_sem, up_done, g_ready, h_ready,
                     turned, hT_ready, down_done, taken):
                @block.tensor
                def _(pe):
                    for t in range(TILES):
                        m = pe.matmul(banks[6][:, t * 8:(t + 1) * 8], xnT[:, t * P:(t + 1) * P], k_f3["wr"],
                                      start=True, stop=True)
                    m.then_inc(routed, 1)
                    pe.wait_ge(chosen_ready, 1)
                    for t in range(TILES):
                        pe.matmul(banks[7][:, t * 8:(t + 1) * 8], k_const["tri"], chosen[:, t, :],
                                  start=True, stop=False)
                        m = pe.matmul(banks[7][:, t * 8:(t + 1) * 8], ones[:, :], ran[:, t, :],
                                      start=False, stop=True)
                    m.then_inc(ranked, 1)

                    def up(s):
                        t, q = steps[s]
                        if s >= 2:
                            pe.wait_ge(g_ready, s - 1)
                        pe.matmul(banks[s % 2][:, :], xnT[:, t * P:(t + 1) * P], k_f3["w1"][:, q * 512:(q + 1) * 512],
                                  start=True, stop=True).then_inc(up_done, 1)

                    def turn(s):
                        pe.wait_ge(h_ready, s + 1)
                        if s >= 2:
                            pe.wait_ge(hT_ready, s - 1)
                        for c in range(4):
                            m = pe.transpose(banks[4 + s % 2][:, c * P:(c + 1) * P], h[s % 2][:, c * P:(c + 1) * P], ident)
                        m.then_inc(turned, 1)

                    def down(s):
                        t, q = steps[s]
                        pe.wait_ge(hT_ready, s + 1)
                        if s == 0:
                            pe.wait_ge(comb_ready, 1)
                        if q == 0 and t >= 2:
                            pe.wait_ge(taken, t - 1)
                        for c in range(4):
                            m = pe.matmul(banks[6 + t % 2][:, 0:D], hT[s % 2][:, c * P:(c + 1) * P],
                                          k_f3["w2"][:, (4 * q + c) * D:(4 * q + c + 1) * D],
                                          start=(q == 0 and c == 0), stop=(q == 3 and c == 3))
                        m.then_inc(down_done, 1)

                    n = len(steps)
                    for s in range(n + 2):
                        if s < n:
                            up(s)
                        if 0 <= s - 2 < n:
                            down(s - 2)
                        if 0 <= s - 1 < n:
                            turn(s - 1)

                @block.scalar
                def _(act):
                    act.wait_ge(routed, 1)
                    act.activation(probs, banks[6][:, 0:32].rearrange("p (t e) -> p t e", t=TILES), ACT.Tanh,
                                   scale=0.5).then_inc(tanh_done, 1)
                    n = len(steps)
                    for s in range(n + 1):
                        if s < n:
                            act.wait_ge(up_done, s + 1)
                            if s >= 2:
                                act.wait_ge(h_ready, s - 1)
                            act.activation(g[s % 2], banks[s % 2][:, :], ACT.Gelu).then_inc(g_ready, 1)
                        if s >= 1:
                            act.wait_ge(turned, s)
                            if s >= 3:
                                act.wait_ge(down_done, s - 2)
                            act.copy(hT[(s - 1) % 2], banks[4 + (s - 1) % 2][:, :]).then_inc(hT_ready, 1)

                @block.vector
                def _(dve):
                    link = Chain(dve, link_sem)
                    dve.wait_ge(tanh_done, 1)
                    link(dve.tensor_scalar(probs, probs, 0.5, 0.5, ALU.mult, ALU.add))
                    best, place = top_two(dve, link, probs, 8, 160)
                    link(dve.memset(top, 1.0))
                    spread(dve, link, chosen, tmp, place, top[:, :, 0:1], top[:, :, 1:2], 8)
                    link(dve.tensor_copy(ran[:, 0, :], run_mask[:, :]))
                    for t in range(TILES):
                        link(dve.tensor_tensor(ran[:, t + 1, :], ran[:, t, :], chosen[:, t, :], ALU.add))
                    dve.sem_inc(chosen_ready, 1)
                    link(dve.tensor_copy(run_mask[:, :], ran[:, TILES, :]))
                    link(dve.tensor_tensor(tot, best[:, :, 0:1], best[:, :, 1:2], ALU.add))
                    link(dve.tensor_scalar(tot, tot, 1e-6, None, ALU.add))
                    link(dve.reciprocal(tot, tot))
                    link(dve.tensor_tensor(wts, best[:, :, 0:2], tot.to_broadcast([P, TILES, 2]), ALU.mult))
                    spread(dve, link, comb, tmp, place, wts[:, :, 0:1], wts[:, :, 1:2], 8)
                    dve.wait_ge(ranked, 1)
                    link(dve.tensor_scalar(tmp, banks[7][:, 0:32].rearrange("p (t e) -> p t e", t=TILES), capacity, None,
                                           ALU.is_lt))
                    link(dve.tensor_tensor(comb, comb, tmp, ALU.mult))
                    dve.sem_inc(comb_ready, 1)
                    n = len(steps)
                    for s in range(n + 2):
                        if s < n:
                            t, q = steps[s]
                            dve.wait_ge(g_ready, s + 1)
                            if s >= 2:
                                dve.wait_ge(turned, s - 1)
                            for j in range(2):
                                ins = dve.tensor_scalar(h[s % 2][:, 256 * j:256 * j + 256], g[s % 2][:, 256 * j:256 * j + 256],
                                                        comb[:, t, 2 * q + j:2 * q + j + 1], None, ALU.mult)
                            ins.then_inc(h_ready, 1)
                        if s >= 2 and steps[s - 2][1] == 3:
                            t = steps[s - 2][0]
                            dve.wait_ge(down_done, s - 1)
                            dve.tensor_tensor(src[:, t, :], banks[6 + t % 2][:, 0:D], src[:, t, :],
                                              ALU.add).then_inc(taken, 1)
            stage("routed tanh chosen ranked comb link up g h turned hT down taken", body)

        with nc.Fori(0, BLOCKS) as i:
            load_block(i)
            layer_norm(x, xn)
            retention()
            layer_norm(x, xn, xnT[:, :])
            ffn0()
            layer_norm(x, xn, xnT[:, :])
            with_bias = add_gated(1)

            def finish1(dve, t, y):
                return with_bias(dve, t, y)

            def add_bias(bias):
                def body(block):
                    @block.gpsimd
                    def _(pool):
                        pool.tensor_tensor(x[:, :, :], x[:, :, :], bias.unsqueeze(1).to_broadcast([P, TILES, D]), ALU.add)
                with nc.Block() as block:
                    body(block)
            add_bias(bo1[:, :])
            attention(xnT[:, :], cT[:, :], k_x1, scaled[:, 0:1], k_x1["bk"], bv1[:, :], None, None, finish1)
            layer_norm(x, xn, xnT[:, :])
            ffn1()
            layer_norm(x, xn, xnT[:, :])
            attention(xnT[:, :], cT[:, :], k_x2, None, None, None, neg2, any2, add_gated(2))
            layer_norm(x, xn, xnT[:, :])
            ffn2()
            layer_norm(x, xn)
            layer_norm(xn, xn, cxT[:, :, 1, :], k_x3["llg"], k_x3["llb"], also=xnT[:, :])
            layer_norm(ctok, xn, cxT[:, :, 0, :], k_x3["lxg"], k_x3["lxb"])
            perceiver()
            layer_norm(x, xn, xnT[:, :])
            add_to_z = lambda dve, t, y: dve.tensor_tensor(xn[:, t, :], y, xn[:, t, :], ALU.add)

            def add_ob(block):
                @block.gpsimd
                def _(pool):
                    pool.tensor_tensor(xn[:, :, :], xn[:, :, :],
                                       k_a3["bo"].unsqueeze(1).to_broadcast([P, TILES, D]), ALU.add)
            with nc.Block() as block:
                add_ob(block)
            attention(xnT[:, :], xnT[:, :], k_a3, scaled[:, 1:2], k_a3["bk"], bv3[:, :], None, None, add_to_z)
            rms_norm(xn, k_f3["n1"], xn, xnT[:, :])
            ffn3(xn)
            rms_norm(xn, k_f3["n2"], gate=tg[:, 7:8])
            store_block(i)


def layouts(a):
    import numpy as np

    f = np.float32
    rows = lambda v: np.broadcast_to(np.asarray(v).reshape(1, -1), (P, np.asarray(v).size))
    col = lambda v: np.asarray(v).reshape(-1, 1)
    pack = lambda *xs: np.ascontiguousarray(np.concatenate([np.asarray(z).reshape(P, -1) for z in xs], axis=1))
    n = np.arange(P)
    gap = n[None, :] - n[:, None]
    same = (n[None, :] // SEQ) == (n[:, None] // SEQ)
    decay = np.where(same & (gap >= 0), 0.9 ** np.maximum(gap, 0), 0.0)
    pmask = (n[:, None] // SEQ) == (n[None, :] // HD % 2)
    out = {"consts": pack(np.eye(P, dtype=f), (n[:, None] // HD == np.arange(HEADS)).astype(f), pmask.astype(f),
                          (gap > 0).astype(f), rows(np.arange(HEADS, dtype=f)), decay.astype(f))}
    out["l0"] = pack(a["L0_ffn_gate_w"].T, a["L0_ffn_shared_gate_w"].T) if False else pack(
        np.concatenate([a["L0_ffn_gate_w"].T, a["L0_ffn_shared_gate_w"].T], axis=1),
        a["L0_ffn_w_gate_up"].reshape(4, 4, D, 2, 64).transpose(2, 0, 3, 1, 4),
        a["L0_ffn_shared_w_gate"].T, a["L0_ffn_shared_w_up"].T,
        a["L0_ffn_w_down"].reshape(8, P, D).transpose(1, 0, 2),
        np.concatenate([a["L0_ffn_shared_w_down"].T, np.zeros((32, D), f)]).reshape(3, P, D).transpose(1, 0, 2))
    out["x1"] = pack(*[a["L1_xattn_w" + c].T for c in "qkvo"], col(a["L1_xattn_bq"]), col(a["L1_xattn_bk"]),
                     rows(a["L1_xattn_bv"]), rows(a["L1_xattn_bo"]))
    chunked = lambda v: v.reshape(8, 4, P).transpose(2, 0, 1)
    out["f1"] = pack(a["L1_ffn_Wr"], rows(a["L1_ffn_br"]), chunked(a["L1_ffn_b1"]), chunked(a["L1_ffn_g1"]),
                     chunked(a["L1_ffn_be1"]), a["L1_ffn_W1"].transpose(1, 0, 2), rows(a["L1_ffn_g2"]))
    out["b2"] = np.ascontiguousarray(rows(a["L1_ffn_b2"]))
    out["f1b"] = np.ascontiguousarray(a["L1_ffn_be2"])
    out["f1d"] = np.ascontiguousarray(a["L1_ffn_W2"].reshape(8, 4, P, D).transpose(2, 1, 0, 3))
    out["gates"] = np.ascontiguousarray(rows(np.concatenate([a["g_xattn"], a["g_ffn"]])))
    out["x2"] = pack(*[a["L2_xattn_W_" + c].T for c in "QKVO"])
    out["f2"] = pack(a["L2_ffn_Wg"].T, rows(a["L2_ffn_bg"]), a["L2_ffn_Wi"].T,
                     a["L2_ffn_Wo"].T.reshape(4, P, D).transpose(1, 0, 2))
    out["lora_a"] = np.ascontiguousarray(a["L2_ffn_A"].transpose(1, 0, 2))
    out["lora_b"] = np.ascontiguousarray(a["L2_ffn_B"].transpose(2, 0, 1))
    twice = lambda v: col(np.concatenate([v, v]))
    out["x3"] = pack(col(a["L3_xattn_ln_x_g"]), col(a["L3_xattn_ln_x_b"]), col(a["L3_xattn_ln_l_g"]),
                     col(a["L3_xattn_ln_l_b"]), twice(a["L3_xattn_qn_g"]), twice(a["L3_xattn_kn_g"]),
                     rows(a["L3_xattn_bout"]), a["L3_xattn_Wq"], a["L3_xattn_Wkv"],
                     a["L3_xattn_Wout"].reshape(8, P, D).transpose(1, 0, 2))
    rep = lambda w: np.repeat(w.reshape(-1, 4, HD), 4, axis=1).reshape(-1, D)
    out["a3"] = pack(a["L3_ffn_qw"], rep(a["L3_ffn_kw"]), rep(a["L3_ffn_vw"]), a["L3_ffn_ow"],
                     col(a["L3_ffn_qb"]), col(rep(a["L3_ffn_kb"])), rows(rep(a["L3_ffn_vb"])), rows(a["L3_ffn_ob"]))
    out["f3"] = pack(a["L3_ffn_gate_w"], rows(a["L3_ffn_norm1_w"]), rows(a["L3_ffn_norm2_w"]),
                     a["L3_ffn_w1"].transpose(1, 0, 2), a["L3_ffn_w2"].reshape(8, 2, P, D).transpose(2, 0, 1, 3))
    out["x"] = np.ascontiguousarray(a["x"]).reshape(BATCH * SEQ, D)
    out["ctx"] = np.ascontiguousarray(a["ctx_1024"]).reshape(BATCH * SEQ, D)
    out["mask2"] = np.ascontiguousarray(a["mask_BxSxS2_bf0"]).reshape(BATCH * SEQ, SEQ).view(np.int32)
    out["mask3"] = np.ascontiguousarray(a["mask_BxS2_bf1"]).view(np.int32)
    return out


def kernel(**inputs):
    import numpy as _np
    import concourse.bacc as _bacc
    from concourse import mybir as _mybir
    from concourse.bass_utils import run_bass_kernel_spmd as _run

    nc = _bacc.Bacc("TRN2", target_bir_lowering=False, num_devices=1)
    arrays, args = {}, {}
    for name, a in layouts({k: _np.asarray(v) for k, v in inputs.items()}).items():
        arrays[f"in_{name}_dram"] = a
        args[name] = nc.dram_tensor(f"in_{name}_dram", a.shape, _mybir.dt.from_np(a.dtype), kind="ExternalInput").ap()
    out = nc.dram_tensor("out_0_dram", (BATCH * SEQ, D), _mybir.dt.float32, kind="ExternalOutput").ap()
    build(nc, args, out)
    r = _run(nc, [arrays], core_ids=[0])
    return r.results[0]["out_0_dram"].reshape(BATCH, SEQ, D)
```

```python
from contextlib import ExitStack

import concourse.bass as bass
from concourse import mybir

F32 = mybir.dt.float32
I32 = mybir.dt.int32
U32 = mybir.dt.uint32
U8 = mybir.dt.uint8
ALU = mybir.AluOpType
ACT = mybir.ActivationFunctionType
AX = mybir.AxisListType.X

P = 128
BATCH, SEQ, D = 32, 64, 128
TILES = 4
TOK = TILES * P
PAIR = P // SEQ
BLOCKS = BATCH * SEQ // TOK
HEADS, HD = 16, 8
HP = HEADS // 2
GROUP = 8
XD = 64
LN_EPS, RMS_EPS = 1e-5, 1e-6
NEG = -1e30

CONST = dict(ident=P, hmask=GROUP, half=2, pmask=P, tri=P, iota=HEADS, decay=P)
L0 = dict(router=17, gu=4 * 512, sgu=704, down=11 * D)
XA = dict(wq=D, wk=D, wv=D, wo=D)
XB = dict(bq=1, bk=1, bv=D, bo=D)
L1F = dict(wr=8, br=8, b1=32, g1=32, be1=32, w1=8 * 512, g2=8 * D)
L2F = dict(wg=4, bg=4, wo=4 * D)
L3X = dict(lxg=1, lxb=1, llg=1, llb=1, qn=1, kn=1, bout=D, wq=1024, wkv=2048, wout=8 * D)
L3F = dict(wr=8, n1=D, n2=D, w1=8 * 256, w2=16 * D)

FILL_BEFORE_ROWS = (0, 3, 3, 3, 3, 3, 3, 3)
FILL_BEFORE_SCORES = {1: 0, 3: 0, 6: 0}


def width(pieces):
    return sum(pieces.values())


def pieces_of(tensor, pieces):
    at, out = 0, {}
    for name, n in pieces.items():
        out[name] = tensor[:, at:at + n]
        at += n
    return out


class Chain:

    def __init__(self, sem):
        self.engine, self.sem, self.n = None, sem, 0

    def on(self, engine):
        self.engine = engine
        return self

    def __call__(self, ins):
        self.n += 1
        ins.then_inc(self.sem, 1)
        self.engine.wait_ge(self.sem, self.n)

    def last_of(self, instructions):
        for ins in instructions:
            self.n += 1
            ins.then_inc(self.sem, 1)
        self.engine.wait_ge(self.sem, self.n)


class Parts:

    def __init__(self):
        self.of = {}

    def tensor(self, part):
        self.of["tensor"] = part

    def vector(self, part):
        self.of["vector"] = part

    def scalar(self, part):
        self.of["scalar"] = part

    def gpsimd(self, part):
        self.of["gpsimd"] = part

    def sync(self, part):
        self.of["sync"] = part


class Ends:

    def __init__(self, bank0, all_used):
        self.bank0, self.all_used = bank0, all_used


def wait_for(engine, signal):
    sem, value = signal
    engine.wait_ge(sem, value)


def rsqrt(dve, link, y, v, tmp):
    vb, yb = v.bitcast(I32), y.bitcast(I32)
    link(dve.tensor_scalar(yb, vb, 1, None, ALU.logical_shift_right))
    yield
    link(dve.tensor_scalar(yb, yb, -1.0, 1597463007.0, ALU.mult, ALU.add))
    yield
    for _ in range(3):
        link(dve.tensor_tensor(tmp, y, y, ALU.mult))
        yield
        link(dve.scalar_tensor_tensor(tmp, tmp, -0.5, v, ALU.mult, ALU.mult))
        yield
        link(dve.scalar_tensor_tensor(y, tmp, 1.5, y, ALU.add, ALU.mult))
        yield


def run(steps):
    for _ in steps:
        pass


def some(steps, n):
    for _ in range(n):
        next(steps, None)


def build(nc, args, out):
    ctx = ExitStack()
    with ctx:
        def sb(name, shape, dt=F32):
            return ctx.enter_context(nc.sbuf_tensor(name, shape, dt))

        consts = sb("consts", [P, width(CONST)])
        ones = sb("ones", [P, P])
        w_l0 = sb("w_l0", [P, width(L0)])
        w_x1 = sb("w_x1", [P, width(XA) + width(XB)])
        w_f1 = sb("w_f1", [P, width(L1F)])
        w_f1b = sb("w_f1b", [8, D])
        w_f1d = sb("w_f1d", [P, 4, 8, D + 1])
        w_x2 = sb("w_x2", [P, width(XA)])
        w_f2 = sb("w_f2", [P, width(L2F)])
        w_f2e = sb("w_f2e", [P, 4, 512])
        w_x3 = sb("w_x3", [P, width(L3X)])
        w_a3 = sb("w_a3", [P, width(XA) + width(XB)])
        w_f3 = sb("w_f3", [P, width(L3F)])
        gates = sb("gates", [P, 8])
        tg = sb("tg", [P, 8])
        expert_bias = sb("expert_bias", [P, 8, D])
        scaled = sb("scaled", [P, 8])
        bo1 = sb("bo1", [P, D])
        bout3 = sb("bout3", [P, D])
        bv1 = sb("bv1", [P, D])
        bv3 = sb("bv3", [P, D])
        run_mask = sb("run_mask", [P, 8])
        v_blocks = sb("v_blocks", [P, TILES, HP, PAIR, 18])
        q_blocks = sb("q_blocks", [P, PAIR, 8, 2, XD])
        x = sb("x", [P, TILES, D])
        cT = sb("cT", [P, TOK])
        xn = sb("xn", [P, TILES, D])
        x_next = sb("x_next", [P, TILES, D])
        xn_next = sb("xn_next", [P, TILES, D])
        xnT = sb("xnT", [P, TOK])
        cxT = sb("cxT", [P, TILES * PAIR, 2, SEQ])
        mask2_words = sb("mask2", [P, TILES, SEQ // 4], I32)
        mask2 = mask2_words[:, :, :].bitcast(U8)
        mask3_words = sb("mask3", [P, TILES * PAIR, SEQ // 4], I32)
        mask3 = mask3_words[:, :, :].bitcast(U8)
        neg2 = sb("neg2", [P, TILES, SEQ])
        any2 = sb("any2", [P, TILES])
        neg3 = sb("neg3", [P, TILES * PAIR, 2, SEQ])
        small = sb("small", [P, 976])
        norm_small = sb("norm_small", [P, 256])
        bn_small = sb("bn_small", [P, 48])
        norm_rows = sb("norm_rows", [P, 2, D])
        work = sb("work", [P, 13312])
        lora_a = work[0:4, 0:4 * D].rearrange("p (e d) -> p e d", e=4)
        lora_b = work[0:4, 1024:1024 + 2048].rearrange("p (e f) -> p e f", e=4)
        b2 = work[:, 4096:4096 + 8 * D]
        wi = work[:, 3072:3072 + 512]

        banks = [ctx.enter_context(nc.psum_tensor(f"bank{i}", [P, 512], F32)) for i in range(8)]

        k_const = pieces_of(consts, CONST)
        k_l0 = pieces_of(w_l0, L0)
        k_x1 = pieces_of(w_x1, {**XA, **XB})
        k_f1 = pieces_of(w_f1, L1F)
        k_x2 = pieces_of(w_x2, XA)
        k_f2 = pieces_of(w_f2, L2F)
        k_x3 = pieces_of(w_x3, L3X)
        k_a3 = pieces_of(w_a3, {**XA, **XB})
        k_f3 = pieces_of(w_f3, L3F)
        ident = k_const["ident"]
        eps_cache = {}

        def named(names):
            named.n += 1
            return [ctx.enter_context(nc.semaphore(f"{n}_{named.n}")) for n in names.split()]
        named.n = 0

        def stage(names, body):
            sems = named(names)
            parts = Parts()
            body(parts, *sems)
            stages.append((parts, sems))
        stages = []

        flow = named("rows_ready rows_turned rowsT_ready dve_steps")
        rows_ready, rows_turned, rowsT_ready, steps_sem = flow
        dve_steps = Chain(steps_sem)

        def norm_all(dve, link):
            run(layer_norm(dve, link, [(x, xn, t) for t in range(TILES)]))
            dve.sem_inc(rows_ready, 2)

        def scratch():
            at = 64 * scratch.turn
            scratch.turn = (scratch.turn + 1) % 4
            return norm_small[:, at:at + 64]
        scratch.turn = 0

        def layer_norm(dve, link, jobs):
            n, s = len(jobs), scratch()
            mv = s[:, 0:2 * n].rearrange("p (t s) -> p t s", t=n)
            ve, rs, tmp = (s[:, 16 + n * k:16 + n * k + n] for k in range(3))
            stats = bn_small[:, 0:6 * n].rearrange("p (t s) -> p t s", t=n)
            link.last_of([dve.bn_stats(stats[:, k, :], src[:, t, :]) for k, (src, _, t) in enumerate(jobs)])
            yield
            link.last_of([dve.bn_aggr(mv[:, k, :], stats[:, k, :]) for k in range(n)])
            yield
            link(dve.tensor_scalar(ve, mv[:, :, 1], LN_EPS, None, ALU.add))
            yield
            yield from rsqrt(dve, link, rs, ve, tmp)
            link.last_of([dve.tensor_scalar(dst[:, t, :], src[:, t, :], mv[:, k, 0:1], rs[:, k:k + 1],
                                            ALU.subtract, ALU.mult) for k, (src, dst, t) in enumerate(jobs)])
            yield

        def pair_tiles(pair):
            return (2 * pair, 2 * pair + 1)

        def norm_pair(dve, link, pair):
            yield from layer_norm(dve, link, [(x, xn, t) for t in pair_tiles(pair)])
            dve.sem_inc(rows_ready, 1)

        def norm_pair_twice(dve, link, pair):
            yield from layer_norm(dve, link, [(x, xn, t) for t in pair_tiles(pair)])
            yield from layer_norm(dve, link, [(xn, xn, t) for t in pair_tiles(pair)])
            dve.sem_inc(rows_ready, 1)

        def rms_scales(dve, link, pair):
            s = scratch()
            ms, rs, tmp = s[:, 0:2], s[:, 2:4], s[:, 4:6]
            link.last_of([dve.scalar_tensor_tensor(norm_rows[:, t % 2, :], xn[:, t, :], 1.0, xn[:, t, :], ALU.mult,
                                                   ALU.mult, accum_out=ms[:, t % 2:t % 2 + 1])
                          for t in pair_tiles(pair)])
            yield
            link(dve.tensor_scalar(ms, ms, 1.0 / D, RMS_EPS, ALU.mult, ALU.add))
            yield
            yield from rsqrt(dve, link, rs, ms, tmp)
            return rs

        def rms_pair(dve, link, pair):
            rs = yield from rms_scales(dve, link, pair)
            link.last_of([dve.scalar_tensor_tensor(xn[:, t, :], xn[:, t, :], rs[:, t % 2:t % 2 + 1], k_f3["n1"],
                                                   ALU.mult, ALU.mult) for t in pair_tiles(pair)])
            dve.sem_inc(rows_ready, 1)

        def rms_last(dve, link, pair):
            rs = yield from rms_scales(dve, link, pair)
            link.last_of([dve.scalar_tensor_tensor(norm_rows[:, t % 2, :], xn[:, t, :], rs[:, t % 2:t % 2 + 1],
                                                   k_f3["n2"], ALU.mult, ALU.mult) for t in pair_tiles(pair)])
            yield
            two = slice(2 * pair, 2 * pair + 2)
            link(dve.scalar_tensor_tensor(x[:, two, :], norm_rows[:, :, :], tg[:, 7:8], x[:, two, :],
                                          ALU.mult, ALU.add))
            dve.sem_inc(rows_ready, 1)

        def keep_clock(pe, bank, n):
            for _ in range(n):
                pe.matmul(bank[:, :], ident, consts[:, 0:512], start=True, stop=True)

        def turn_pairs(pe, prev, turn, rows):
            if prev is not None:
                wait_for(pe, prev.bank0)
            for pair in range(2):
                if pair == 0:
                    keep_clock(pe, banks[1], FILL_BEFORE_ROWS[turn])
                pe.wait_ge(rows_ready, 2 * turn + pair + 1)
                for t in pair_tiles(pair):
                    m = pe.transpose(banks[pair][:, (t % 2) * P:(t % 2 + 1) * P], rows[:, t, :], ident)
                m.then_inc(rows_turned, 1)

        def take_pairs(act, turn):
            for pair in range(2):
                act.wait_ge(rows_turned, 2 * turn + pair + 1)
                act.copy(xnT[:, pair * 2 * P:(pair + 1) * 2 * P], banks[pair][:, 0:2 * P]).then_inc(rowsT_ready, 1)

        def top_two(dve, link, scores, n, at):
            best = small[:, at:at + 32].rearrange("p (t s) -> p t s", t=TILES)
            where = small[:, at + 32:at + 64].bitcast(U32).rearrange("p (t s) -> p t s", t=TILES)
            place = small[:, at + 64:at + 72].rearrange("p (t s) -> p t s", t=TILES)
            link.last_of([dve.max(best[:, t, :], scores[:, t, :]) for t in range(TILES)])
            link.last_of([dve.max_index(where[:, t, :], best[:, t, :], scores[:, t, :]) for t in range(TILES)])
            link(dve.tensor_copy(place, where[:, :, 0:2]))
            return best, place

        def spread(dve, link, dst, tmp, place, first, second, n):
            iota = k_const["iota"][:, 0:n].unsqueeze(1).to_broadcast([P, TILES, n])

            def wide(a):
                return a.to_broadcast([P, TILES, n])
            link.last_of([dve.tensor_tensor(dst, iota, wide(place[:, :, 0:1]), ALU.is_equal),
                          dve.tensor_tensor(tmp, iota, wide(place[:, :, 1:2]), ALU.is_equal)])
            link.last_of([dve.tensor_tensor(dst, dst, wide(first), ALU.mult),
                          dve.tensor_tensor(tmp, tmp, wide(second), ALU.mult)])
            link(dve.tensor_tensor(dst, dst, tmp, ALU.add))

        class KeysValues:

            def __init__(self, w, src, k_bias, v_bias):
                self.w, self.src, self.k_bias, self.v_bias = w, src, k_bias, v_bias
                self.sems = named("k_done v_done k_ready v_ready kx_ready")
                self.k_done, self.v_done, self.k_ready, self.v_ready, self.kx_ready = self.sems

            def keys(self, pe, bank):
                pe.matmul(bank[:, :], self.w["wk"], self.src[:, :], start=True, stop=True).then_inc(self.k_done, 1)

            def values(self, pe, half, bank):
                for b in range(4):
                    at = (4 * half + b) * SEQ
                    for h2 in range(2):
                        m = pe.matmul(bank[64 * h2:64 * h2 + 64, b * P:(b + 1) * P], self.src[:, at:at + SEQ],
                                      self.w["wv"], start=True, stop=True)
                m.then_inc(self.v_done, 1)

            def take_keys(self, act, bank):
                act.wait_ge(self.k_done, 1)
                act.activation(kT, bank[:, :], ACT.Identity,
                               bias=0.0 if self.k_bias is None else self.k_bias).then_inc(self.k_ready, 1)

            def place_values(self, dve, link, t, bank):
                dve.wait_ge(self.v_done, t // 2 + 1)
                at = (t % 2) * 256
                vv = bank[:, at:at + 256].rearrange("p (b c d) -> p c b d", b=PAIR, c=HP)
                dst = v_blocks[:, t, :, :, 0:16]

                def wide(a):
                    return a.rearrange("p (c d) -> p c d", c=HP).unsqueeze(2).to_broadcast([P, HP, PAIR, 16])
                ins = dve.tensor_tensor(dst, vv, wide(k_const["pmask"]), ALU.mult)
                if self.v_bias is not None:
                    link(ins)
                    ins = dve.tensor_tensor(dst, dst, wide(self.v_bias), ALU.add)
                ins.then_inc(self.v_ready, 1)

            def key_blocks(self, engine, t):
                engine.tensor_tensor(kx[:, 2 * t:2 * t + 2, :, :],
                                     kT[:, t * P:(t + 1) * P].rearrange("p (b k) -> p b k", k=SEQ)
                                     .unsqueeze(2).to_broadcast([P, PAIR, GROUP, SEQ]),
                                     k_const["hmask"].unsqueeze(1).unsqueeze(3).to_broadcast([P, PAIR, GROUP, SEQ]),
                                     ALU.mult).then_inc(self.kx_ready, 1)

        kx = work[:, 4096:8192].rearrange("p (b h k) -> p b h k", b=TILES * PAIR, h=GROUP)
        kT = work[:, 12288:12800]
        kv1 = KeysValues(k_x1, cT, k_x1["bk"], bv1[:, :])
        kv2 = KeysValues(k_x2, cT, None, None)
        kv3 = KeysValues(k_a3, xnT, k_a3["bk"], bv3[:, :])

        def attention(prev, turn_no, after, w, kv, kv_waits, scale_bias, neg, anyrow, finish):
            here = kv_waits is None
            qT = [work[:, 0:512], work[:, 12800:13312]]
            s_sb = [work[:, 512 + 1024 * i:1536 + 1024 * i] for i in range(2)]
            p_sb = s_sb
            pT = [work[:, 2560:3584], work[:, 8192:9216]]
            mx = small[:, 0:64].rearrange("p (t h) -> p t h", t=TILES)
            rc = small[:, 64:128].rearrange("p (t h) -> p t h", t=TILES)
            o_sb = [small[:, 128 + D * i:128 + D * (i + 1)] for i in range(2)]
            oT = [small[:, 384 + D * i:384 + D * (i + 1)] for i in range(2)]

            def body(block, q_done, q_ready, scored,
                     s_ready, p_ready, turned, pT_ready, mixed, o_ready, o_turned, oT_ready, done, taken):
                def heads(a):
                    return a.rearrange("p (h k) -> p h k", k=SEQ)

                @block.tensor
                def _(pe):
                    if not here:
                        for signal in kv_waits:
                            wait_for(pe, signal)
                    turn_pairs(pe, prev, turn_no, xn)
                    wait_for(pe, prev.all_used)
                    if kv is kv1:
                        pe.wait_ge(weights_loaded, 16 * 4)
                    pe.wait_ge(rowsT_ready, 2 * turn_no + 2)
                    pe.matmul(banks[4][:, :], w["wq"], xnT[:, :], start=True, stop=True).then_inc(q_done, 1)
                    keep_clock(pe, banks[2], FILL_BEFORE_SCORES[turn_no])
                    if here:
                        kv.keys(pe, banks[5])
                        kv.values(pe, 0, banks[6])
                        kv.values(pe, 1, banks[7])

                    def scores(t):
                        if t == 0:
                            pe.wait_ge(q_ready, 2)
                        pe.wait_ge(kv.kx_ready, t + 1)
                        if t >= 2:
                            pe.wait_ge(s_ready, t - 1)
                        for b in range(PAIR):
                            for g in range(HEADS // GROUP):
                                m = pe.matmul(banks[2 * (t % 2) + g][64 * b:64 * b + 64, :],
                                              qT[g][:, (2 * t + b) * SEQ:(2 * t + b + 1) * SEQ],
                                              kx[:, 2 * t + b, :, :], start=True, stop=True)
                        m.then_inc(scored, 1)

                    def turn(t):
                        pe.wait_ge(p_ready, t + 1)
                        if t == 0:
                            if here:
                                pe.wait_ge(kv.k_ready, 1)
                            pe.wait_ge(q_ready, 2)
                        else:
                            pe.wait_ge(pT_ready, 2 * t)
                        for c in range(8):
                            m = pe.transpose(banks[4 + c // 4][:, (c % 4) * P:(c % 4 + 1) * P],
                                             p_sb[t % 2][:, c * P:(c + 1) * P], ident)
                        m.then_inc(turned, 1)

                    def mix(t):
                        pe.wait_ge(pT_ready, 2 * t + 2)
                        if t == 0 and here:
                            pe.wait_ge(kv.v_ready, TILES)
                        if t >= 1:
                            pe.wait_ge(o_ready, 2 * t)
                        for c in range(8):
                            m = pe.matmul(banks[6][:, c * 36:(c + 1) * 36], pT[t % 2][:, c * P:(c + 1) * P],
                                          v_blocks[:, t, c, :, :], start=True, stop=True)
                        m.then_inc(mixed, 1)

                    def turn_mixed(t):
                        pe.wait_ge(o_ready, 2 * t + 2)
                        if t >= 1:
                            pe.wait_ge(taken, t)
                        pe.transpose(banks[7][:, 0:P], o_sb[t % 2], ident).then_inc(o_turned, 1)

                    def project(t):
                        pe.wait_ge(oT_ready, t + 1)
                        pe.matmul(banks[7][:, P:P + D], oT[t % 2], w["wo"], start=True, stop=True).then_inc(done, 1)

                    for step in range(-1, TILES + 3):
                        if 0 <= step - 1 < TILES:
                            turn(step - 1)
                        if 0 <= step - 3 < TILES:
                            turn_mixed(step - 3)
                        if 0 <= step - 2 < TILES:
                            mix(step - 2)
                        if 0 <= step - 3 < TILES:
                            project(step - 3)
                        if step + 1 < TILES:
                            scores(step + 1)

                @block.scalar
                def _(act):
                    take_pairs(act, turn_no)
                    act.wait_ge(q_done, 1)
                    for g in range(2):
                        act.activation(qT[g], banks[4][:, :], ACT.Identity, scale=scaled[:, 5 + g:6 + g],
                                       bias=0.0 if scale_bias is None else scale_bias[:, g:g + 1]).then_inc(q_ready, 1)
                    if here:
                        kv.take_keys(act, banks[5])

                    def exps(t):
                        act.wait_ge(s_ready, t + 1)
                        act.activation(p_sb[t % 2], s_sb[t % 2], ACT.Exp).then_inc(p_ready, 1)

                    def take_pT(t):
                        act.wait_ge(turned, t + 1)
                        if t >= 2:
                            act.wait_ge(mixed, t - 1)
                        for half in range(2):
                            act.copy(pT[t % 2][:, 512 * half:512 * half + 512],
                                     banks[4 + half][:, :]).then_inc(pT_ready, 1)

                    def take_oT(t):
                        act.wait_ge(o_turned, t + 1)
                        act.copy(oT[t % 2], banks[7][:, 0:P]).then_inc(oT_ready, 1)

                    for step in range(TILES + 3):
                        if 0 <= step - 1 < TILES:
                            take_pT(step - 1)
                        if 0 <= step - 3 < TILES:
                            take_oT(step - 3)
                        if step < TILES:
                            exps(step)

                @block.vector
                def _(dve):
                    link = dve_steps.on(dve)
                    if here:
                        dve.wait_ge(kv.k_ready, 1)
                        kv.key_blocks(dve, 0)
                        kv.key_blocks(dve, 1)
                        for t in range(TILES):
                            kv.place_values(dve, link, t, banks[6 + t // 2])

                    def shift(t):
                        dve.wait_ge(scored, t + 1)
                        if t >= 2:
                            dve.wait_ge(turned, t - 1)
                        for half in range(2):
                            s = heads(banks[2 * (t % 2) + half][:, :])
                            d = heads(s_sb[t % 2][:, 512 * half:512 * half + 512])
                            hs = slice(8 * half, 8 * half + 8)
                            if neg is not None:
                                link(dve.tensor_tensor(d, s, neg[:, t, :].unsqueeze(1).to_broadcast([P, 8, SEQ]),
                                                       ALU.add))
                                s = d
                            link(dve.tensor_reduce(mx[:, t, hs], s, AX, ALU.max))
                            ins = dve.tensor_tensor(d, s, mx[:, t, hs].unsqueeze(2).to_broadcast([P, 8, SEQ]),
                                                    ALU.subtract)
                            if half == 0:
                                link(ins)
                        ins.then_inc(s_ready, 1)

                    def normalise(t):
                        dve.wait_ge(mixed, t + 1)
                        o = banks[6][:, 0:288].rearrange("p (c b d) -> p c b d", c=HP, b=PAIR)
                        rv = rc[:, t, :].rearrange("p (c h) -> p c h", c=HP)
                        link.last_of([dve.reciprocal(rv[64 * b:64 * b + 64], o[64 * b:64 * b + 64, :, b, 16:18])
                                      for b in range(PAIR)])
                        if anyrow is not None:
                            link(dve.tensor_scalar(rc[:, t, :], rc[:, t, :], anyrow[:, t:t + 1], None, ALU.mult))
                        for b in range(PAIR):
                            r = slice(64 * b, 64 * b + 64)
                            dve.tensor_tensor(o_sb[t % 2][r].rearrange("p (c h d) -> p c h d", c=HP, h=2),
                                              o[r, :, b, 0:16].rearrange("p c (h d) -> p c h d", h=2),
                                              rv[r].unsqueeze(3).to_broadcast([SEQ, HP, 2, HD]),
                                              ALU.mult).then_inc(o_ready, 1)

                    next_rows = iter(())
                    for step in range(TILES + 3):
                        if step < TILES:
                            shift(step)
                        if step == 0 and here:
                            kv.key_blocks(dve, 2)
                            kv.key_blocks(dve, 3)
                        if 0 <= step - 2 < TILES:
                            normalise(step - 2)
                        some(next_rows, 7 if step == 5 else 99)
                        if 0 <= step - 3 < TILES:
                            dve.wait_ge(done, step - 2)
                            finish(dve, link, step - 3, banks[7][:, P:P + D]).then_inc(taken, 1)
                        if step in (4, 6):
                            dve.wait_ge(taken, step - 2)
                            next_rows = after(dve, link, (step - 4) // 2)
                            some(next_rows, 7)
                    run(next_rows)
                ends.append(Ends((s_ready, 3), (taken, 4)))
            ends = []
            stage("q_done q_ready scored s_ready p_ready turned pT_ready "
                  "mixed o_ready o_turned oT_ready done taken", body)
            return ends[0]

        def add_gated(gate, bias=None):
            def finish(dve, link, t, y):
                ins = dve.scalar_tensor_tensor(x[:, t, :], y, tg[:, gate:gate + 1], x[:, t, :], ALU.mult, ALU.add)
                if bias is None:
                    return ins
                link(ins)
                return dve.tensor_tensor(x[:, t, :], x[:, t, :], bias, ALU.add)
            return finish

        def add_to_z(dve, link, t, y):
            link(dve.tensor_tensor(xn[:, t, :], y, xn[:, t, :], ALU.add))
            return dve.tensor_tensor(xn[:, t, :], xn[:, t, :], k_a3["bo"], ALU.add)

        x_in = work[:, 9216:9728].rearrange("p (t d) -> p t d", t=TILES)
        ctok = work[:, 9728:10240].rearrange("p (t d) -> p t d", t=TILES)
        decaying = work[:, 10240:10752].rearrange("p (t d) -> p t d", t=TILES)
        part = work[:, 10752:11264].rearrange("p (t d) -> p t d", t=TILES)
        cn = work[:, 11264:11776].rearrange("p (t d) -> p t d", t=TILES)
        opening = named("x_loaded c_loaded masks_loaded c_turned c_normed cn_turned c_taken squared summed x_done")
        x_loaded, c_loaded, masks_loaded, c_turned, c_normed, cn_turned, c_taken, squared, summed, x_done = opening
        l0_loaded, weights_loaded, stored = lasting = named("l0_loaded weights_loaded stored")

        def load_block(sp, i):
            xs = args["x"].rearrange("(i t p) d -> i p t d", t=TILES, p=P)
            cs = args["ctx"].rearrange("(i t p) d -> i p t d", t=TILES, p=P)
            m2 = args["mask2"].rearrange("(i t p) k -> i p t k", t=TILES, p=P)
            m3 = args["mask3"].rearrange("(i b) k -> i b k", b=TILES * PAIR)
            sp.dma_start(x_in, xs[bass.ds(i, 1)].rearrange("a p t d -> (a p) t d")).then_inc(x_loaded, 16)
            sp.dma_start(ctok, cs[bass.ds(i, 1)].rearrange("a p t d -> (a p) t d")).then_inc(c_loaded, 16)
            sp.dma_start(mask2_words[:, :, :], m2[bass.ds(i, 1)].rearrange("a p t k -> (a p) t k"))\
                .then_inc(masks_loaded, 16)
            sp.dma_start(mask3_words[:, :, :], m3[bass.ds(i, 1)].to_broadcast([P, TILES * PAIR, SEQ // 4]))\
                .then_inc(masks_loaded, 16)

        def square_context(pool):
            pool.wait_ge(c_loaded, 16)
            pool.tensor_tensor(decaying, ctok, ctok, ALU.mult).then_inc(squared, 1)

        def turn_context(pe):
            pe.wait_ge(c_loaded, 16)
            for t in range(TILES):
                m = pe.transpose(banks[3][:, t * P:(t + 1) * P], ctok[:, t, :], ident)
            m.then_inc(c_turned, 1)

        def sum_over_time(pe):
            pe.wait_ge(squared, 1)
            for t in range(TILES):
                m = pe.matmul(banks[2][:, t * D:(t + 1) * D], k_const["decay"], decaying[:, t, :], start=True, stop=True)
            m.then_inc(summed, 1)

        def context_keys(pe):
            pe.wait_ge(c_taken, 1)
            kv1.keys(pe, banks[3])

        def context_values(pe, half):
            if half == 0:
                pe.wait_ge(x_done, 1)
            else:
                pe.wait_ge(kv1.k_ready, 1)
            kv1.values(pe, half, banks[2 + half])

        def turn_normed_context(pe):
            pe.wait_ge(c_normed, 1)
            pe.wait_ge(kv1.v_ready, 2)
            for t in range(TILES):
                m = pe.transpose(banks[2][:, t * P:(t + 1) * P], cn[:, t, :], ident)
            m.then_inc(cn_turned, 1)

        def take_context(act):
            act.wait_ge(c_turned, 1)
            act.copy(cT[:, :], banks[3][:, :]).then_inc(c_taken, 1)

        def take_normed_context(act):
            act.wait_ge(cn_turned, 1)
            act.activation(cxT[:, :, 0, :], banks[2][:, :].rearrange("p (b s) -> p b s", s=SEQ), ACT.Identity,
                           bias=k_x3["lxb"], scale=k_x3["lxg"]).then_inc(c_taken, 1)

        def open_rows(dve, link):
            dve.wait_ge(x_loaded, 16)
            yield from layer_norm(dve, link, [(x_in, xn_next, t) for t in range(TILES)])
            dve.wait_ge(summed, 1)
            link(dve.scalar_tensor_tensor(part, banks[2][:, :].rearrange("p (t d) -> p t d", t=TILES),
                                          tg[:, 0:1], xn_next[:, :, :], ALU.mult, ALU.mult))
            yield
            link(dve.tensor_tensor(x_next[:, :, :], x_in, part, ALU.add))
            dve.sem_inc(x_done, 1)
            yield
            yield from layer_norm(dve, link, [(x_next, xn_next, t) for t in range(TILES)])
            for t in (0, 1):
                kv1.place_values(dve, link, t, banks[2])
                yield
            dve.wait_ge(c_loaded, 16)
            yield from layer_norm(dve, link, [(ctok, cn, t) for t in range(TILES)])
            dve.sem_inc(c_normed, 1)
            for t in (2, 3):
                kv1.place_values(dve, link, t, banks[3])
                yield
            dve.wait_ge(masks_loaded, 32)
            link(dve.tensor_scalar(neg2[:, :, :], mask2, NEG, None, ALU.mult))
            yield
            link(dve.tensor_reduce(any2[:, :], neg2[:, :, :], AX, ALU.max))
            yield
            link(dve.tensor_scalar(any2[:, :], any2[:, :], 0.5 * NEG, None, ALU.is_gt))
            yield
            link(dve.tensor_scalar(neg3[:, :, 0, :], mask3, -NEG, NEG, ALU.mult, ALU.add))

        def finish_block(i, turn_no):
            def body(block):
                os_ = out.rearrange("(i t p) d -> i p t d", t=TILES, p=P)

                @block.sync
                def _(sp):
                    sp.wait_ge(rows_ready, 2 * 6 + 2)
                    load_block(sp, i + 1)
                    sp.wait_ge(rows_ready, 2 * turn_no + 2)
                    sp.dma_start(os_[bass.ds(i, 1)].rearrange("a p t d -> (a p) t d"), x[:, :, :]).then_inc(stored, 16)
            stage("", body)

        def ffn0(i, prev, turn_no, after):
            logits = small[:, 0:68].rearrange("p (t e) -> p t e", t=TILES)
            lg = small[:, 72:136].rearrange("p (t e) -> p t e", t=TILES)
            halves = small[:, 136:144].rearrange("p (t s) -> p t s", t=TILES)
            sig = small[:, 144:152].rearrange("p (t s) -> p t s", t=TILES)
            rest = small[:, 152:156].rearrange("p (t s) -> p t s", t=TILES)
            comb = small[:, 256:320].rearrange("p (t e) -> p t e", t=TILES)
            tmp = small[:, 320:384].rearrange("p (t e) -> p t e", t=TILES)
            sil = [work[:, 512 * i:512 * i + 512] for i in range(2)]
            hid = [work[:, 1024 + 512 * i:1536 + 512 * i] for i in range(2)]
            hidT = [work[:, 2048 + 512 * i:2560 + 512 * i] for i in range(2)]
            h_shared = work[:, 3072:3840].rearrange("p (i f) -> p i f", i=2)
            steps = [(t, g) for t in range(TILES) for g in range(5)]

            ends = []

            def body(block, rest_cleared, routed, halves_ready, sig_ready, comb_ready, up_done, sil_ready, weighted, hid_ready,
                     turned, hidT_ready, down_done, taken):
                def h_of(s):
                    return h_shared[:, (s // 5) % 2, :] if steps[s][1] == 4 else hid[s % 2]

                @block.tensor
                def _(pe):
                    turn_pairs(pe, prev, turn_no, xn_next)
                    pe.wait_ge(l0_loaded, 16)
                    pe.wait_ge(rowsT_ready, 2 * turn_no + 2)
                    for t in range(TILES):
                        m = pe.matmul(banks[6][:, t * 17:(t + 1) * 17], xnT[:, t * P:(t + 1) * P], k_l0["router"],
                                      start=True, stop=True)
                    m.then_inc(routed, 1)

                    def up(s):
                        t, g = steps[s]
                        if s >= 2:
                            pe.wait_ge(hid_ready, s - 1)
                        a, b = banks[2 * (s % 2)], banks[2 * (s % 2) + 1]
                        xt = xnT[:, t * P:(t + 1) * P]
                        if g < 4:
                            m = pe.matmul(a[:, :], xt, k_l0["gu"][:, g * 512:(g + 1) * 512], start=True, stop=True)
                        else:
                            pe.matmul(a[:, 0:352], xt, k_l0["sgu"][:, 0:352], start=True, stop=True)
                            m = pe.matmul(b[:, 0:352], xt, k_l0["sgu"][:, 352:704], start=True, stop=True)
                        m.then_inc(up_done, 1)

                    def turn(s):
                        pe.wait_ge(hid_ready, s + 1)
                        if s == 4:
                            pe.wait_ge(rest_cleared, 1)
                        if s >= 2:
                            pe.wait_ge(hidT_ready, s - 1)
                        for c in range(3 if steps[s][1] == 4 else 2):
                            m = pe.transpose(banks[4 + s % 2][:, c * P:(c + 1) * P], h_of(s)[:, c * P:(c + 1) * P],
                                             ident)
                        m.then_inc(turned, 1)

                    def down(s):
                        t, g = steps[s]
                        pe.wait_ge(hidT_ready, s + 1)
                        if g == 0 and t >= 2:
                            pe.wait_ge(taken, t - 1)
                        if s == 0:
                            pe.wait_ge(comb_ready, 1)
                        n = 3 if g == 4 else 2
                        for c in range(n):
                            m = pe.matmul(banks[6 + t % 2][:, 0:D], hidT[s % 2][:, c * P:(c + 1) * P],
                                          k_l0["down"][:, (2 * g + c) * D:(2 * g + c + 1) * D],
                                          start=(g == 0 and c == 0), stop=(g == 4 and c == 2))
                        m.then_inc(down_done, 1)

                    n = len(steps)
                    for s in range(n + 2):
                        if s < n:
                            up(s)
                        if 0 <= s - 2 < n:
                            down(s - 2)
                        if 0 <= s - 1 < n:
                            turn(s - 1)

                @block.scalar
                def _(act):
                    take_pairs(act, turn_no)
                    act.wait_ge(halves_ready, 1)
                    act.activation(sig, halves, ACT.Tanh).then_inc(sig_ready, 1)

                    def silu(s):
                        act.wait_ge(up_done, s + 1)
                        if s >= 2:
                            act.wait_ge(hid_ready, s - 1)
                        n = 352 if steps[s][1] == 4 else 256
                        act.activation(sil[s % 2][:, 0:n], banks[2 * (s % 2)][:, 0:n], ACT.Silu).then_inc(sil_ready, 1)

                    def take_T(s):
                        act.wait_ge(turned, s + 1)
                        if s >= 2:
                            act.wait_ge(down_done, s - 1)
                        n = 384 if steps[s][1] == 4 else 256
                        act.copy(hidT[s % 2][:, 0:n], banks[4 + s % 2][:, 0:n]).then_inc(hidT_ready, 1)

                    for s in range(len(steps) + 1):
                        if s < len(steps):
                            silu(s)
                        if s >= 1:
                            take_T(s - 1)

                @block.gpsimd
                def _(pool):
                    pool.memset(h_shared[:, :, 352:384], 0.0).then_inc(rest_cleared, 1)
                    pool.wait_ge(comb_ready, 1)
                    for s, (t, g) in enumerate(steps):
                        if g < 4:
                            pool.wait_ge(sil_ready, s + 1)
                            q = sil[s % 2][:, 0:256].rearrange("p (e f) -> p e f", e=4)
                            c = comb[:, t, 4 * g:4 * g + 4].unsqueeze(2).to_broadcast([P, 4, 64])
                            pool.tensor_tensor(q, q, c, ALU.mult).then_inc(weighted, 1)
                        else:
                            kv1.key_blocks(pool, t)

                @block.vector
                def _(dve):
                    link = dve_steps.on(dve)
                    dve.wait_ge(stored, 16 * i + 16)
                    link(dve.tensor_copy(x[:, :, :], x_next[:, :, :]))
                    dve.sem_inc(rows_ready, 2)
                    dve.wait_ge(routed, 1)
                    link(dve.tensor_copy(logits, banks[6][:, 0:68].rearrange("p (t e) -> p t e", t=TILES)))
                    link(dve.tensor_copy(lg, logits[:, :, 0:16]))
                    best, place = top_two(dve, link, lg, 16, 160)
                    link(dve.tensor_tensor(halves[:, :, 0:1], best[:, :, 0:1], best[:, :, 1:2], ALU.subtract))
                    link(dve.tensor_scalar(halves[:, :, 0:1], halves[:, :, 0:1], 0.5, None, ALU.mult))
                    dve.tensor_scalar(halves[:, :, 1:2], logits[:, :, 16:17], 0.5, None,
                                      ALU.mult).then_inc(halves_ready, 1)
                    dve.wait_ge(sig_ready, 1)
                    link(dve.tensor_scalar(sig, sig, 0.5, 0.5, ALU.mult, ALU.add))
                    link(dve.tensor_scalar(rest, sig[:, :, 0:1], -1.0, 1.0, ALU.mult, ALU.add))
                    spread(dve, link, comb, tmp, place, sig[:, :, 0:1], rest, 16)
                    dve.sem_inc(comb_ready, 1)

                    def gate_up(s):
                        t, g = steps[s]
                        dve.wait_ge(sil_ready, s + 1)
                        if s >= 2:
                            dve.wait_ge(turned, s - 1)
                        a, b = banks[2 * (s % 2)], banks[2 * (s % 2) + 1]
                        if g < 4:
                            dve.wait_ge(weighted, 4 * t + g + 1)
                            dve.tensor_tensor(h_of(s)[:, 0:256], a[:, 256:512], sil[s % 2][:, 0:256],
                                              ALU.mult).then_inc(hid_ready, 1)
                        else:
                            dve.scalar_tensor_tensor(h_of(s)[:, 0:352], b[:, 0:352], sig[:, t, 1:2],
                                                     sil[s % 2][:, 0:352], ALU.mult, ALU.mult).then_inc(hid_ready, 1)

                    n = len(steps)
                    next_rows = iter(())
                    for s in range(n + 2):
                        if s < n:
                            gate_up(s)
                            some(next_rows, 4)
                        if s >= 2 and steps[s - 2][1] == 4:
                            t = steps[s - 2][0]
                            dve.wait_ge(down_done, s - 1)
                            dve.scalar_tensor_tensor(x[:, t, :], banks[6 + t % 2][:, 0:D], tg[:, 4:5], x[:, t, :],
                                                     ALU.mult, ALU.add).then_inc(taken, 1)
                            if t % 2 == 1:
                                dve.wait_ge(taken, t + 1)
                                next_rows = after(dve, link, t // 2)
                    run(next_rows)
                ends.append(Ends((hid_ready, len(steps) - 1), (taken, 4)))
            stage("cleared routed halves sig comb up sil weighted hid turned hidT down taken", body)
            return ends[0]

        def ffn1(prev, turn_no, after):
            lg = small[:, 72:104].rearrange("p (t e) -> p t e", t=TILES)
            half = small[:, 136:140].rearrange("p (t s) -> p t s", t=TILES)
            sig = small[:, 144:148].rearrange("p (t s) -> p t s", t=TILES)
            rest = small[:, 152:156].rearrange("p (t s) -> p t s", t=TILES)
            comb = small[:, 256:288].rearrange("p (t e) -> p t e", t=TILES)
            tmp = small[:, 288:320].rearrange("p (t e) -> p t e", t=TILES)
            comb_e = small[:, 320:352].rearrange("p (e t) -> p e t", t=TILES)
            combT = small[0:8, 384:896]
            sums = small[:, 352:360].rearrange("p (t s) -> p t s", t=TILES)
            vs, rs, t4 = small[:, 952:960], small[:, 960:968], small[:, 968:972]
            stats = small[:, 896:920].rearrange("p (t s) -> p t s", t=TILES)
            mv = small[:, 920:928].rearrange("p (t s) -> p t s", t=TILES)
            r2, u4 = small[:, 932:936], small[:, 936:944]
            hT = [work[:, 2048 * i:2048 * i + 2048].rearrange("p (c n) -> p c n", c=4) for i in range(2)]
            sq = [work[:, 4096 + 2048 * i:6144 + 2048 * i].rearrange("p (c n) -> p c n", c=4) for i in range(2)]
            y = [work[:, 8192 + 512 * i:8704 + 512 * i].rearrange("p (t d) -> p t d", t=TILES) for i in range(2)]
            z = [work[:, 9216 + 512 * i:9728 + 512 * i].rearrange("p (t d) -> p t d", t=TILES) for i in range(2)]
            acc = work[:, 10240:10752].rearrange("p (t d) -> p t d", t=TILES)

            ends = []

            def body(block, x_done, routed, half_ready, sig_ready, comb_ready, up_done, hT_ready, squares_summed,
                     squared, down_done, y_raw, z_ready, added, combT_done, combT_ready, last_done, pool_link):
                @block.tensor
                def _(pe):
                    turn_pairs(pe, prev, turn_no, xn)
                    wait_for(pe, prev.all_used)
                    pe.wait_ge(rowsT_ready, 2 * turn_no + 2)
                    for t in range(TILES):
                        m = pe.matmul(banks[3][:, t * 8:(t + 1) * 8], xnT[:, t * P:(t + 1) * P], k_f1["wr"],
                                      start=True, stop=True)
                    m.then_inc(routed, 1)

                    def up(e):
                        for c in range(4):
                            n = 4 * e + c
                            if n >= 3:
                                pe.wait_ge(hT_ready, n - 2)
                            pe.matmul(banks[n % 3][:, :], k_f1["w1"][:, e * 512 + c * P:e * 512 + (c + 1) * P], xnT[:, :],
                                      start=True, stop=True).then_inc(up_done, 1)

                    def down(e):
                        pe.wait_ge(hT_ready, 4 * e + 4)
                        if e >= 2:
                            pe.wait_ge(y_raw, e - 1)

                        def zb(t):
                            return banks[4 + 2 * (e % 2) + t // 2][:, (t % 2) * 130:(t % 2) * 130 + 130]
                        for t in range(TILES):
                            for c in range(4):
                                pe.matmul(zb(t)[:, 0:129], hT[e % 2][:, c, t * P:(t + 1) * P], w_f1d[:, c, e, :],
                                          start=(c == 0), stop=(c == 3))
                        pe.wait_ge(squares_summed, e + 1)
                        for t in range(TILES):
                            m = pe.matmul(zb(t)[:, 129:130], sq[e % 2][:, 0, t * P:(t + 1) * P], ones[:, 0:1],
                                          start=True, stop=True)
                        m.then_inc(down_done, 1)

                    for e in range(9):
                        if e < 8:
                            up(e)
                        if e >= 1:
                            down(e - 1)
                    pe.wait_ge(hT_ready, 32)
                    kv2.keys(pe, banks[0])
                    pe.wait_ge(comb_ready, 1)
                    for t in range(TILES):
                        m = pe.transpose(banks[3][0:8, t * P:(t + 1) * P], comb[:, t, :], ident)
                    m.then_inc(combT_done, 1)
                    kv2.values(pe, 0, banks[1])
                    pe.wait_ge(combT_ready, 1)
                    for t in range(TILES):
                        m = pe.matmul(banks[3][:, t * D:(t + 1) * D], combT[:, t * P:(t + 1) * P], w_f1b[:, :],
                                      start=True, stop=True)
                    m.then_inc(last_done, 1)
                    kv2.values(pe, 1, banks[2])

                @block.scalar
                def _(act):
                    take_pairs(act, turn_no)
                    for e in range(8):
                        if e == 1:
                            act.wait_ge(half_ready, 1)
                            act.activation(sig, half, ACT.Tanh).then_inc(sig_ready, 1)
                        for c in range(4):
                            n = 4 * e + c
                            act.wait_ge(up_done, n + 1)
                            if e >= 2 and c == 0:
                                act.wait_ge(down_done, e - 1)
                            act.activation(hT[e % 2][:, c, :], banks[n % 3][:, :], ACT.Relu,
                                           bias=k_f1["b1"][:, n:n + 1]).then_inc(hT_ready, 1)
                        act.wait_ge(hT_ready, 4 * e + 4)
                        act.activation(sq[e % 2], hT[e % 2], ACT.Square).then_inc(squared, 1)
                    kv2.take_keys(act, banks[0])
                    act.wait_ge(combT_done, 1)
                    act.copy(combT, banks[3][0:8, :]).then_inc(combT_ready, 1)

                @block.gpsimd
                def _(pool):
                    link = Chain(pool_link).on(pool)
                    pool.wait_ge(rows_ready, 2 * turn_no + 2)
                    link(pool.memset(acc, 0.0))
                    for e in range(10):
                        if e < 8:
                            pool.wait_ge(squared, e + 1)
                            link(pool.tensor_tensor(sq[e % 2][:, 0:2, :], sq[e % 2][:, 0:2, :], sq[e % 2][:, 2:4, :],
                                                    ALU.add))
                            pool.tensor_tensor(sq[e % 2][:, 0, :], sq[e % 2][:, 0, :], sq[e % 2][:, 1, :],
                                               ALU.add).then_inc(squares_summed, 1)
                        if e >= 2:
                            q = e - 2
                            pool.wait_ge(z_ready, q + 1)
                            g2 = k_f1["g2"][:, q * D:(q + 1) * D].unsqueeze(1).to_broadcast([P, TILES, D])
                            link(pool.tensor_tensor(z[q % 2], z[q % 2], g2, ALU.mult))
                            ins = pool.tensor_tensor(acc, acc, z[q % 2], ALU.add)
                            ins.then_inc(added, 1)
                            pool.wait_ge(added, q + 1)
                        if e >= 8:
                            pool.wait_ge(down_done, 8)
                            pool.wait_ge(kv2.k_ready, 1)
                            for t in pair_tiles(e - 8):
                                kv2.key_blocks(pool, t)

                @block.vector
                def _(dve):
                    link = dve_steps.on(dve)
                    dve.wait_ge(routed, 1)
                    link(dve.tensor_tensor(lg, banks[3][:, 0:32].rearrange("p (t e) -> p t e", t=TILES),
                                           k_f1["br"].unsqueeze(1).to_broadcast([P, TILES, 8]), ALU.add))
                    best, place = top_two(dve, link, lg, 8, 160)
                    link(dve.tensor_tensor(half, best[:, :, 0:1], best[:, :, 1:2], ALU.subtract))
                    dve.tensor_scalar(half, half, 0.5, None, ALU.mult).then_inc(half_ready, 1)
                    link(dve.memset(vs, 1.0))

                    def sums_of(e):
                        dve.wait_ge(down_done, e + 1)
                        link.last_of([dve.tensor_scalar(sums[:, 2 * j:2 * j + 2, :], zs(e, j)[:, :, 128:130], 1.0 / 512,
                                                        None, ALU.mult) for j in range(2)])
                        link(dve.tensor_tensor(t4, sums[:, :, 0], sums[:, :, 0], ALU.mult))
                        link(dve.tensor_tensor(vs[:, 0:4], sums[:, :, 1], t4, ALU.subtract))
                        link(dve.tensor_scalar(vs[:, 0:4], vs[:, 0:4], 0.0, LN_EPS, ALU.max, ALU.add))

                    def zs(e, j):
                        return banks[4 + 2 * (e % 2) + j][:, 0:260].rearrange("p (t d) -> p t d", t=2)

                    def second_norm(e):
                        link(dve.tensor_tensor(r2, rs[:, 4:8], comb_e[:, e, :], ALU.mult))
                        if e >= 2:
                            dve.wait_ge(added, e - 1)
                        for t in range(TILES):
                            ins = dve.tensor_scalar(z[e % 2][:, t, :], y[e % 2][:, t, :], mv[:, t, 0:1], r2[:, t:t + 1],
                                                    ALU.subtract, ALU.mult)
                        ins.then_inc(z_ready, 1)

                    def first_norm(e):
                        if e >= 2:
                            dve.wait_ge(z_ready, e - 1)
                        for t in range(TILES):
                            ins = dve.scalar_tensor_tensor(y[e % 2][:, t, :], zs(e, t // 2)[:, t % 2, 0:D], rs[:, t:t + 1],
                                                           expert_bias[:, e, :], ALU.mult, ALU.add)
                        ins.then_inc(y_raw, 1)
                        dve.wait_ge(y_raw, e + 1)
                        link(dve.tensor_scalar(y[e % 2], y[e % 2], 0.0, None, ALU.max))
                        link.last_of([dve.bn_stats(stats[:, t, :], y[e % 2][:, t, :]) for t in range(TILES)])
                        if e >= 1:
                            dve.wait_ge(z_ready, e)
                        link.last_of([dve.bn_aggr(mv[:, t, :], stats[:, t, :]) for t in range(TILES)])
                        link(dve.tensor_scalar(vs[:, 4:8], mv[:, :, 1], LN_EPS, None, ALU.add))

                    def gates_of_tiles():
                        dve.wait_ge(sig_ready, 1)
                        link(dve.tensor_scalar(sig, sig, 0.5, 0.5, ALU.mult, ALU.add))
                        link(dve.tensor_scalar(rest, sig, -1.0, 1.0, ALU.mult, ALU.add))
                        spread(dve, link, comb, tmp, place, sig, rest, 8)
                        link(dve.tensor_copy(comb_e, comb.rearrange("p t e -> p e t")))
                        dve.sem_inc(comb_ready, 1)

                    for e in range(10):
                        if e == 1:
                            gates_of_tiles()
                        if 1 <= e < 9:
                            sums_of(e - 1)
                        if e >= 1:
                            run(rsqrt(dve, link, rs, vs, u4))
                        if e >= 2:
                            second_norm(e - 2)
                        if 1 <= e < 9:
                            first_norm(e - 1)
                    for t in range(TILES):
                        kv2.place_values(dve, link, t, banks[1 + t // 2])
                    dve.wait_ge(last_done, 1)
                    dve.wait_ge(added, 8)
                    link(dve.tensor_tensor(acc, acc, banks[3][:, :].rearrange("p (t d) -> p t d", t=TILES), ALU.add))
                    link(dve.scalar_tensor_tensor(x[:, :, :], acc, tg[:, 5:6], x[:, :, :], ALU.mult, ALU.add))
                    dve.sem_inc(x_done, 1)
                    after(dve, link)
                ends.append(Ends((hT_ready, 32), (x_done, 1)))
            stage("x_done routed half sig comb up hT sq_sum squared down y_raw z_ready added combTd combTr last plink", body)
            return ends[0]

        def ffn2(prev, turn_no, after):
            lg = small[:, 72:104].rearrange("p (t e) -> p t e", t=TILES)
            ex = small[:, 104:120].rearrange("p (t e) -> p t e", t=TILES)
            den = small[:, 120:124].rearrange("p (t s) -> p t s", t=TILES)
            top = small[:, 124:132].rearrange("p (t s) -> p t s", t=TILES)
            comb = small[:, 256:272].rearrange("p (t e) -> p t e", t=TILES)
            tmp = small[:, 272:288].rearrange("p (t e) -> p t e", t=TILES)
            r = [[work[:, 2048 * i + 512 * e:2048 * i + 512 * e + 512] for e in range(4)] for i in range(2)]
            gT = [work[:, 4096 + 512 * i:4608 + 512 * i] for i in range(2)]

            ends = []

            def body(block, routed, shifted, exp_ready, comb_ready, up_done, r_ready, pair_ready,
                     sum_ready, turned, gT_ready, down_done, taken):
                @block.tensor
                def _(pe):
                    turn_pairs(pe, prev, turn_no, xn)
                    wait_for(pe, prev.all_used)
                    pe.wait_ge(rowsT_ready, 2 * turn_no + 2)
                    for t in range(TILES):
                        m = pe.matmul(banks[6][:, t * 4:(t + 1) * 4], xnT[:, t * P:(t + 1) * P], k_f2["wg"],
                                      start=True, stop=True)
                    m.then_inc(routed, 1)

                    def up(t):
                        for e in range(4):
                            n = 4 * t + e
                            if n >= 4:
                                pe.wait_ge(r_ready, n - 3)
                            pe.matmul(banks[e][:, :], xnT[:, t * P:(t + 1) * P], w_f2e[:, e, :],
                                      start=True, stop=True).then_inc(up_done, 1)

                    def turn(t):
                        pe.wait_ge(sum_ready, t + 1)
                        if t >= 2:
                            pe.wait_ge(gT_ready, t - 1)
                        for c in range(4):
                            m = pe.transpose(banks[4 + t % 2][:, c * P:(c + 1) * P], r[t % 2][0][:, c * P:(c + 1) * P],
                                             ident)
                        m.then_inc(turned, 1)
                        pe.wait_ge(gT_ready, t + 1)
                        if t >= 2:
                            pe.wait_ge(taken, t - 1)
                        for c in range(4):
                            m = pe.matmul(banks[6 + t % 2][:, 0:D], gT[t % 2][:, c * P:(c + 1) * P],
                                          k_f2["wo"][:, c * D:(c + 1) * D], start=(c == 0), stop=(c == 3))
                        m.then_inc(down_done, 1)

                    for t in range(TILES + 1):
                        if t < TILES:
                            up(t)
                        if t == 0:
                            pe.wait_ge(comb_ready, 1)
                        if t >= 1:
                            turn(t - 1)

                @block.scalar
                def _(act):
                    take_pairs(act, turn_no)
                    act.wait_ge(shifted, 1)
                    act.activation(ex, lg[:, :, 0:4], ACT.Exp).then_inc(exp_ready, 1)
                    act.wait_ge(comb_ready, 1)
                    for t in range(TILES + 1):
                        if t < TILES:
                            for e in range(4):
                                act.wait_ge(up_done, 4 * t + e + 1)
                                if t >= 2 and e == 0:
                                    act.wait_ge(turned, t - 1)
                                act.activation(r[t % 2][e], banks[e][:, :], ACT.Relu,
                                               scale=comb[:, t, e:e + 1]).then_inc(r_ready, 1)
                        if t >= 1:
                            act.wait_ge(turned, t)
                            if t >= 3:
                                act.wait_ge(down_done, t - 2)
                            act.copy(gT[(t - 1) % 2], banks[4 + (t - 1) % 2][:, :]).then_inc(gT_ready, 1)

                @block.gpsimd
                def _(pool):
                    for t in range(TILES):
                        pool.wait_ge(r_ready, 4 * t + 4)
                        pool.tensor_tensor(r[t % 2][2], r[t % 2][2], r[t % 2][3], ALU.add).then_inc(pair_ready, 1)

                @block.vector
                def _(dve):
                    link = dve_steps.on(dve)
                    link(dve.memset(lg, NEG))
                    dve.wait_ge(routed, 1)
                    link(dve.tensor_tensor(lg[:, :, 0:4], banks[6][:, 0:16].rearrange("p (t e) -> p t e", t=TILES),
                                           k_f2["bg"].unsqueeze(1).to_broadcast([P, TILES, 4]), ALU.add))
                    best, place = top_two(dve, link, lg, 8, 160)
                    link(dve.tensor_tensor(lg[:, :, 0:4], lg[:, :, 0:4], best[:, :, 0:1].to_broadcast([P, TILES, 4]),
                                           ALU.subtract))
                    dve.sem_inc(shifted, 1)
                    dve.wait_ge(exp_ready, 1)
                    link(dve.tensor_reduce(den[:, :, 0], ex, AX, ALU.add))
                    link(dve.reciprocal(den, den))
                    link(dve.tensor_tensor(ex, ex, den.to_broadcast([P, TILES, 4]), ALU.mult))
                    link.last_of([dve.memset(top, 1.0)])
                    spread(dve, link, comb, tmp, place, top[:, :, 0:1], top[:, :, 1:2], 4)
                    link(dve.tensor_tensor(comb, comb, ex, ALU.mult))
                    dve.sem_inc(comb_ready, 1)
                    next_rows = iter(())
                    for t in range(TILES + 1):
                        some(next_rows, 8)
                        if t < TILES:
                            dve.wait_ge(r_ready, 4 * t + 2)
                            link(dve.tensor_tensor(r[t % 2][0], r[t % 2][0], r[t % 2][1], ALU.add))
                            some(next_rows, 10)
                            dve.wait_ge(pair_ready, t + 1)
                            dve.tensor_tensor(r[t % 2][0], r[t % 2][0], r[t % 2][2], ALU.add).then_inc(sum_ready, 1)
                        if t >= 1:
                            dve.wait_ge(down_done, t)
                            dve.scalar_tensor_tensor(x[:, t - 1, :], banks[6 + (t - 1) % 2][:, 0:D], tg[:, 6:7],
                                                     x[:, t - 1, :], ALU.mult, ALU.add).then_inc(taken, 1)
                            if t % 2 == 0:
                                run(next_rows)
                                dve.wait_ge(taken, t)
                                next_rows = after(dve, link, t // 2 - 1)
                    run(next_rows)
                ends.append(Ends((r_ready, 14), (taken, 4)))
            stage("routed shifted expd comb up r pair sum turned gT down taken", body)
            return ends[0]

        def perceiver(prev, turn_no, after):
            ssq = small[:, 0:48]
            negmax = [small[:, 64 + 8 * i:72 + 8 * i] for i in range(2)]
            den = [small[:, 80 + 8 * i:88 + 8 * i] for i in range(2)]
            rden = [small[:, 96 + 8 * i:104 + 8 * i] for i in range(2)]
            q_ssq, q_rs, half_power = small[:, 128:144], small[:, 144:160], small[:, 160:176]
            oT = [work[:, 1024 * i:1024 * i + 1024].rearrange("p (c b q) -> p c b q", c=8, b=2) for i in range(2)]
            ksq = work[:, 2048:3072]
            k_rows = work[:, 3072:4096]
            kT = work[:, 4096:5120]
            v = [work[:, 5120 + 1024 * i:6144 + 1024 * i] for i in range(3)]
            s_sb = [work[:, 8192 + 1024 * i:9216 + 1024 * i] for i in range(2)]
            pT = work[:, 10240:11264]
            q_rows = work[:, 11264:12288]
            q_sq = work[:, 12288:13312]
            n = TILES * PAIR

            ends = []

            def body(block, latents_ready, pool_link, q_done, q_copied, q_squared, q_summed, q_normed, q_turned, q_ready, k_done,
                     k_squared, k_normed, k_turned, kT_ready, v_done, v_ready, scored, scores_taken, mx_ready, p_ready, r_ready,
                     p_scaled, p_turned, pT_ready, mixed, oT_ready, done, taken):
                @block.tensor
                def _(pe):
                    def queries(t):
                        if t == 1:
                            pe.wait_ge(v_ready, 4)
                        elif t >= 2:
                            pe.wait_ge(pT_ready, 2 * (2 * t - 2))
                        for i in range(2):
                            m = pe.matmul(banks[2 + i][:, :], xnT[:, t * P:(t + 1) * P],
                                          k_x3["wq"][:, 512 * i:512 * i + 512], start=True, stop=True)
                        m.then_inc(q_done, 1)

                    def values(b):
                        if b >= 3:
                            pe.wait_ge(pT_ready, 2 * (b - 2))
                        elif b == 1:
                            pe.wait_ge(v_ready, 2)
                        if b % 2 == 0:
                            pe.wait_ge(q_copied, b // 2 + 1)
                        for i in range(2):
                            m = pe.matmul(banks[2 + i][:, :], cxT[:, b, :, :],
                                          k_x3["wkv"][:, 1024 + 512 * i:1536 + 512 * i], start=True, stop=True)
                        m.then_inc(v_done, 1)

                    def keys(b):
                        if b >= 1:
                            pe.wait_ge(k_normed, b)
                        for i in range(2):
                            m = pe.matmul(banks[i][:, :], cxT[:, b, :, :], k_x3["wkv"][:, 512 * i:512 * i + 512],
                                          start=True, stop=True)
                        m.then_inc(k_done, 1)

                    def turn_keys(b):
                        pe.wait_ge(k_normed, b + 1)
                        if b >= 1:
                            pe.wait_ge(scores_taken, 2 * b)
                        for c in range(8):
                            m = pe.transpose(banks[4 + c // 4][:, (c % 4) * P:(c % 4 + 1) * P],
                                             k_rows[:, c * P:(c + 1) * P], ident)
                        m.then_inc(k_turned, 1)

                    def turn_queries(t):
                        pe.wait_ge(q_normed, t + 1)
                        pe.wait_ge(kT_ready, 2 * (2 * t) + 2)
                        for c in range(8):
                            m = pe.transpose(banks[4 + c // 4][:, (c % 4) * P:(c % 4 + 1) * P],
                                             q_rows[:, c * P:(c + 1) * P], ident)
                        m.then_inc(q_turned, 1)

                    def scores(b):
                        pe.wait_ge(kT_ready, 2 * b + 2)
                        pe.wait_ge(q_ready, 2 * (b // 2) + 2)
                        for c in range(8):
                            m = pe.matmul(banks[4 + c // 4][:, (c % 4) * P:(c % 4 + 1) * P],
                                          q_blocks[:, b % 2, c, :, :], kT[:, c * P:(c + 1) * P],
                                          start=True, stop=True)
                        m.then_inc(scored, 1)

                    def turn_probs(b):
                        pe.wait_ge(p_scaled, b + 1)
                        pe.wait_ge(v_ready, 2 * min(b + 2, n - 1) + 2)
                        if b >= n - 2 and b >= 1:
                            pe.wait_ge(pT_ready, 2 * b)
                        for c in range(8):
                            m = pe.transpose(banks[2 + c // 4][:, (c % 4) * P:(c % 4 + 1) * P],
                                             s_sb[b % 2][:, c * P:(c + 1) * P], ident)
                        m.then_inc(p_turned, 1)

                    def mix(b):
                        pe.wait_ge(pT_ready, 2 * b + 2)
                        if b >= 1:
                            pe.wait_ge(oT_ready, 4 * b)
                        for c in (4, 5, 6, 7, 0, 1, 2, 3):
                            if c == 0 and b >= 2 and b % 2 == 0:
                                pe.wait_ge(taken, b // 2)
                            m = pe.matmul(banks[6 + c // 4][:, (c % 4) * P:(c % 4 + 1) * P], v[b % 3][:, c * P:(c + 1) * P],
                                          pT[:, c * P:(c + 1) * P], start=True, stop=True)
                        m.then_inc(mixed, 1)

                    def project(t):
                        pe.wait_ge(oT_ready, 8 * t + 8)
                        for c in range(8):
                            m = pe.matmul(banks[6][:, 0:D], oT[t % 2][:, c, :, :], k_x3["wout"][:, c * D:(c + 1) * D],
                                          start=(c == 0), stop=(c == 7))
                        m.then_inc(done, 1)

                    turn_pairs(pe, prev, turn_no, xn)
                    wait_for(pe, prev.all_used)
                    pe.wait_ge(rowsT_ready, 2 * turn_no + 2)
                    pe.wait_ge(latents_ready, 2)
                    for i in range(-1, n + 3):
                        if i + 1 < n:
                            keys(i + 1)
                        if 0 <= i - 2 < n - 2:
                            turn_probs(i - 2)
                        if 0 <= i < n:
                            turn_keys(i)
                        if i % 2 == 1 and i + 1 < n:
                            queries((i + 1) // 2)
                        if 0 <= i - 2 < n:
                            mix(i - 2)
                        if i % 2 == 0 and i < n:
                            turn_queries(i // 2)
                        if i + 1 < n:
                            values(i + 1)
                        if 0 <= i < n:
                            scores(i)
                        if n - 2 <= i - 1 < n:
                            turn_probs(i - 1)
                        if i >= 3 and i % 2 == 1:
                            project((i - 3) // 2)

                @block.scalar
                def _(act):
                    for pair in range(2):
                        act.wait_ge(rows_turned, 2 * turn_no + pair + 1)
                        half = banks[pair][:, 0:2 * P]
                        act.activation(xnT[:, pair * 2 * P:(pair + 1) * 2 * P], half, ACT.Identity,
                                       bias=k_x3["llb"], scale=k_x3["llg"]).then_inc(rowsT_ready, 1)
                        act.activation(cxT[:, 4 * pair:4 * pair + 4, 1, :], half.rearrange("p (b s) -> p b s", s=SEQ),
                                       ACT.Identity, bias=k_x3["llb"], scale=k_x3["llg"]).then_inc(latents_ready, 1)
                    def take_keys(b):
                        act.wait_ge(k_turned, b + 1)
                        if b >= 1:
                            act.wait_ge(scored, b)
                        for j in range(2):
                            act.activation(kT[:, 512 * j:512 * j + 512], banks[4 + j][:, :], ACT.Identity,
                                           scale=scaled[:, 4:5]).then_inc(kT_ready, 1)

                    def exps(b, half):
                        act.wait_ge(mx_ready, b + 1)
                        if b >= 2:
                            act.wait_ge(r_ready, b - 1)
                        for c in range(4 * half, 4 * half + 4):
                            ins = act.activation(s_sb[b % 2][:, c * P:(c + 1) * P], s_sb[b % 2][:, c * P:(c + 1) * P],
                                                 ACT.Exp, bias=negmax[b % 2][:, c:c + 1],
                                                 accum_out=den[b % 2][:, c:c + 1])
                        ins.then_inc(p_ready, 1)

                    def square_keys(b):
                        act.wait_ge(k_done, b + 1)
                        for j in range(2):
                            ins = act.activation(ksq[:, 512 * j:512 * j + 512], banks[j][:, :], ACT.Square)
                        ins.then_inc(k_squared, 1)

                    def take_queries(t):
                        act.wait_ge(q_done, t + 1)
                        if t >= 1:
                            act.wait_ge(q_turned, t)
                        for j in range(2):
                            ins = act.copy(q_rows[:, 512 * j:512 * j + 512], banks[2 + j][:, :])
                        ins.then_inc(q_copied, 1)

                    def place_queries(t):
                        act.wait_ge(q_turned, t + 1)
                        for h2 in range(2):
                            r = slice(64 * h2, 64 * h2 + 64)
                            for j in range(2):
                                ins = act.copy(q_blocks[r, :, 4 * j:4 * j + 4, h2, :].rearrange("p b c q -> p c b q"),
                                               banks[4 + j][r, :].rearrange("p (c b q) -> p c b q", c=4, b=2))
                            ins.then_inc(q_ready, 1)

                    def take_mixed(b):
                        act.wait_ge(mixed, b + 1)
                        if b % 2 == 0 and b >= 4:
                            act.wait_ge(done, (b - 4) // 2 + 1)
                        for h2 in range(2):
                            r = slice(64 * h2, 64 * h2 + 64)
                            for j in (1, 0):
                                act.copy(oT[(b // 2) % 2][r, 4 * j:4 * j + 4, b % 2, :],
                                         banks[6 + j][r, :].rearrange("p (c h q) -> p c h q", c=4, h=2)[:, :, h2, :])\
                                    .then_inc(oT_ready, 1)

                    def take_values(b):
                        act.wait_ge(v_done, b + 1)
                        if b >= 3:
                            act.wait_ge(mixed, b - 2)
                        for j in range(2):
                            act.copy(v[b % 3][:, 512 * j:512 * j + 512], banks[2 + j][:, :]).then_inc(v_ready, 1)

                    def take_probs(b):
                        act.wait_ge(p_turned, b + 1)
                        if b >= 1:
                            act.wait_ge(mixed, b)
                        for j in range(2):
                            act.copy(pT[:, 512 * j:512 * j + 512], banks[2 + j][:, :]).then_inc(pT_ready, 1)

                    for i in range(-1, n + 3):
                        if i + 1 < n:
                            square_keys(i + 1)
                        if 0 <= i - 2 < n - 2:
                            take_probs(i - 2)
                        if 0 <= i < n:
                            take_keys(i)
                        if 0 <= i - 1 < n:
                            exps(i - 1, 0)
                        if i % 2 == 1 and i + 1 < n:
                            take_queries((i + 1) // 2)
                        if i % 2 == 0 and i < n:
                            place_queries(i // 2)
                        if 0 <= i - 1 < n:
                            exps(i - 1, 1)
                        if 0 <= i - 2 < n:
                            take_mixed(i - 2)
                        if i + 1 < n:
                            take_values(i + 1)
                        if n - 2 <= i - 1 < n:
                            take_probs(i - 1)

                @block.gpsimd
                def _(pool):
                    link = Chain(pool_link).on(pool)
                    pool.wait_ge(rowsT_ready, 2 * turn_no + 2)
                    link(pool.memset(half_power, -0.5))

                    def scale_probs(b):
                        pool.wait_ge(r_ready, b + 1)
                        s3 = s_sb[b % 2].rearrange("p (c j) -> p c j", c=8)
                        pool.tensor_tensor(s3, s3, rden[b % 2].unsqueeze(2).to_broadcast([P, 8, P]),
                                           ALU.mult).then_inc(p_scaled, 1)

                    def square_queries(t):
                        pool.wait_ge(q_copied, t + 1)
                        if t >= 1:
                            pool.wait_ge(q_normed, t)
                        pool.tensor_tensor(q_sq, q_rows, q_rows, ALU.mult).then_inc(q_squared, 1)

                    def scale_queries(t):
                        pool.wait_ge(q_summed, t + 1)
                        link(pool.tensor_tensor(q_rs, q_ssq, half_power, ALU.pow))
                        q3 = q_rows.rearrange("p (h d) -> p h d", d=XD)
                        pool.tensor_tensor(q3, q3, q_rs.unsqueeze(2).to_broadcast([P, HEADS, XD]),
                                           ALU.mult).then_inc(q_normed, 1)

                    for i in range(-1, n + 1):
                        if i % 2 == 1 and i + 1 < n:
                            square_queries((i + 1) // 2)
                        if i >= 1:
                            scale_probs(i - 1)
                        if i % 2 == 1 and i + 1 < n:
                            scale_queries((i + 1) // 2)

                @block.vector
                def _(dve):
                    link = dve_steps.on(dve)

                    def norms(sq):
                        link(dve.tensor_reduce(ssq[:, 0:16], sq.rearrange("p (h d) -> p h d", d=XD), AX, ALU.add))
                        link(dve.tensor_scalar(ssq[:, 0:16], ssq[:, 0:16], 1.0 / XD, 1e-16, ALU.mult, ALU.max))
                        run(rsqrt(dve, link, ssq[:, 16:32], ssq[:, 0:16], ssq[:, 32:48]))

                    def scale_rows(dst, src, j):
                        return dve.tensor_tensor(dst[:, 512 * j:512 * j + 512].rearrange("p (h d) -> p h d", d=XD),
                                                 src.rearrange("p (h d) -> p h d", d=XD),
                                                 ssq[:, 16 + 8 * j:24 + 8 * j].unsqueeze(2).to_broadcast([P, 8, XD]),
                                                 ALU.mult)

                    def norm_keys(b):
                        dve.wait_ge(k_squared, b + 1)
                        norms(ksq)

                    def scale_keys(b):
                        if b >= 1:
                            dve.wait_ge(k_turned, b)
                        link.last_of([scale_rows(k_rows, banks[j][:, :], j) for j in range(2)])
                        dve.sem_inc(k_normed, 1)

                    def sum_queries(t):
                        dve.wait_ge(q_squared, t + 1)
                        link(dve.tensor_reduce(q_ssq, q_sq.rearrange("p (h d) -> p h d", d=XD), AX, ALU.add))
                        dve.tensor_scalar(q_ssq, q_ssq, 1.0 / XD, 1e-16, ALU.mult, ALU.max).then_inc(q_summed, 1)

                    def invert_sums(b):
                        dve.wait_ge(p_ready, 2 * b + 2)
                        if b >= 2:
                            dve.wait_ge(p_scaled, b - 1)
                        dve.reciprocal(rden[b % 2], den[b % 2]).then_inc(r_ready, 1)

                    def mask_and_max(b):
                        dve.wait_ge(scored, b + 1)
                        if b >= 2:
                            dve.wait_ge(p_turned, b - 1)
                        s3 = s_sb[b % 2].rearrange("p (c j) -> p c j", c=8)
                        nb = neg3[:, b, :, :].rearrange("p a s -> p (a s)")
                        for j in range(2):
                            dve.tensor_tensor(s3[:, 4 * j:4 * j + 4, :],
                                              banks[4 + j][:, :].rearrange("p (c j) -> p c j", c=4),
                                              nb.unsqueeze(1).to_broadcast([P, 4, P]), ALU.add).then_inc(scores_taken, 1)
                        dve.wait_ge(scores_taken, 2 * b + 2)
                        dve.tensor_reduce(negmax[b % 2], s3, AX, ALU.max, negate=True).then_inc(mx_ready, 1)

                    for i in range(-1, n + 3):
                        if i >= 4 and i % 2 == 0:
                            t = (i - 4) // 2
                            dve.wait_ge(done, t + 1)
                            link(dve.scalar_tensor_tensor(x[:, t, :], banks[6][:, 0:D], tg[:, 3:4], x[:, t, :],
                                                          ALU.mult, ALU.add))
                            dve.tensor_tensor(x[:, t, :], x[:, t, :], bout3[:, :], ALU.add).then_inc(taken, 1)
                        if i + 1 < n:
                            norm_keys(i + 1)
                        if i + 1 < n:
                            scale_keys(i + 1)
                        if 0 <= i - 1 < n:
                            invert_sums(i - 1)
                        if i % 2 == 1 and i + 1 < n:
                            sum_queries((i + 1) // 2)
                        if 0 <= i < n:
                            mask_and_max(i)
                        if i in (6, 10):
                            dve.wait_ge(taken, (i - 4) // 2 + 1)
                            run(after(dve, link, (i - 6) // 4))
                ends.append(Ends((k_normed, 8), (taken, 4)))
            stage("latents plink q_done q_copied q_sq q_summed q_normed q_turned q_ready k_done k_sq k_normed k_turned kT_ready "
                  "v_done v_ready scored scores_taken mx_ready p_ready r_ready p_scaled p_turned pT_ready mixed oT_ready done taken",
                  body)
            return ends[0]

        def ffn3(prev, turn_no, after):
            probs = small[:, 72:104].rearrange("p (t e) -> p t e", t=TILES)
            tot = small[:, 136:140].rearrange("p (t s) -> p t s", t=TILES)
            wts = small[:, 140:148].rearrange("p (t s) -> p t s", t=TILES)
            comb = small[:, 256:288].rearrange("p (t e) -> p t e", t=TILES)
            chosen = small[:, 288:320].rearrange("p (t e) -> p t e", t=TILES)
            tmp = small[:, 320:352].rearrange("p (t e) -> p t e", t=TILES)
            ran = small[:, 352:392].rearrange("p (t e) -> p t e", t=TILES + 1)
            top = small[:, 392:400].rearrange("p (t s) -> p t s", t=TILES)
            h = [work[:, 512 * i:512 * i + 512] for i in range(2)]
            hT = [work[:, 1024 + 512 * i:1536 + 512 * i] for i in range(2)]
            g = [work[:, 2048 + 512 * i:2560 + 512 * i] for i in range(2)]
            capacity = float(int(1.25 * BATCH * SEQ * 2 / 8))
            steps = [(t, q) for t in range(TILES) for q in range(4)]

            def body(block, routed, tanh_done, chosen_ready, ranked, comb_ready, up_done, g_ready, h_ready,
                     turned, hT_ready, down_done, taken):
                @block.tensor
                def _(pe):
                    turn_pairs(pe, prev, turn_no, xn)
                    wait_for(pe, prev.all_used)
                    pe.wait_ge(rowsT_ready, 2 * turn_no + 2)
                    for t in range(TILES):
                        m = pe.matmul(banks[6][:, t * 8:(t + 1) * 8], xnT[:, t * P:(t + 1) * P], k_f3["wr"],
                                      start=True, stop=True)
                    m.then_inc(routed, 1)
                    pe.wait_ge(chosen_ready, 1)
                    for t in range(TILES):
                        pe.matmul(banks[7][:, t * 8:(t + 1) * 8], k_const["tri"], chosen[:, t, :],
                                  start=True, stop=False)
                        m = pe.matmul(banks[7][:, t * 8:(t + 1) * 8], ones[:, :], ran[:, t, :],
                                      start=False, stop=True)
                    m.then_inc(ranked, 1)

                    def up(s):
                        t, q = steps[s]
                        if s >= 2:
                            pe.wait_ge(g_ready, s - 1)
                        pe.matmul(banks[s % 2][:, :], xnT[:, t * P:(t + 1) * P], k_f3["w1"][:, q * 512:(q + 1) * 512],
                                  start=True, stop=True).then_inc(up_done, 1)

                    def turn(s):
                        pe.wait_ge(h_ready, s + 1)
                        if s >= 2:
                            pe.wait_ge(hT_ready, s - 1)
                        for c in range(4):
                            m = pe.transpose(banks[4 + s % 2][:, c * P:(c + 1) * P], h[s % 2][:, c * P:(c + 1) * P], ident)
                        m.then_inc(turned, 1)

                    def down(s):
                        t, q = steps[s]
                        pe.wait_ge(hT_ready, s + 1)
                        if s == 0:
                            pe.wait_ge(comb_ready, 1)
                        if q == 0 and t >= 2:
                            pe.wait_ge(taken, t - 1)
                        for c in range(4):
                            m = pe.matmul(banks[6 + t % 2][:, 0:D], hT[s % 2][:, c * P:(c + 1) * P],
                                          k_f3["w2"][:, (4 * q + c) * D:(4 * q + c + 1) * D],
                                          start=(q == 0 and c == 0), stop=(q == 3 and c == 3))
                        m.then_inc(down_done, 1)

                    n = len(steps)
                    for s in range(n + 2):
                        if s < n:
                            up(s)
                        if 0 <= s - 2 < n:
                            down(s - 2)
                        if 0 <= s - 1 < n:
                            turn(s - 1)
                        if s == 1:
                            turn_context(pe)
                        if s == 4:
                            sum_over_time(pe)
                        if s == 6:
                            context_keys(pe)
                        if s in (8, 11):
                            context_values(pe, (s - 8) // 3)
                        if s == n - 1:
                            turn_normed_context(pe)

                @block.gpsimd
                def _(pool):
                    square_context(pool)

                @block.scalar
                def _(act):
                    take_pairs(act, turn_no)
                    act.wait_ge(routed, 1)
                    act.activation(probs, banks[6][:, 0:32].rearrange("p (t e) -> p t e", t=TILES), ACT.Tanh,
                                   scale=0.5).then_inc(tanh_done, 1)
                    n = len(steps)
                    for s in range(n + 1):
                        if s < n:
                            act.wait_ge(up_done, s + 1)
                            if s >= 2:
                                act.wait_ge(h_ready, s - 1)
                            act.activation(g[s % 2], banks[s % 2][:, :], ACT.Gelu).then_inc(g_ready, 1)
                        if s >= 1:
                            act.wait_ge(turned, s)
                            if s >= 3:
                                act.wait_ge(down_done, s - 2)
                            act.copy(hT[(s - 1) % 2], banks[4 + (s - 1) % 2][:, :]).then_inc(hT_ready, 1)
                        if s == 2:
                            take_context(act)
                        if s == 7:
                            kv1.take_keys(act, banks[3])
                    take_normed_context(act)

                @block.vector
                def _(dve):
                    link = dve_steps.on(dve)
                    dve.wait_ge(tanh_done, 1)
                    link(dve.tensor_scalar(probs, probs, 0.5, 0.5, ALU.mult, ALU.add))
                    best, place = top_two(dve, link, probs, 8, 160)
                    link(dve.memset(top, 1.0))
                    spread(dve, link, chosen, tmp, place, top[:, :, 0:1], top[:, :, 1:2], 8)
                    link(dve.tensor_copy(ran[:, 0, :], run_mask[:, :]))
                    for t in range(TILES):
                        link(dve.tensor_tensor(ran[:, t + 1, :], ran[:, t, :], chosen[:, t, :], ALU.add))
                    dve.sem_inc(chosen_ready, 1)
                    link(dve.tensor_copy(run_mask[:, :], ran[:, TILES, :]))
                    link(dve.tensor_tensor(tot, best[:, :, 0:1], best[:, :, 1:2], ALU.add))
                    link(dve.tensor_scalar(tot, tot, 1e-6, None, ALU.add))
                    link(dve.reciprocal(tot, tot))
                    link(dve.tensor_tensor(wts, best[:, :, 0:2], tot.to_broadcast([P, TILES, 2]), ALU.mult))
                    spread(dve, link, comb, tmp, place, wts[:, :, 0:1], wts[:, :, 1:2], 8)
                    dve.wait_ge(ranked, 1)
                    link(dve.tensor_scalar(tmp, banks[7][:, 0:32].rearrange("p (t e) -> p t e", t=TILES), capacity, None,
                                           ALU.is_lt))
                    link(dve.tensor_tensor(comb, comb, tmp, ALU.mult))
                    dve.sem_inc(comb_ready, 1)
                    n = len(steps)
                    next_block, next_rows = open_rows(dve, link), iter(())
                    for s in range(n + 2):
                        if s < n:
                            t, q = steps[s]
                            dve.wait_ge(g_ready, s + 1)
                            if s >= 2:
                                dve.wait_ge(turned, s - 1)
                            for j in range(2):
                                ins = dve.tensor_scalar(h[s % 2][:, 256 * j:256 * j + 256], g[s % 2][:, 256 * j:256 * j + 256],
                                                        comb[:, t, 2 * q + j:2 * q + j + 1], None, ALU.mult)
                            ins.then_inc(h_ready, 1)
                            some(next_rows, 4)
                            some(next_block, 4 if t < 2 else 3)
                        if s >= 2 and steps[s - 2][1] == 3:
                            t = steps[s - 2][0]
                            dve.wait_ge(down_done, s - 1)
                            dve.tensor_tensor(xn[:, t, :], banks[6 + t % 2][:, 0:D], xn[:, t, :],
                                              ALU.add).then_inc(taken, 1)
                            if t % 2 == 1:
                                dve.wait_ge(taken, t + 1)
                                next_rows = after(dve, link, t // 2)
                    run(next_rows)
                    run(next_block)
            stage("routed tanh chosen ranked comb up g h turned hT down taken", body)

        def clear(sems):
            nums = sorted(s.num for s in sems)
            for a in nums:
                if a - 1 in nums:
                    continue
                b = a
                while b in nums:
                    b += 1
                nc.vector.sem_clear(range(a, b))
            nc.all_engine_barrier()

        def prepare(block, first_loaded, prep_loaded, set_up, means, evacuated, tanh_done, pool_link):
            w2_raw = w_f1d[:, :, :, 0:D]

            @block.sync
            def _(sp):
                for name, dst in (("consts", consts[:, :]), ("gates", gates[:, :]), ("x1", w_x1[:, :])):
                    sp.dma_start(dst, args[name]).then_inc(first_loaded, 16)
                load_block(sp, 0)
                for c in range(4):
                    sp.dma_start(w_f1d[:, c, :, 0:D], args["f1d"][:, c, :, :]).then_inc(prep_loaded, 16)
                for name, dst in (("lora_a", lora_a), ("lora_b", lora_b), ("b2", b2), ("wi", wi), ("x3", w_x3[:, :]),
                                  ("a3", w_a3[:, :]), ("f1", w_f1[:, :])):
                    sp.dma_start(dst, args[name]).then_inc(prep_loaded, 16)
                sp.dma_start(w_l0[:, :], args["l0"]).then_inc(l0_loaded, 16)
                for name, dst in (("f1b", w_f1b[:, :]), ("x2", w_x2[:, :]), ("f2", w_f2[:, :]), ("f3", w_f3[:, :])):
                    sp.dma_start(dst, args[name]).then_inc(weights_loaded, 16)

            @block.gpsimd
            def _(pool):
                link = Chain(pool_link).on(pool)
                pool.memset(ones[:, :], 1.0).then_inc(set_up, 1)
                pool.memset(neg3[:, :, :, :], 0.0).then_inc(set_up, 1)
                square_context(pool)
                link(pool.memset(v_blocks[:, :, :, :, :], 0.0))
                for h2 in range(2):
                    link(pool.memset(v_blocks[64 * h2:64 * h2 + 64, :, :, :, 16 + h2:17 + h2], 1.0))
                    pool.sem_inc(set_up, 1)
                pool.memset(run_mask[:, :], 0.0)
                pool.memset(w_f1d[:, :, :, D:D + 1], 1.0)
                pool.memset(q_blocks[:, :, :, :, :], 0.0)

            @block.tensor
            def _(pe):
                pe.wait_ge(first_loaded, 48)
                turn_context(pe)
                sum_over_time(pe)
                context_keys(pe)
                context_values(pe, 0)
                context_values(pe, 1)
                turn_normed_context(pe)
                pe.wait_ge(prep_loaded, 16 * 11)
                for e in range(8):
                    for c in range(4):
                        m = pe.matmul(banks[e // 4][:, (e % 4) * D:(e % 4 + 1) * D],
                                      k_f1["be1"][:, e * 4 + c:e * 4 + c + 1].to_broadcast([P, P]),
                                      w_f1d[:, c, e, 0:D], start=(c == 0), stop=(c == 3))
                m.then_inc(means, 1)
                for e in range(4):
                    m = pe.matmul(banks[4 + e][:, :], lora_a[:, e, :], lora_b[:, e, :], start=True, stop=True)
                m.then_inc(means, 1)
                pe.wait_ge(evacuated, 1)
                pe.wait_ge(set_up, 2)
                pe.wait_ge(x_done, 1)
                pe.wait_ge(c_taken, 2)
                pe.wait_ge(kv1.v_ready, TILES)
                for half in range(2):
                    for c in range(4):
                        m = pe.matmul(banks[2 + half][:, :], ones[:, :], w_f1d[:, c, 4 * half:4 * half + 4, 0:D],
                                      start=(c == 0), stop=(c == 3))
                m.then_inc(means, 1)

            @block.scalar
            def _(act):
                act.wait_ge(first_loaded, 48)
                act.activation(tg[:, :], gates[:, :], ACT.Tanh).then_inc(tanh_done, 1)
                take_context(act)
                kv1.take_keys(act, banks[3])
                act.wait_ge(prep_loaded, 16 * 11)
                take_normed_context(act)

            @block.vector
            def _(dve):
                link = dve_steps.on(dve)
                dve.sem_inc(stored, 16)
                dve.wait_ge(tanh_done, 1)
                dve.wait_ge(set_up, 4)
                dve.wait_ge(first_loaded, 48)
                link(dve.tensor_tensor(bv1[:, :], k_x1["bv"], k_const["pmask"], ALU.mult))
                run(open_rows(dve, link))
                dve.wait_ge(prep_loaded, 16 * 11)
                dve.wait_ge(means, 1)
                for half in range(2):
                    dve.tensor_tensor(expert_bias[:, 4 * half:4 * half + 4, :],
                                      banks[half][:, :].rearrange("p (e d) -> p e d", d=D),
                                      b2[:, 512 * half:512 * half + 512].rearrange("p (e d) -> p e d", d=D),
                                      ALU.add)
                for c in range(4):
                    g1 = k_f1["g1"][:, c:32:4]
                    m = dve.tensor_tensor(w_f1d[:, c, :, 0:D], w_f1d[:, c, :, 0:D],
                                          g1.unsqueeze(2).to_broadcast([P, 8, D]), ALU.mult)
                m.then_inc(evacuated, 1)
                dve.wait_ge(means, 2)
                for e in range(4):
                    dve.tensor_tensor(w_f2e[:, e, :], banks[4 + e][:, :], wi[:, :], ALU.add)
                dve.tensor_scalar(bo1[:, :], k_x1["bo"], tg[:, 1:2], None, ALU.mult)
                dve.tensor_scalar(bout3[:, :], k_x3["bout"], tg[:, 3:4], None, ALU.mult)
                dve.tensor_tensor(bv3[:, :], k_a3["bv"], k_const["pmask"], ALU.mult)
                for at, bq in ((0, k_x1["bq"]), (2, k_a3["bq"])):
                    dve.tensor_scalar(scaled[:, at:at + 2], k_const["half"], bq, HD ** -0.5, ALU.mult, ALU.mult)
                dve.tensor_scalar(scaled[:, 5:7], k_const["half"], HD ** -0.5, None, ALU.mult)
                dve.scalar_tensor_tensor(scaled[:, 4:5], k_x3["qn"], XD ** -0.5, k_x3["kn"], ALU.mult, ALU.mult)
                dve.wait_ge(means, 3)
                for half in range(2):
                    for c in range(4):
                        w = w_f1d[:, c, 4 * half:4 * half + 4, 0:D]
                        dve.scalar_tensor_tensor(w, banks[2 + half][:, :].rearrange("p (e d) -> p e d", d=D),
                                                 -1.0 / 512, w, ALU.mult, ALU.add)

        with ExitStack() as before_loop:
            prepared = [before_loop.enter_context(nc.semaphore(n)) for n in
                        "first_loaded prep_loaded set_up means evacuated tanh_done pool_link".split()]
            with nc.Block() as block:
                prepare(block, *prepared)
            clear(flow + opening + kv1.sems + prepared)
        dve_steps.n = 0

        with nc.Fori(0, BLOCKS) as i:
            prev = ffn0(i, None, 0, norm_pair)
            prev = attention(prev, 1, norm_pair, k_x1, kv1, [], scaled[:, 0:2], None, None, add_gated(1, bo1[:, :]))
            prev = ffn1(prev, 2, norm_all)
            prev = attention(prev, 3, norm_pair, k_x2, kv2, [(kv2.k_ready, 1), (kv2.v_ready, TILES)], None, neg2, any2,
                             add_gated(2))
            prev = ffn2(prev, 4, norm_pair_twice)
            prev = perceiver(prev, 5, norm_pair)
            prev = attention(prev, 6, rms_pair, k_a3, kv3, None, scaled[:, 2:4], None, None, add_to_z)
            ffn3(prev, 7, rms_last)
            finish_block(i, 8)

            with nc.Block() as block:
                @block.sync
                def _(sp):
                    for parts, _ in stages:
                        if "sync" in parts.of:
                            parts.of["sync"](sp)

                @block.tensor
                def _(pe):
                    for parts, _ in stages:
                        if "tensor" in parts.of:
                            parts.of["tensor"](pe)

                @block.scalar
                def _(act):
                    for parts, _ in stages:
                        if "scalar" in parts.of:
                            parts.of["scalar"](act)

                @block.gpsimd
                def _(pool):
                    for parts, _ in stages:
                        if "gpsimd" in parts.of:
                            parts.of["gpsimd"](pool)

                @block.vector
                def _(dve):
                    for parts, _ in stages:
                        if "vector" in parts.of:
                            parts.of["vector"](dve)

            clear(flow + opening + kv1.sems + kv2.sems + kv3.sems + [s for _, sems in stages for s in sems])
        with nc.Block() as block:
            @block.sync
            def _(sp):
                sp.wait_ge(stored, 16 * BLOCKS + 16)


def layouts(a):
    import numpy as np

    f = np.float32
    rows = lambda v: np.broadcast_to(np.asarray(v).reshape(1, -1), (P, np.asarray(v).size))
    col = lambda v: np.asarray(v).reshape(-1, 1)
    pack = lambda *xs: np.ascontiguousarray(np.concatenate([np.asarray(z).reshape(P, -1) for z in xs], axis=1))
    n = np.arange(P)
    gap = n[None, :] - n[:, None]
    same = (n[None, :] // SEQ) == (n[:, None] // SEQ)
    decay = np.where(same & (gap >= 0), 0.9 ** np.maximum(gap, 0), 0.0)
    pmask = (n[:, None] // SEQ) == (n[None, :] // HD % 2)
    out = {"consts": pack(np.eye(P, dtype=f), (n[:, None] // HD % GROUP == np.arange(GROUP)).astype(f),
                          (n[:, None] // 64 == np.arange(2)).astype(f), pmask.astype(f),
                          (gap > 0).astype(f), rows(np.arange(HEADS, dtype=f)), decay.astype(f))}
    out["l0"] = pack(a["L0_ffn_gate_w"].T, a["L0_ffn_shared_gate_w"].T) if False else pack(
        np.concatenate([a["L0_ffn_gate_w"].T, a["L0_ffn_shared_gate_w"].T], axis=1),
        a["L0_ffn_w_gate_up"].reshape(4, 4, D, 2, 64).transpose(2, 0, 3, 1, 4),
        a["L0_ffn_shared_w_gate"].T, a["L0_ffn_shared_w_up"].T,
        a["L0_ffn_w_down"].reshape(8, P, D).transpose(1, 0, 2),
        np.concatenate([a["L0_ffn_shared_w_down"].T, np.zeros((32, D), f)]).reshape(3, P, D).transpose(1, 0, 2))
    out["x1"] = pack(*[a["L1_xattn_w" + c].T for c in "qkvo"], col(a["L1_xattn_bq"]), col(a["L1_xattn_bk"]),
                     rows(a["L1_xattn_bv"]), rows(a["L1_xattn_bo"]))
    chunked = lambda v: v.reshape(8, 4, P).transpose(2, 0, 1)
    out["f1"] = pack(a["L1_ffn_Wr"], rows(a["L1_ffn_br"]), chunked(a["L1_ffn_b1"]), chunked(a["L1_ffn_g1"]),
                     chunked(a["L1_ffn_be1"]), a["L1_ffn_W1"].transpose(1, 0, 2), rows(a["L1_ffn_g2"]))
    out["b2"] = np.ascontiguousarray(rows(a["L1_ffn_b2"]))
    out["f1b"] = np.ascontiguousarray(a["L1_ffn_be2"])
    out["f1d"] = np.ascontiguousarray(a["L1_ffn_W2"].reshape(8, 4, P, D).transpose(2, 1, 0, 3))
    out["gates"] = np.ascontiguousarray(rows(np.concatenate([a["g_xattn"], a["g_ffn"]])))
    out["x2"] = pack(*[a["L2_xattn_W_" + c].T for c in "QKVO"])
    out["f2"] = pack(a["L2_ffn_Wg"].T, rows(a["L2_ffn_bg"]),
                     a["L2_ffn_Wo"].T.reshape(4, P, D).transpose(1, 0, 2))
    out["wi"] = np.ascontiguousarray(a["L2_ffn_Wi"].T)
    out["lora_a"] = np.ascontiguousarray(a["L2_ffn_A"].transpose(1, 0, 2))
    out["lora_b"] = np.ascontiguousarray(a["L2_ffn_B"].transpose(2, 0, 1))
    twice = lambda v: col(np.concatenate([v, v]))
    out["x3"] = pack(col(a["L3_xattn_ln_x_g"]), col(a["L3_xattn_ln_x_b"]), col(a["L3_xattn_ln_l_g"]),
                     col(a["L3_xattn_ln_l_b"]), twice(a["L3_xattn_qn_g"]), twice(a["L3_xattn_kn_g"]),
                     rows(a["L3_xattn_bout"]), a["L3_xattn_Wq"], a["L3_xattn_Wkv"],
                     a["L3_xattn_Wout"].reshape(8, P, D).transpose(1, 0, 2))
    rep = lambda w: np.repeat(w.reshape(-1, 4, HD), 4, axis=1).reshape(-1, D)
    out["a3"] = pack(a["L3_ffn_qw"], rep(a["L3_ffn_kw"]), rep(a["L3_ffn_vw"]), a["L3_ffn_ow"],
                     col(a["L3_ffn_qb"]), col(rep(a["L3_ffn_kb"])), rows(rep(a["L3_ffn_vb"])), rows(a["L3_ffn_ob"]))
    out["f3"] = pack(a["L3_ffn_gate_w"], rows(a["L3_ffn_norm1_w"]), rows(a["L3_ffn_norm2_w"]),
                     a["L3_ffn_w1"].transpose(1, 0, 2), a["L3_ffn_w2"].reshape(8, 2, P, D).transpose(2, 0, 1, 3))
    more = lambda v, rows: np.ascontiguousarray(np.concatenate([v, v[:rows]]))
    out["x"] = more(a["x"].reshape(BATCH * SEQ, D), TOK)
    out["ctx"] = more(a["ctx_1024"].reshape(BATCH * SEQ, D), TOK)
    out["mask2"] = more(a["mask_BxSxS2_bf0"].reshape(BATCH * SEQ, SEQ), TOK).view(np.int32)
    out["mask3"] = more(a["mask_BxS2_bf1"], TILES * PAIR).view(np.int32)
    return out


def kernel(**inputs):
    import numpy as _np
    import concourse.bacc as _bacc
    from concourse import mybir as _mybir
    from concourse.bass_utils import run_bass_kernel_spmd as _run

    nc = _bacc.Bacc("TRN2", target_bir_lowering=False, num_devices=1)
    arrays, args = {}, {}
    for name, a in layouts({k: _np.asarray(v) for k, v in inputs.items()}).items():
        arrays[f"in_{name}_dram"] = a
        args[name] = nc.dram_tensor(f"in_{name}_dram", a.shape, _mybir.dt.from_np(a.dtype), kind="ExternalInput").ap()
    out = nc.dram_tensor("out_0_dram", (BATCH * SEQ, D), _mybir.dt.float32, kind="ExternalOutput").ap()
    build(nc, args, out)
    r = _run(nc, [arrays], core_ids=[0])
    return r.results[0]["out_0_dram"].reshape(BATCH, SEQ, D)
```
